# Optimizing a Trainium2 kernel written in Bass

```python
import numpy as np
import jax
import jax.numpy as jnp

def _softmax(x, axis=-1):
    return jax.nn.softmax(x, axis=axis)

def _gelu(x):
    return jax.nn.gelu(x, approximate=True)

def _silu(x):
    return jax.nn.silu(x)

def _sigmoid(x):
    return jax.nn.sigmoid(x)

def _layernorm(x, axis=-1, eps=1e-05):
    m = jnp.mean(x, axis=axis, keepdims=True)
    v = jnp.var(x, axis=axis, keepdims=True)
    return (x - m) / jnp.sqrt(v + eps)

def _scatter_add(tgt, idx, src, axis=0):
    return tgt.at[idx].add(src)

def _segment_sum(src, seg, n):
    return jax.ops.segment_sum(src, seg, n)
kernel_name = 'mk_audio_tower_d2_tok_audfeat512_r4_deafbc'

def setup_inputs(seed: int=0):
    np.random.seed(seed)
    _w = jnp.asarray

    def _rec_inputs():
        import jax
        import jax.numpy as jnp
        _rk = jax.random.key(seed)
        x = -0.000292821 + 1.00034 * jax.random.normal(jax.random.fold_in(_rk, 1), (4, 750, 128), jnp.float32)
        return x
    x = _rec_inputs()

    def _L0_tok_setup():
        import jax, jax.numpy as jnp
        import numpy as np
        B, T, C, HID, K, H = (8, 256, 128, 512, 31, 4)
        key = jax.random.key(seed)
        ks = jax.random.split(key, 8)
        n = lambda k_, sh, sc: jax.random.normal(k_, sh, dtype=jnp.float32) * sc
        return {'x': n(ks[0], (B, T, C), 1.0), 'Wl': n(ks[1], (H * K, C), 0.05), 'bl': n(ks[2], (H * K,), 0.01), 'bias': n(ks[3], (C,), 0.02), 'Wc': n(ks[4], (HID, C, K), 0.01), 'bc': n(ks[5], (HID,), 0.01), 'W2': n(ks[6], (C, HID), 0.01), 'b2': n(ks[7], (C,), 0.01)}
    _L0_tok_all = _L0_tok_setup()
    _L0_tok_in = {k: v for k, v in _L0_tok_all.items() if k in ('Wl', 'bl', 'bias', 'Wc', 'bc', 'W2', 'b2')}
    del _L0_tok_all

    def _L0_attn_setup():
        import jax, jax.numpy as jnp
        import numpy as np
        CAUSAL = True
        key = jax.random.key(seed)
        k1, k2, k3 = jax.random.split(key, 3)
        B, S, D_IN, D_INNER, D_OUT = (4, 1024, 128, 64, 128)
        x = jax.random.normal(k1, (B, S, D_IN), dtype=jnp.float32)
        W_qkv = jax.random.normal(k2, (D_IN, 3 * D_INNER), dtype=jnp.float32) * D_IN ** (-0.5)
        W_out = jax.random.normal(k3, (D_INNER, D_OUT), dtype=jnp.float32) * D_INNER ** (-0.5)
        b_out = jnp.zeros((D_OUT,), dtype=jnp.float32)
        return {'x': x, 'W_qkv': W_qkv, 'W_out': W_out, 'b_out': b_out}
    _L0_attn_all = _L0_attn_setup()
    _L0_attn_in = {k: v for k, v in _L0_attn_all.items() if k in ('W_qkv', 'W_out', 'b_out')}
    del _L0_attn_all

    def _L0_ffn_setup():
        import jax, jax.numpy as jnp
        import numpy as np
        MARK_AX, OP_ADD, OP_SUB = (0, 1, 2)
        ALU_LO, ALU_HI = (16, 32)
        AX_CARRY_LO, AX_CARRY_HI = (48, 64)
        OPCODE_BASE = 80
        OUTPUT_LO, OUTPUT_HI, CARRY = (128, 144, 160)
        NIB_A, NIB_B, OP_START = (0, 1, 10)
        RESULT, CARRY_OUT = (100, 101)
        GE_POS, GE_DIM = (8, 160)
        OPC_ADD, OPC_SUB = (25, 26)
        B, S, D = (8, 1024, 128)

        def _decode_nibble(x, base):
            return jnp.argmax(x[..., base:base + 16] > 0.5, axis=-1).astype(x.dtype)

        def _pipeline(h, W, b):
            for i in range(3):
                h = jnp.einsum('bspd,od->bspo', h, W[i]) + b[i]
                if i < 2:
                    h = jax.nn.relu(h)
            return h
        key = jax.random.key(seed)
        kx, k1, k2, k3, k4 = jax.random.split(key, 5)
        x_bd = jax.random.uniform(kx, (B, S, D), dtype=jnp.float32)
        Wa = jax.random.normal(k1, (3, GE_DIM, GE_DIM), dtype=jnp.float32) * 0.05
        ba = jax.random.normal(k2, (3, GE_DIM), dtype=jnp.float32) * 0.05
        Ws = jax.random.normal(k3, (3, GE_DIM, GE_DIM), dtype=jnp.float32) * 0.05
        bs = jax.random.normal(k4, (3, GE_DIM), dtype=jnp.float32) * 0.05
        return {'x_bd': x_bd, 'Wa': Wa, 'ba': ba, 'Ws': Ws, 'bs': bs}
    _L0_ffn_all = _L0_ffn_setup()
    _L0_ffn_in = {k: v for k, v in _L0_ffn_all.items() if k in ('Wa', 'ba', 'Ws', 'bs')}
    del _L0_ffn_all

    def _L1_attn_setup():
        import jax, jax.numpy as jnp
        import numpy as np
        N_HEAD = 1
        D_MODEL = 128
        D_K = 128
        D_V = 128
        LN_EPS = 1e-05
        key = jax.random.key(seed)
        ks = jax.random.split(key, 8)
        B, Lq, Hs, Ws = (8, 900, 60, 60)
        q = jax.random.normal(ks[0], (B, Lq, D_MODEL), dtype=jnp.float32)
        k = jax.random.normal(ks[1], (B, D_MODEL, Hs, Ws), dtype=jnp.float32)
        v = jax.random.normal(ks[2], (B, D_MODEL, Hs, Ws), dtype=jnp.float32)
        w_qkvs = jax.random.normal(ks[3], (N_HEAD * D_K, D_MODEL), dtype=jnp.float32) * np.sqrt(2.0 / (D_MODEL + D_K)).astype(np.float32)
        fc_w = jax.random.normal(ks[4], (D_MODEL, N_HEAD * D_V), dtype=jnp.float32) * np.sqrt(2.0 / (D_MODEL + N_HEAD * D_V)).astype(np.float32)
        fc_b = jnp.zeros((D_MODEL,), dtype=jnp.float32)
        gamma = jnp.ones((D_MODEL,), dtype=jnp.float32)
        beta = jnp.zeros((D_MODEL,), dtype=jnp.float32)
        return {'q': q, 'k': k, 'v': v, 'w_qkvs': w_qkvs, 'fc_w': fc_w, 'fc_b': fc_b, 'gamma': gamma, 'beta': beta}
    _L1_attn_all = _L1_attn_setup()
    _L1_attn_in = {k: v for k, v in _L1_attn_all.items() if k in ('k', 'v', 'w_qkvs', 'fc_w', 'fc_b', 'gamma', 'beta')}
    del _L1_attn_all

    def _L1_ffn_setup():
        import jax, jax.numpy as jnp
        import numpy as np
        TOP_K = 6
        CAP_FACTOR = 2.0
        key = jax.random.key(seed)
        ks = jax.random.split(key, 9)
        B, S, D, F, E, SH = (4, 512, 128, 64, 64, 2)
        return {'x': jax.random.normal(ks[0], (B, S, D), jnp.float32), 'router_w': jax.random.normal(ks[1], (E, D), jnp.float32) * 0.02, 'bias': jnp.zeros((E,), jnp.float32), 'shared_w_gate': jax.random.normal(ks[2], (SH, F, D), jnp.float32) * 0.02, 'shared_w_up': jax.random.normal(ks[3], (SH, F, D), jnp.float32) * 0.02, 'shared_w_down': jax.random.normal(ks[4], (SH, D, F), jnp.float32) * 0.02, 'w_gate': jax.random.normal(ks[5], (E, F, D), jnp.float32) * 0.02, 'w_up': jax.random.normal(ks[6], (E, F, D), jnp.float32) * 0.02, 'w_down': jax.random.normal(ks[7], (E, D, F), jnp.float32) * 0.02}
    _L1_ffn_all = _L1_ffn_setup()
    _L1_ffn_in = {k: v for k, v in _L1_ffn_all.items() if k in ('router_w', 'bias', 'shared_w_gate', 'shared_w_up', 'shared_w_down', 'w_gate', 'w_up', 'w_down')}
    del _L1_ffn_all
    return {'x': x, 'L0_tok_Wl': _L0_tok_in['Wl'], 'L0_tok_bl': _L0_tok_in['bl'], 'L0_tok_bias': _L0_tok_in['bias'], 'L0_tok_Wc': _L0_tok_in['Wc'], 'L0_tok_bc': _L0_tok_in['bc'], 'L0_tok_W2': _L0_tok_in['W2'], 'L0_tok_b2': _L0_tok_in['b2'], 'L0_attn_W_qkv': _L0_attn_in['W_qkv'], 'L0_attn_W_out': _L0_attn_in['W_out'], 'L0_attn_b_out': _L0_attn_in['b_out'], 'L0_ffn_Wa': _L0_ffn_in['Wa'], 'L0_ffn_ba': _L0_ffn_in['ba'], 'L0_ffn_Ws': _L0_ffn_in['Ws'], 'L0_ffn_bs': _L0_ffn_in['bs'], 'L1_attn_k': _L1_attn_in['k'], 'L1_attn_v': _L1_attn_in['v'], 'L1_attn_w_qkvs': _L1_attn_in['w_qkvs'], 'L1_attn_fc_w': _L1_attn_in['fc_w'], 'L1_attn_fc_b': _L1_attn_in['fc_b'], 'L1_attn_gamma': _L1_attn_in['gamma'], 'L1_attn_beta': _L1_attn_in['beta'], 'L1_ffn_router_w': _L1_ffn_in['router_w'], 'L1_ffn_bias': _L1_ffn_in['bias'], 'L1_ffn_shared_w_gate': _L1_ffn_in['shared_w_gate'], 'L1_ffn_shared_w_up': _L1_ffn_in['shared_w_up'], 'L1_ffn_shared_w_down': _L1_ffn_in['shared_w_down'], 'L1_ffn_w_gate': _L1_ffn_in['w_gate'], 'L1_ffn_w_up': _L1_ffn_in['w_up'], 'L1_ffn_w_down': _L1_ffn_in['w_down']}

def reference(x, L0_tok_Wl, L0_tok_bl, L0_tok_bias, L0_tok_Wc, L0_tok_bc, L0_tok_W2, L0_tok_b2, L0_attn_W_qkv, L0_attn_W_out, L0_attn_b_out, L0_ffn_Wa, L0_ffn_ba, L0_ffn_Ws, L0_ffn_bs, L1_attn_k, L1_attn_v, L1_attn_w_qkvs, L1_attn_fc_w, L1_attn_fc_b, L1_attn_gamma, L1_attn_beta, L1_ffn_router_w, L1_ffn_bias, L1_ffn_shared_w_gate, L1_ffn_shared_w_up, L1_ffn_shared_w_down, L1_ffn_w_gate, L1_ffn_w_up, L1_ffn_w_down):
    import jax
    import jax.numpy as jnp

    def _L0_tok_ref(x, Wl, bl, bias, Wc, bc, W2, b2):
        import jax, jax.numpy as jnp
        import numpy as np
        B, T, C, HID, K, H = (8, 256, 128, 512, 31, 4)
        Bq, Tq, Cq = x.shape
        d = Cq // H
        logits = (x @ Wl.T + bl).reshape(Bq, Tq, H, K)
        offs = jnp.arange(K) - (K - 1) // 2
        pos = jnp.arange(Tq)[:, None] + offs[None, :]
        valid = (pos >= 0) & (pos < Tq)
        logits = jnp.where(valid[None, :, None, :], logits, -jnp.inf)
        w = jax.nn.softmax(logits, axis=-1)
        xg = x.reshape(Bq, Tq, H, d)[:, jnp.clip(pos, 0, Tq - 1)]
        y = jnp.einsum('bthk,btkhd->bthd', w, xg).reshape(Bq, Tq, Cq)
        y = y.transpose(0, 2, 1) + bias[None, :, None]
        z = jax.lax.conv_general_dilated(y, Wc, (1,), 'VALID', dimension_numbers=('NCH', 'OIH', 'NCH'))
        z = z + bc[None, :, None]
        z = jax.nn.selu(z.transpose(0, 2, 1))
        return z @ W2.T + b2

    def _L0_attn_ref(x, W_qkv, W_out, b_out):
        import jax, jax.numpy as jnp
        import numpy as np
        CAUSAL = True
        d_inner = W_out.shape[0]
        scale = d_inner ** (-0.5)
        qkv = jnp.einsum('bsi,io->bso', x, W_qkv)
        q, k, v = jnp.split(qkv, 3, axis=-1)
        sim = jnp.einsum('bid,bjd->bij', q, k) * scale
        if CAUSAL:
            S = x.shape[1]
            mask = jnp.triu(jnp.ones((S, S), dtype=bool), k=1)
            sim = jnp.where(mask[None], -jnp.finfo(q.dtype).max, sim)
        attn = jax.nn.softmax(sim, axis=-1)
        out = jnp.einsum('bij,bjd->bid', attn, v)
        return jnp.einsum('bid,do->bio', out, W_out) + b_out

    def _L0_ffn_ref(x_bd, Wa, ba, Ws, bs):
        import jax, jax.numpy as jnp
        import numpy as np
        MARK_AX, OP_ADD, OP_SUB = (0, 1, 2)
        ALU_LO, ALU_HI = (16, 32)
        AX_CARRY_LO, AX_CARRY_HI = (48, 64)
        OPCODE_BASE = 80
        OUTPUT_LO, OUTPUT_HI, CARRY = (128, 144, 160)
        NIB_A, NIB_B, OP_START = (0, 1, 10)
        RESULT, CARRY_OUT = (100, 101)
        GE_POS, GE_DIM = (8, 160)
        OPC_ADD, OPC_SUB = (25, 26)
        B, S, D = (8, 1024, 128)

        def _decode_nibble(x, base):
            return jnp.argmax(x[..., base:base + 16] > 0.5, axis=-1).astype(x.dtype)

        def _pipeline(h, W, b):
            for i in range(3):
                h = jnp.einsum('bspd,od->bspo', h, W[i]) + b[i]
                if i < 2:
                    h = jax.nn.relu(h)
            return h
        x = x_bd
        Bsz, seq, _ = x.shape
        x_ge = jnp.zeros((Bsz, seq, GE_POS, GE_DIM), dtype=x.dtype)
        x_ge = x_ge.at[..., 0, NIB_A].set(_decode_nibble(x, ALU_LO))
        x_ge = x_ge.at[..., 1, NIB_A].set(_decode_nibble(x, ALU_HI))
        x_ge = x_ge.at[..., 0, NIB_B].set(_decode_nibble(x, AX_CARRY_LO))
        x_ge = x_ge.at[..., 1, NIB_B].set(_decode_nibble(x, AX_CARRY_HI))
        x_ge = x_ge.at[..., :, OP_START + OPC_ADD].set(x[..., OPCODE_BASE + OPC_ADD][..., None])
        x_ge = x_ge.at[..., :, OP_START + OPC_SUB].set(x[..., OPCODE_BASE + OPC_SUB][..., None])
        mark = x[..., MARK_AX] > 0.5
        m_add = mark & (x[..., OP_ADD] > 0.5)
        m_sub = mark & ~(x[..., OP_ADD] > 0.5) & (x[..., OP_SUB] > 0.5)
        active = (m_add | m_sub).astype(x.dtype)
        y_add = _pipeline(x_ge, Wa, ba)
        y_sub = _pipeline(x_ge, Ws, bs)
        y = jnp.where(m_add[..., None, None], y_add, jnp.where(m_sub[..., None, None], y_sub, x_ge))
        res_lo = jnp.clip(jnp.round(y[..., 0, RESULT]), 0, 15).astype(jnp.int32)
        res_hi = jnp.clip(jnp.round(y[..., 1, RESULT]), 0, 15).astype(jnp.int32)
        oh_lo = jax.nn.one_hot(res_lo, 16, dtype=x.dtype) * active[..., None]
        oh_hi = jax.nn.one_hot(res_hi, 16, dtype=x.dtype) * active[..., None]
        carry = (jnp.round(y[..., 1, CARRY_OUT]) > 0.5).astype(x.dtype) * active
        out = x
        out = out.at[..., OUTPUT_LO:OUTPUT_LO + 16].add(2.0 * oh_lo)
        out = out.at[..., OUTPUT_HI:OUTPUT_HI + 16].add(2.0 * oh_hi)
        out = out.at[..., CARRY].add(carry)
        return out

    def _L1_attn_ref(q, k, v, w_qkvs, fc_w, fc_b, gamma, beta):
        import jax, jax.numpy as jnp
        import numpy as np
        N_HEAD = 1
        D_MODEL = 128
        D_K = 128
        D_V = 128
        LN_EPS = 1e-05
        B, Lq, D = q.shape
        temperature = jnp.asarray(np.power(D_K, 0.5), dtype=q.dtype)
        k = jnp.transpose(k.reshape(B, D, -1), (0, 2, 1))
        v = jnp.transpose(v.reshape(B, D, -1), (0, 2, 1))
        Lk = k.shape[1]
        residual = q
        qp = (q @ w_qkvs.T).reshape(B, Lq, N_HEAD, D_K)
        kp = (k @ w_qkvs.T).reshape(B, Lk, N_HEAD, D_K)
        vp = (v @ w_qkvs.T).reshape(B, Lk, N_HEAD, D_V)
        qh = jnp.transpose(qp, (2, 0, 1, 3)).reshape(N_HEAD * B, Lq, D_K)
        kh = jnp.transpose(kp, (2, 0, 1, 3)).reshape(N_HEAD * B, Lk, D_K)
        vh = jnp.transpose(vp, (2, 0, 1, 3)).reshape(N_HEAD * B, Lk, D_V)
        scores = jnp.einsum('bqd,bkd->bqk', qh, kh) / temperature
        attn = jax.nn.softmax(scores, axis=2)
        out = jnp.einsum('bqk,bkd->bqd', attn, vh)
        out = out.reshape(N_HEAD, B, Lq, D_V)
        out = jnp.transpose(out, (1, 2, 0, 3)).reshape(B, Lq, N_HEAD * D_V)
        out = out @ fc_w.T + fc_b
        out = out + residual
        mean = jnp.mean(out, axis=-1, keepdims=True)
        var = jnp.mean(jnp.square(out - mean), axis=-1, keepdims=True)
        out = (out - mean) * jax.lax.rsqrt(var + LN_EPS) * gamma + beta
        return out

    def _L1_ffn_ref(x, router_w, bias, shared_w_gate, shared_w_up, shared_w_down, w_gate, w_up, w_down):
        import jax, jax.numpy as jnp
        import numpy as np
        TOP_K = 6
        CAP_FACTOR = 2.0
        B, S, D = x.shape
        E = router_w.shape[0]
        K = TOP_K
        N = B * S
        C = max(1, int(N * K * CAP_FACTOR / E))
        router_logits = jnp.einsum('bsd,ed->bse', x, router_w) + bias
        hg = jnp.einsum('bsd,efd->bsef', x, shared_w_gate)
        hu = jnp.einsum('bsd,efd->bsef', x, shared_w_up)
        shared_out = jnp.einsum('bsef,edf->bsd', jax.nn.silu(hg) * hu, shared_w_down)
        shared_out = shared_out / shared_w_gate.shape[0]
        router_probs = jax.nn.softmax(router_logits, axis=-1)
        topk_p, topk_i = jax.lax.top_k(router_probs, K)
        topk_p = topk_p / (jnp.sum(topk_p, axis=-1, keepdims=True) + 1e-09)
        x_flat = x.reshape(N, D)
        flat_e = topk_i.reshape(-1)
        flat_g = topk_p.reshape(-1)
        token_ids = jnp.repeat(jnp.arange(N), K)
        order = jnp.argsort(flat_e)
        se = flat_e[order]
        st = token_ids[order]
        sg = flat_g[order]
        M = se.shape[0]
        pos = jnp.arange(M)
        is_first = jnp.concatenate([jnp.ones((1,), bool), se[1:] != se[:-1]])
        group_starts = jax.lax.cummax(pos * is_first.astype(pos.dtype))
        slot = pos - group_starts
        valid = slot < C
        safe_slot = jnp.where(valid, slot, C)
        expert_in = jnp.zeros((E, C + 1, D), x.dtype).at[se, safe_slot].set(x_flat[st])
        expert_gate = jnp.zeros((E, C + 1), x.dtype).at[se, safe_slot].set(sg)
        expert_tok = jnp.full((E, C + 1), N, jnp.int32).at[se, safe_slot].set(st.astype(jnp.int32))
        expert_mask = jnp.zeros((E, C + 1), bool).at[se, safe_slot].set(valid)
        expert_in = expert_in[:, :C]
        expert_gate = expert_gate[:, :C]
        expert_tok = expert_tok[:, :C]
        expert_mask = expert_mask[:, :C]
        hg = jnp.einsum('ecd,efd->ecf', expert_in, w_gate)
        hu = jnp.einsum('ecd,efd->ecf', expert_in, w_up)
        expert_out = jnp.einsum('ecf,edf->ecd', jax.nn.silu(hg) * hu, w_down)
        fm = expert_mask.reshape(-1)
        dst = jnp.where(fm, expert_tok.reshape(-1), N)
        fg = jnp.where(fm, expert_gate.reshape(-1), jnp.zeros((), x.dtype))
        sparse = jax.ops.segment_sum(fg[:, None] * expert_out.reshape(-1, D), dst, num_segments=N + 1)[:N]
        return shared_out + sparse.reshape(B, S, D)
    h = _L0_tok_ref(x, L0_tok_Wl, L0_tok_bl, L0_tok_bias, L0_tok_Wc, L0_tok_bc, L0_tok_W2, L0_tok_b2)
    h = h + _L0_attn_ref(_layernorm(h, axis=-1), L0_attn_W_qkv, L0_attn_W_out, L0_attn_b_out)
    h = h + _L0_ffn_ref(_layernorm(h, axis=-1), L0_ffn_Wa, L0_ffn_ba, L0_ffn_Ws, L0_ffn_bs)
    h = h + _L1_attn_ref(_layernorm(h, axis=-1), L1_attn_k, L1_attn_v, L1_attn_w_qkvs, L1_attn_fc_w, L1_attn_fc_b, L1_attn_gamma, L1_attn_beta)
    h = h + _L1_ffn_ref(_layernorm(h, axis=-1), L1_ffn_router_w, L1_ffn_bias, L1_ffn_shared_w_gate, L1_ffn_shared_w_up, L1_ffn_shared_w_down, L1_ffn_w_gate, L1_ffn_w_up, L1_ffn_w_down)
    return h

_drawn_inputs = setup_inputs


def setup_inputs(seed=0):
    import zlib

    import numpy as np

    out = dict(_drawn_inputs(seed))
    spreads = {'L0_attn_b_out': (0.0, 0.1),
     'L1_attn_fc_b': (0.0, 0.723),
     'L1_attn_gamma': (1.0, 0.2),
     'L1_attn_beta': (0.0, 0.1),
     'L1_ffn_bias': (0.0, 0.8)}
    factors = {'L0_tok_bl': 8.0,
     'L1_attn_k': 3.849,
     'L1_attn_v': 4.064,
     'L1_attn_w_qkvs': 4.006,
     'L1_attn_fc_w': 3.779,
     'L1_ffn_router_w': 8.0,
     'L1_ffn_shared_w_gate': 8.0,
     'L1_ffn_shared_w_up': 8.0,
     'L1_ffn_shared_w_down': 8.0,
     'L1_ffn_w_gate': 8.0,
     'L1_ffn_w_up': 8.0,
     'L1_ffn_w_down': 8.0}
    for name, (base, spread) in spreads.items():
        noise = np.random.default_rng([zlib.crc32(name.encode()), seed]).standard_normal(out[name].shape)
        drawn = base * np.exp(spread * noise) if base else spread * noise
        out[name] = jnp.asarray(drawn.astype(out[name].dtype))
    for name, factor in factors.items():
        out[name] = (out[name] * factor).astype(out[name].dtype)
    return out
```

```python
from contextlib import ExitStack, contextmanager

import numpy as np
import concourse.bass as bass
from concourse import mybir

F32 = mybir.dt.float32
F16 = mybir.dt.float16
ALU = mybir.AluOpType
ACT = mybir.ActivationFunctionType
AX = mybir.AxisListType.X

B, T_IN, C = 4, 750, 128
HEADS, TAPS = 4, 31
HID = 512
MC = HID // 128
T = T_IN - TAPS + 1
P = 120
R = T // P
HALF = T // 2
LEFT = (TAPS - 1) // 2
WT = 94
WIN = WT + TAPS - 1
NW = 8
GW = 4
TP = NW * WT
KEYS = 7200
CH = 720
NCH = KEYS // CH
KT = KEYS // P
E, FF, TOPK = 64, 64, 6
CAP = int(B * T * TOPK * 2.0 / E)
PAIRS = E // 2
NSEQ = PAIRS + 1
MT = 480
NMC = B * T // MT
EPS = 1e-5
SELU_SCALE = 1.0507009873554804934193349852946
SELU_ALPHA = 1.6732632423543772848170429916717
W_SCALE = 256.0
X_SCALE = 16.0
WCH = TAPS * HID // 8


class Order:

    def __init__(self, eng, sem):
        self.eng, self.sem, self.base, self.n = eng, sem, 0, 0

    def link(self, ins):
        ins.then_inc(self.sem, 1)
        self.n += 1
        self.eng.wait_ge(self.sem, self.base + self.n)

    @contextmanager
    def loop(self, count, per):
        before = self.base + self.n
        with self.eng.Fori(0, count) as i:
            self.base, self.n = before + i * per, 0
            yield i
            assert self.n == per, f"the body links {self.n} times, not {per}"
        self.base, self.n = before + count * per, 0


class Region:

    def __init__(self, tensor, words):
        self.tensor, self.words, self.at = tensor, words, 0

    def take(self, *shape, dtype=F32):
        n = int(np.prod(shape))
        words = n if dtype == F32 else (n + 1) // 2
        assert self.at + words <= self.words, (self.at + words, self.words)
        piece = self.tensor[:, self.at:self.at + words]
        self.at += words
        if dtype != F32:
            piece = piece.bitcast(dtype)
        if len(shape) == 2:
            piece = piece.rearrange("p (a b) -> p a b", a=shape[0])
        if len(shape) == 3:
            piece = piece.rearrange("p (a b c) -> p a b c", a=shape[0], b=shape[1])
        return piece


def tower(nc, d, out, stop_after=9):
    ctx = ExitStack()
    with ctx:
        def sb(name, shape, dt=F32):
            return ctx.enter_context(nc.sbuf_tensor(name, shape, dt))

        def sem(name):
            return ctx.enter_context(nc.semaphore(name))

        ps = ctx.enter_context(nc.psum_tensor("ps", [128, 8, 512], F32))

        h = sb("h", [P, B * R, C])
        xres = sb("xres", [P, B * R, C])
        gates = sb("gates", [128, B * T], F16)

        ident = sb("ident", [128, 128])
        ones = sb("ones", [128, 128])
        ones16 = sb("ones16", [128, 128], F16)
        causal = sb("causal", [P, P])
        before = sb("before", [P, P])
        bc_sb = sb("bc_sb", [128, MC])
        tokb = sb("tokb", [128, 1])
        w2_sb = sb("w2_sb", [128, MC, C])
        rows = sb("rows", [P, 6, C])
        rw_sb = sb("rw_sb", [128, E])
        rb_sb = sb("rb_sb", [1, E])
        g0 = sb("g0", [128, 128])
        m0 = sb("m0", [128, 128])
        g1 = sb("g1", [128, 128])
        m1 = sb("m1", [128, 128])
        zrow = sb("zrow", [1, 512], F16)
        carry = sb("carry", [P, E])
        stats = sb("stats", [P, R, 6])
        mv = sb("mv", [P, R, 2])
        rstd = sb("rstd", [P, R])
        vare = sb("vare", [P, R])
        power = sb("power", [P, R])
        eps = sb("eps", [P, R])
        idle = sb("idle", [P, 1])
        mx2 = sb("mx2", [P, 2])
        nm = sb("nm", [P, R])
        sums = sb("sums", [P, R, 2])
        den = sb("den", [P, R])
        rden = sb("rden", [P, R])

        region_a = Region(sb("region_a", [128, 15872]), 15872)
        wc_hi = region_a.take(TAPS, HID, dtype=F16)
        wc_lo = region_a.take(TAPS, HID, dtype=F16)
        region_a.at = 0
        k_hi = region_a.take(KEYS, dtype=F16)
        k_lo = region_a.take(KEYS, dtype=F16)
        vp = region_a.take(KT, C + 1)[0:P]

        region_b = Region(sb("region_b", [128, 3010]), 3010)
        y_hi = region_b.take(B, TP, dtype=F16)
        y_lo = region_b.take(B, TP, dtype=F16)
        region_b.at = 0
        q_hi = region_b.take(B, T, dtype=F16)
        q_lo = region_b.take(B, T, dtype=F16)
        x_hi = q_hi.rearrange("p b t -> p (b t)")
        x_lo = q_lo.rearrange("p b t -> p (b t)")

        region_m = Region(sb("region_m", [128, 14800]), 14800)
        xt = [region_m.take(GW * WT) for _ in range(2)]
        mask = region_m.take(2, GW * HEADS * TAPS)[0:WT]
        lgs = region_m.take(GW * HEADS, TAPS)[0:WT]
        lgm = region_m.take(GW * HEADS, TAPS)[0:WT]
        ew = region_m.take(GW * HEADS, TAPS)[0:WT]
        wn = [region_m.take(GW * HEADS, TAPS)[0:WT] for _ in range(2)]
        wmx = region_m.take(GW * HEADS)[0:WT]
        wsum = region_m.take(GW * HEADS)[0:WT]
        wrs = region_m.take(GW * HEADS)[0:WT]
        zero = region_m.take(HEADS * WIN)[0:WT]
        wl_sb = region_m.take(HEADS * TAPS)
        bl_sb = region_m.take(HEADS * TAPS)[0:1]
        wc_f = [region_m.take(WCH) for _ in range(2)]
        at_m = region_m.at
        band = [region_m.take(HEADS * WIN)[0:WT] for _ in range(4)]
        xw = [region_m.take(C)[0:WIN] for _ in range(4)]
        bandT = [region_m.take(HEADS * WT)[0:WIN] for _ in range(2)]
        ytmp = region_m.take(TP)
        region_m.at = 0
        zt = region_m.take(MC, HALF)
        zn = region_m.take(MC, HALF)
        zz = [region_m.take(MC, HALF) for _ in range(2)]
        region_m.at = 0
        wg_hi = region_m.take(NSEQ * 128, dtype=F16)
        wg_lo = region_m.take(NSEQ * 128, dtype=F16)
        wu_hi = region_m.take(NSEQ * 128, dtype=F16)
        wu_lo = region_m.take(NSEQ * 128, dtype=F16)
        wd_sb = region_m.take(NSEQ * C)
        sel_sb = region_m.take(PAIRS * 128, dtype=F16)

        region_c = Region(sb("region_c", [128, 8800]), 8800)
        wq_sb = region_c.take(128)[0:64]
        wk_sb = region_c.take(128)[0:64]
        wv_sb = region_c.take(128)[0:64]
        wo_sb = region_c.take(128)[0:64]
        w1_sb = region_c.take(128)
        fc_sb = region_c.take(128)
        region_c.at = 0
        hb = region_c.take(R, C)[0:P]
        xn = region_c.take(R, C)[0:P]
        xnT = region_c.take(T)
        at_c = region_c.at
        qg = region_c.take(T)
        v0 = region_c.take(R, C)[0:P]
        pr = [region_c.take(T)[0:P] for _ in range(2)]
        prT = [region_c.take(T)[0:P] for _ in range(2)]
        region_c.at = at_c
        kf = [region_c.take(CH) for _ in range(2)]
        vf = [region_c.take(CH) for _ in range(2)]
        at_c = region_c.at
        pt = [region_c.take(T)[0:P] for _ in range(2)]
        qb_hi = region_c.take(T, dtype=F16)
        qb_lo = region_c.take(T, dtype=F16)
        shift = region_c.take(R, P, dtype=F16)[0:P]
        mxk = region_c.take(R, NCH)[0:P]
        region_c.at = at_c
        lg = region_c.take(R, E)[0:P]
        probs = region_c.take(R, E + 2)[0:P]
        rep = region_c.take(R, E + 2)[0:P]
        top8 = region_c.take(R, 8)[0:P]
        top6 = region_c.take(R, 8)[0:P]
        msk = region_c.take(R, E)[0:P]
        gate2 = region_c.take(R, 2 * E)[0:P]
        slot = region_c.take(R, E)[0:P]
        g_tmp = region_c.take(T, dtype=F16)
        region_c.at = 0
        wstage = [region_c.take(NSEQ * 128 // 3) for _ in range(2)]
        region_c.at = 0
        sg = [region_c.take(MT) for _ in range(2)]
        su = [region_c.take(MT) for _ in range(2)]
        ac = [region_c.take(MT) for _ in range(2)]
        fin = region_c.take(MT // P, C)[0:P]

        band_dram = nc.dram_tensor("band_dram", [B * NW, WT, HEADS * WIN], F32).ap()

        names = """const_in ones_ready su_ready dve_own act_own pool_own wprod_ps
            xt_free logits_ready logits_free shifted exp_done w_ready zero_ready zero_out
            wc_free wc_hi_ready
            band_free bandT_ready bandT_ps_free bandT_sb bandT_free yps_ready yps_free
            y_done y_hi_done y_taken
            conv_done z_taken zneg_ready zexp_done z_ready h_ps_ready h_ps_free h_done
            xn_ready xT_ps xT_sb qg_ps qg_sb v_ps v_sb var_ready rstd_ready
            s_ps s_exp s_free nmax_ready pT_ps pT_sb o_ps o_free
            q1_ps q1_hi q1_done att0_done
            kf_free vf_free khi_ready klo_ready vps_ready vps_free vp_ready mx_ps mx_free shift_ready
            st_ps st_free pt_ready pt_free acc_ps acc_free qb_ready
            rl_ps rl_sh rl_exp pos_ps msk_ready gT_in gT_ps gT_hi gT_done x3_hi xm_done batch_done
            ws_free ws_hi ws_done up_ps up_free silu_done a_ready a_free moe_ps moe_free fin_ready fin_out
            stage""".split()
        s = {n: sem(n) for n in names}
        s_xt = [sem(f"xt_in{u}") for u in range(2)]
        s_wc = [sem(f"wc_in{u}") for u in range(2)]
        s_bw = [sem(f"band_written{u}") for u in range(2)]
        s_band = [sem(f"band_in{u}") for u in range(4)]
        s_kf = [sem(f"kf_in{u}") for u in range(2)]
        s_vf = [sem(f"vf_in{u}") for u in range(2)]
        s_ws = [sem(f"ws_in{u}") for u in range(2)]

        def bank(n, parts=128):
            return ps[0:parts, n]

        def two(n, parts=128):
            return ps[0:parts, n:n + 2, 0:HALF]

        def halves(ap):
            return ap.rearrange("p (a b) -> p a b", a=2)

        def stage_end(eng, n):
            eng.drain()
            eng.sem_inc(s["stage"], 1)
            eng.wait_ge(s["stage"], 5 * n)

        row = HEADS * WIN

        def band_taps(i):
            return bass.AP(tensor=band_dram.tensor, offset=i * (WT * row),
                           ap=[[row + 1, WT], [WIN, HEADS], [1, TAPS]])

        const_loads = [
            (ident, "ident"), (causal, "causal"), (before, "before"),
            (wl_sb, "WlT"), (bl_sb, "bl"), (mask, "mask"), (tokb, "tok_bias"),
            (wq_sb, "WqT"), (wk_sb, "WkT"), (wv_sb, "WvT"), (wo_sb, "Wo"),
            (w1_sb, "W1"), (fc_sb, "fcT"), (bc_sb, "bc"), (w2_sb, "W2T"),
            (rw_sb, "rwT"), (rb_sb, "rb"),
        ]
        row_loads = ["b2", "bo", "fcb", "gamma", "beta"]
        CONST_IN = 16 * (len(const_loads) + len(row_loads))

        block = ctx.enter_context(nc.Block())

        @block.sync
        def _(sp):
            for dst, name in const_loads:
                sp.dma_start(dst[:], d[name]).then_inc(s["const_in"], 16)
            for n, name in enumerate(row_loads):
                sp.dma_start(rows[:, n, :], d[name].partition_broadcast(P)).then_inc(s["const_in"], 16)
            with sp.Fori(0, B) as b:
                for u in range(2):
                    sp.wait_ge(s["xt_free"], 2 * b + u + 1)
                    sp.dma_start(xt[u], d["xT"][2 * b + u]).then_inc(s_xt[u], 16)
                    sp.wait_ge(s["wc_free"], 2 * b + u + 1)
                    sp.dma_start(wc_f[u], d["WcT"][2 * b + u]).then_inc(s_wc[u], 16)
            for u in range(2):
                sp.wait_ge(s_bw[u], 16 * GW * (B + 1))
            with sp.Fori(0, B) as b:
                for j in range(NW):
                    sp.wait_ge(s["band_free"], NW * b + j + 1)
                    sp.dma_start(band[j % 4], band_dram[NW * b + j]).then_inc(s_band[j % 4], 16)
                    sp.dma_start(xw[j % 4], d["xw"][NW * b + j]).then_inc(s_band[j % 4], 16)
            stage_end(sp, 1)
            stage_end(sp, 2)
            sp.dma_start(wd_sb, d["wdT"]).then_inc(s["const_in"], 16)
            sp.dma_start(sel_sb, d["sel"]).then_inc(s["const_in"], 16)
            stage_end(sp, 3)
            for n in range(6):
                if n >= 2:
                    sp.wait_ge(s["ws_done"], n - 1)
                sp.dma_start(wstage[n % 2], d["wgu"][n]).then_inc(s_ws[n % 2], 16)
            stage_end(sp, 4)
            if stop_after >= 4:
                with sp.Fori(0, B) as b:
                    with sp.Fori(0, NCH // 2) as c2:
                        for u in range(2):
                            at = bass.ds(sp.snap(c2 * (2 * CH) + u * CH), CH)
                            sp.wait_ge(s["kf_free"], NCH * b + 2 * c2 + u + 1)
                            sp.dma_start(kf[u], d["k"][b, :, at]
                                         ).then_inc(s_kf[u], 16)
                            sp.wait_ge(s["vf_free"], NCH * b + 2 * c2 + u + 1)
                            sp.dma_start(vf[u], d["v"][b, :, at]
                                         ).then_inc(s_vf[u], 16)
            stage_end(sp, 5)
            out_t = out.rearrange("b (r p) c -> p (b r) c", p=P)
            if stop_after < 9:
                sp.dma_start(out_t, h[:]).then_inc(s["fin_out"], 16)
                sp.wait_ge(s["fin_out"], 32)
                return
            with sp.Fori(0, NMC) as c:
                sp.wait_ge(s["fin_ready"], c + 1)
                sp.dma_start(out_t[:, bass.ds(c * (MT // P), MT // P), :], fin).then_inc(s["fin_out"], 16)
            sp.wait_ge(s["fin_out"], 16 * (NMC + 1))

        @block.gpsimd
        def _(pool):
            g = nc.gpsimd
            for name, n in (("xt_free", 2), ("logits_free", 2), ("wc_free", 2), ("band_free", 4),
                            ("bandT_ps_free", 2), ("bandT_free", 2), ("yps_free", 2),
                            ("kf_free", 2), ("vf_free", 2), ("mx_free", 2), ("vps_free", 1), ("st_free", 2),
                            ("h_done", 1), ("y_taken", 1), ("pt_free", 2), ("up_free", 2), ("a_free", 2),
                            ("fin_out", 16), ("h_ps_free", 1), ("moe_free", 1),
                            ("s_free", 2), ("pT_sb", 0)):
                if n:
                    pool.sem_inc(s[name], n)
            for u in range(2):
                pool.sem_inc(s_bw[u], 16 * GW)
            g.memset(zero, 0.0).then_inc(s["zero_ready"], 1)
            g.memset(power[:], -0.5)
            g.memset(eps[:], EPS)
            g.memset(carry[:], 0.0)
            g.memset(ones16[:], 1.0)
            g.memset(zrow[:], 0.0)
            g.memset(ones[:], 1.0).then_inc(s["ones_ready"], 1)
            stage_end(pool, 1)
            stage_end(pool, 2)
            own = Order(pool, s["pool_own"])

            def power_of_variance(n):
                pool.wait_ge(s["var_ready"], n)
                own.link(g.tensor_tensor(vare[:], mv[:, :, 1], eps[:], ALU.add))
                g.tensor_tensor(rstd[:], vare[:], power[:], ALU.pow).then_inc(s["rstd_ready"], 1)

            with own.loop(B, 3) as b:
                for n in range(3):
                    power_of_variance(3 * b + n + 1)
            stage_end(pool, 3)
            stage_end(pool, 4)
            if stop_after >= 4:
                with own.loop(B, 2) as b:
                    with pool.Fori(0, NCH // 2) as c2:
                        for u in range(2):
                            at = bass.ds(c2 * (2 * CH) + u * CH, CH)
                            pool.wait_ge(s["khi_ready"], NCH * b + 2 * c2 + u + 1)
                            g.tensor_tensor(k_lo[:, at], kf[u], k_hi[:, at], ALU.subtract
                                            ).then_inc(s["klo_ready"], 1)
                            pool.wait_ge(s["klo_ready"], NCH * b + 2 * c2 + u + 1)
                            pool.sem_inc(s["kf_free"], 1)
                    for n in range(2):
                        power_of_variance(3 * B + 2 * b + n + 1)
            stage_end(pool, 5)

        @block.scalar
        def _(act):
            a = nc.scalar

            act.wait_ge(s["zero_ready"], 1)
            act.dma_start(band_dram.rearrange("i p n -> p i n"),
                          zero.unsqueeze(1).broadcast_to((WT, B * NW, row))).then_inc(s["zero_out"], 16)
            act.wait_ge(s["wprod_ps"], 1)
            for n, (dst, scale) in enumerate(((g0, 64 ** -0.5), (m0, 1.0), (g1, C ** -0.5), (m1, 1.0))):
                a.activation(dst[:], bank(6)[:, 128 * n:128 * (n + 1)], ACT.Copy, scale=scale)
            act.wait_ge(s["zero_out"], 16)
            with act.Fori(0, B) as b:
                for u in range(2):
                    n = 2 * b + u
                    act.wait_ge(s["shifted"], n + 1)
                    a.activation(ew, lgm, ACT.Exp).then_inc(s["exp_done"], 1)
                    act.wait_ge(s_wc[u], 16 * (b + 1))
                    at = bass.ds(n * WCH, WCH)
                    a.activation(wc_hi.rearrange("p k m -> p (k m)")[:, at], wc_f[u], ACT.Copy,
                                 scale=W_SCALE).then_inc(s["wc_hi_ready"], 1)
                    act.wait_ge(s["w_ready"], n + 1)
                    for j in range(GW):
                        act.dma_start(band_taps(NW * b + GW * u + j), wn[u][:, HEADS * j:HEADS * (j + 1), :]
                                      ).then_inc(s_bw[u], 16)
            with act.Fori(0, B) as b:
                for j in range(NW):
                    n = NW * b + j
                    act.wait_ge(s["bandT_ready"], n + 1)
                    act.wait_ge(s["bandT_free"], n + 1)
                    a.activation(bandT[j % 2], bank(2 + j % 2, WIN)[:, 0:HEADS * WT], ACT.Copy
                                 ).then_inc(s["bandT_sb"], 1)
                act.wait_ge(s["y_done"], b + 1)
                a.activation(y_hi[:, b, :], ytmp, ACT.Copy).then_inc(s["y_hi_done"], 1)
            stage_end(act, 1)
            with act.Fori(0, B) as b:
                for u in range(2):
                    act.wait_ge(s["zneg_ready"], 2 * b + u + 1)
                    a.activation(zz[u], zn, ACT.Exp).then_inc(s["zexp_done"], 1)
            stage_end(act, 2)
            own = Order(act, s["act_own"])
            with act.Fori(0, B) as b:
                act.wait_ge(s["xT_ps"], 2 * b + 1)
                a.activation(halves(xnT), two(0), ACT.Copy).then_inc(s["xT_sb"], 1)
                act.wait_ge(s["qg_ps"], b + 1)
                a.activation(halves(qg), two(2), ACT.Copy).then_inc(s["qg_sb"], 1)

                def exponentials(r):
                    act.wait_ge(s["nmax_ready"], R * b + r + 1)
                    n1 = min(r + 1, 3) * P
                    last = a.activation(pr[r % 2][:, 0:n1], bank(2 * (r % 2), P)[:, 0:n1], ACT.Exp,
                                        bias=nm[:, r:r + 1], accum_out=sums[:, r, 0:1])
                    if r >= 3:
                        n2 = (r - 2) * P
                        last = a.activation(pr[r % 2][:, HALF:HALF + n2], bank(2 * (r % 2) + 1, P)[:, 0:n2],
                                            ACT.Exp, bias=nm[:, r:r + 1], accum_out=sums[:, r, 1:2])
                    last.then_inc(s["s_exp"], 1)

                exponentials(0)
                for r in range(R):
                    if r + 1 < R:
                        exponentials(r + 1)
                    act.wait_ge(s["pT_ps"], R * b + r + 1)
                    last = a.activation(prT[r % 2][:, 0:min(r + 1, 3) * P], bank(4, P)[:, 0:min(r + 1, 3) * P],
                                        ACT.Copy)
                    if r >= 3:
                        last = a.activation(prT[r % 2][:, HALF:(r + 1) * P], bank(5, P)[:, 0:(r - 2) * P], ACT.Copy)
                    last.then_inc(s["pT_sb"], 1)
                act.wait_ge(s["xT_ps"], 2 * b + 2)
                a.activation(halves(xnT), two(0), ACT.Copy).then_inc(s["xT_sb"], 1)
                act.wait_ge(s["q1_ps"], b + 1)
                a.activation(halves(q_hi[:, b, :]), two(2), ACT.Copy).then_inc(s["q1_hi"], 1)
            stage_end(act, 3)
            for n in range(6):
                dst = (wg_hi, wu_hi)[n // 3].rearrange("p (a b) -> p a b", a=3)[:, n % 3, :]
                act.wait_ge(s_ws[n % 2], 16 * (n // 2 + 1))
                a.activation(dst, wstage[n % 2], ACT.Copy, scale=X_SCALE).then_inc(s["ws_hi"], 1)
            stage_end(act, 4)
            if stop_after >= 4:
                with act.Fori(0, B) as b:
                    with act.Fori(0, NCH // 2) as c2:
                        for u in range(2):
                            n = NCH * b + 2 * c2 + u
                            act.wait_ge(s_kf[u], 16 * ((NCH // 2) * b + c2 + 1))
                            a.activation(k_hi[:, bass.ds(c2 * (2 * CH) + u * CH, CH)], kf[u], ACT.Copy
                                         ).then_inc(s["khi_ready"], 1)
                            act.wait_ge(s["vps_ready"], n + 1)
                            a.activation(vp[:, bass.ds(c2 * 12 + 6 * u, 6), 0:C].rearrange(
                                "p (a r) c -> p a r c", a=2),
                                ps[0:P, 4:6, 0:3 * C].rearrange("p a (r c) -> p a r c", c=C), ACT.Copy
                            ).then_inc(s["vp_ready"], 1)
                            act.wait_ge(s["vp_ready"], n + 1)
                            act.sem_inc(s["vps_free"], 1)
                    with act.Fori(0, KT // 2) as i:
                        for u in range(2):
                            n = KT * b + 2 * i + u
                            act.wait_ge(s["st_ps"], n + 1)
                            act.wait_ge(s["pt_free"], n + 1)
                            a.activation(halves(pt[u]), two(2 * u, P), ACT.Exp).then_inc(s["pt_ready"], 1)
                            act.wait_ge(s["pt_ready"], n + 1)
                            act.sem_inc(s["st_free"], 1)
                    act.wait_ge(s["xT_ps"], 2 * B + b + 1)
                    a.activation(halves(xnT), two(0), ACT.Copy).then_inc(s["xT_sb"], 1)
                    act.wait_ge(s["rl_sh"], b + 1)
                    a.activation(probs[:, :, 0:E], lg, ACT.Exp).then_inc(s["rl_exp"], 1)
                    act.wait_ge(s["xT_sb"], 2 * B + b + 1)
                    a.activation(q_hi[:, b, :], xnT, ACT.Copy).then_inc(s["x3_hi"], 1)
                    act.wait_ge(s["gT_ps"], b + 1)
                    a.activation(halves(gates[0:E, bass.ds(b * T, T)]), two(2, E), ACT.Copy)
                    a.activation(halves(g_tmp[E:128]), ps[E:128, 2:4, 0:HALF], ACT.Copy
                                 ).then_inc(s["gT_hi"], 1)
            stage_end(act, 5)
            if stop_after >= 9:
                with act.Fori(0, NMC) as c:
                    act.wait_ge(s["up_ps"], NSEQ * c + 1)
                    a.activation(sg[0], bank(0)[:, 0:MT], ACT.Silu, scale=1 / X_SCALE).then_inc(s["silu_done"], 1)
                    with act.Fori(0, PAIRS // 2) as i:
                        for u in (1, 0):
                            n = NSEQ * c + 2 * i + (2 - u)
                            act.wait_ge(s["up_ps"], n + 1)
                            act.wait_ge(s["up_free"], n + 1)
                            a.activation(sg[u], bank(3 * u)[:, 0:MT], ACT.Silu, scale=1 / X_SCALE
                                         ).then_inc(s["silu_done"], 1)

        @block.vector
        def _(dve):
            v = nc.vector
            own = Order(dve, s["dve_own"])

            dve.wait_ge(s["const_in"], CONST_IN)
            with own.loop(B, 2 * 5) as b:
                for u in range(2):
                    n = 2 * b + u
                    dve.wait_ge(s["logits_ready"], n + 1)
                    ins = v.tensor_tensor(lgs, bank(u, WT)[:, 0:GW * HEADS * TAPS].rearrange(
                        "p (a k) -> p a k", k=TAPS), mask[:, u, :].rearrange("p (a k) -> p a k", k=TAPS), ALU.add)
                    own.link(ins)
                    dve.sem_inc(s["logits_free"], 1)
                    dve.sem_inc(s["xt_free"], 1)
                    own.link(v.tensor_reduce(wmx, lgs, AX, ALU.max))
                    v.tensor_tensor(lgm, lgs, wmx.unsqueeze(2).broadcast_to((WT, GW * HEADS, TAPS)),
                                    ALU.subtract).then_inc(s["shifted"], 1)
                    dve.wait_ge(s["exp_done"], n + 1)
                    own.link(v.tensor_reduce(wsum, ew, AX, ALU.add))
                    own.link(v.reciprocal(wrs, wsum))
                    dve.wait_ge(s_bw[u], 16 * GW * (b + 1))
                    v.tensor_tensor(wn[u], ew, wrs.unsqueeze(2).broadcast_to((WT, GW * HEADS, TAPS)),
                                    ALU.mult).then_inc(s["w_ready"], 1)
                    dve.wait_ge(s["w_ready"], n + 1)
                    dve.wait_ge(s["wc_hi_ready"], n + 1)
                    at = bass.ds(n * WCH, WCH)
                    own.link(v.scalar_tensor_tensor(out=wc_lo.rearrange("p k m -> p (k m)")[:, at], in0=wc_f[u],
                                                    scalar=W_SCALE, in1=wc_hi.rearrange("p k m -> p (k m)")[:, at],
                                                    op0=ALU.mult, op1=ALU.subtract))
                    dve.sem_inc(s["wc_free"], 1)
            with own.loop(B, 1) as b:
                for j in range(NW):
                    n = NW * b + j
                    dve.wait_ge(s["yps_ready"], n + 1)
                    if j == 0:
                        dve.wait_ge(s["y_taken"], b + 1)
                    for g in range(HEADS):
                        lo, hi = g * 32, (g + 1) * 32
                        last = v.tensor_scalar(ytmp[lo:hi, j * WT:(j + 1) * WT],
                                               ps[lo:hi, 4 + j % 2, g * WT:(g + 1) * WT],
                                               tokb[lo:hi, :], None, ALU.add)
                    last.then_inc(s["yps_free"], 1)
                dve.wait_ge(s["yps_free"], NW * b + NW + 2)
                dve.sem_inc(s["y_done"], 1)
                dve.wait_ge(s["y_hi_done"], b + 1)
                own.link(v.tensor_tensor(y_lo[:, b, :], ytmp, y_hi[:, b, :], ALU.subtract))
                dve.sem_inc(s["y_taken"], 1)
            stage_end(dve, 1)

            with own.loop(B, 2 * 4 + 2) as b:
                for u in range(2):
                    n = 2 * b + u
                    dve.wait_ge(s["conv_done"], n + 1)
                    for m in range(MC):
                        last = v.tensor_scalar(zt[:, m, :], bank(4 * u + m)[:, 0:HALF], 1 / W_SCALE,
                                               bc_sb[:, m:m + 1], ALU.mult, ALU.add)
                    own.link(last)
                    dve.sem_inc(s["z_taken"], 1)
                    v.tensor_scalar(zn, zt, 0.0, None, ALU.min).then_inc(s["zneg_ready"], 1)
                    own.link(v.tensor_scalar(zt, zt, 0.0, SELU_SCALE, ALU.max, ALU.mult))
                    dve.wait_ge(s["zexp_done"], n + 1)
                    own.link(v.tensor_scalar(zz[u], zz[u], -1.0, SELU_SCALE * SELU_ALPHA, ALU.add, ALU.mult))
                    own.link(v.tensor_tensor(zz[u], zz[u], zt, ALU.add))
                    dve.sem_inc(s["z_ready"], 1)
                for u in range(2):
                    dve.wait_ge(s["h_ps_ready"], 2 * b + u + 1)
                    own.link(v.tensor_tensor(
                        h[:, bass.ds(b * R + 3 * u, 3), :],
                        bank(4 * u, P)[:, 0:3 * C].rearrange("p (r c) -> p r c", c=C),
                        rows[:, 0:1, :].broadcast_to((P, 3, C)), ALU.add))
                dve.sem_inc(s["h_done"], 1)
            stage_end(dve, 2)

            def layer_norm(dst, n):
                for r in range(R):
                    last = v.bn_stats(stats[:, r, :], hb[:, r, :])
                own.link(last)
                v.memset(idle[:], 0.0)
                for r in range(R):
                    last = v.bn_aggr(mv[:, r, :], stats[:, r, :])
                last.then_inc(s["var_ready"], 1)
                dve.wait_ge(s["var_ready"], n)
                dve.wait_ge(s["rstd_ready"], n)
                for r in range(R):
                    last = v.tensor_scalar(dst[:, r, :], hb[:, r, :], mv[:, r, 0:1], rstd[:, r:r + 1],
                                           ALU.subtract, ALU.mult)
                own.link(last)

            att_links = 1 + 2 + 1 + 6 * R + 1 + 2 + 1 + 2 + 1 + 1
            with own.loop(B, att_links) as b:
                at = bass.ds(b * R, R)
                own.link(v.tensor_copy(hb, h[:, at, :]))
                layer_norm(xn, 3 * b + 1)
                dve.sem_inc(s["xn_ready"], 1)
                dve.wait_ge(s["v_ps"], b + 1)
                own.link(v.tensor_copy(v0.rearrange("p (a r) c -> p a r c", a=2),
                                       ps[0:P, 4:6, 0:3 * C].rearrange("p a (r c) -> p a r c", c=C)))
                dve.sem_inc(s["v_sb"], 1)

                def maximum(r):
                    dve.wait_ge(s["s_ps"], R * b + r + 1)
                    diag = bank(2 * (r % 2) + r // 3, P)[:, (r % 3) * P:(r % 3 + 1) * P]
                    own.link(v.tensor_tensor(diag, diag, causal[:], ALU.add))
                    last = v.tensor_reduce(mx2[:, 0:1], bank(2 * (r % 2), P)[:, 0:min(r + 1, 3) * P], AX, ALU.max)
                    if r >= 3:
                        last = v.tensor_reduce(mx2[:, 1:2], bank(2 * (r % 2) + 1, P)[:, 0:(r - 2) * P], AX, ALU.max)
                    own.link(last)
                    own.link(v.tensor_reduce(nm[:, r:r + 1], mx2[:, 0:1 + r // 3], AX, ALU.max, negate=True))
                    dve.sem_inc(s["nmax_ready"], 1)

                maximum(0)
                for r in range(R):
                    if r + 1 < R:
                        maximum(r + 1)
                    dve.wait_ge(s["s_exp"], R * b + r + 1)
                    own.link(v.tensor_reduce(den[:, r:r + 1], sums[:, r, 0:1 + r // 3], AX, ALU.add))
                    own.link(v.reciprocal(rden[:, r:r + 1], den[:, r:r + 1]))
                    dve.wait_ge(s["o_ps"], R * b + r + 1)
                    own.link(v.scalar_tensor_tensor(out=hb[:, r, :], in0=bank(6 + r % 2, P)[:, 0:C],
                                                    scalar=rden[:, r:r + 1], in1=hb[:, r, :],
                                                    op0=ALU.mult, op1=ALU.add))
                    dve.sem_inc(s["o_free"], 1)
                own.link(v.tensor_tensor(hb, hb, rows[:, 1:2, :].broadcast_to((P, R, C)), ALU.add))
                layer_norm(xn, 3 * b + 2)
                own.link(v.tensor_tensor(hb, hb, xn, ALU.add))
                layer_norm(xn, 3 * b + 3)
                dve.sem_inc(s["xn_ready"], 1)
                v.tensor_copy(h[:, at, :], hb)
                own.link(v.tensor_copy(xres[:, at, :], xn))
                dve.wait_ge(s["q1_hi"], b + 1)
                own.link(v.tensor_tensor(halves(q_lo[:, b, :]), two(2), halves(q_hi[:, b, :]), ALU.subtract))
                dve.sem_inc(s["q1_done"], 1)
            stage_end(dve, 3)
            for n in range(6):
                hi = (wg_hi, wu_hi)[n // 3].rearrange("p (a b) -> p a b", a=3)[:, n % 3, :]
                lo = (wg_lo, wu_lo)[n // 3].rearrange("p (a b) -> p a b", a=3)[:, n % 3, :]
                dve.wait_ge(s["ws_hi"], n + 1)
                v.scalar_tensor_tensor(out=lo, in0=wstage[n % 2], scalar=X_SCALE, in1=hi,
                                       op0=ALU.mult, op1=ALU.subtract).then_inc(s["ws_done"], 1)
            own.link(v.memset(vp[:, :, C:C + 1], 1.0))
            stage_end(dve, 4)
            if stop_after < 4:
                stage_end(dve, 5)
                return

            f_links = 15 + R + 16
            with own.loop(B, f_links) as b:
                at = bass.ds(b * R, R)
                with dve.Fori(0, NCH // 2) as c2:
                    for u in range(2):
                        for r in range(R):
                            n = R * (NCH * b + 2 * c2 + u) + r
                            dve.wait_ge(s["mx_ps"], n + 1)
                            v.tensor_reduce(mxk[:, r, bass.ds(2 * c2 + u, 1)], two(2 * (r % 2), P),
                                            mybir.AxisListType.XY, ALU.max).then_inc(s["mx_free"], 1)
                dve.wait_ge(s["mx_free"], R * NCH * (b + 1) + 2)
                own.link(v.tensor_reduce(nm[:], mxk, AX, ALU.max, negate=True))
                for r in range(R):
                    last = v.tensor_scalar(shift[:, r, :], ident[0:P, 0:P], nm[:, r:r + 1], None, ALU.mult)
                own.link(last)
                v.tensor_copy(qb_hi, q_hi[:, b, :])
                own.link(v.tensor_copy(qb_lo, q_lo[:, b, :]))
                dve.sem_inc(s["shift_ready"], 1)
                dve.wait_ge(s["acc_ps"], b + 1)
                v.tensor_copy(hb, xres[:, at, :])
                for r in range(R):
                    o = (r % 3) * (C + 1)
                    last = v.reciprocal(rden[:, r:r + 1], ps[0:P, 6 + r // 3, o + C:o + C + 1])
                own.link(last)
                for r in range(R):
                    o = (r % 3) * (C + 1)
                    own.link(v.scalar_tensor_tensor(out=hb[:, r, :], in0=ps[0:P, 6 + r // 3, o:o + C],
                                                    scalar=rden[:, r:r + 1], in1=hb[:, r, :],
                                                    op0=ALU.mult, op1=ALU.add))
                dve.sem_inc(s["acc_free"], 1)
                own.link(v.tensor_tensor(hb, hb, rows[:, 2:3, :].broadcast_to((P, R, C)), ALU.add))
                layer_norm(xn, 3 * B + 2 * b + 1)
                own.link(v.tensor_tensor(xn, xn, rows[:, 3:4, :].broadcast_to((P, R, C)), ALU.mult))
                own.link(v.tensor_tensor(xn, xn, rows[:, 4:5, :].broadcast_to((P, R, C)), ALU.add))
                own.link(v.tensor_tensor(hb, xn, h[:, at, :], ALU.add))
                layer_norm(xn, 3 * B + 2 * b + 2)
                dve.sem_inc(s["xn_ready"], 1)
                own.link(v.tensor_copy(h[:, at, :], hb))
                dve.wait_ge(s["rl_ps"], b + 1)
                rl = bank(4, P)[:, 0:R * E].rearrange("p (r e) -> p r e", e=E)
                own.link(v.tensor_reduce(den[:], rl, AX, ALU.max))
                v.tensor_tensor(lg, rl, den[:].unsqueeze(2).broadcast_to((P, R, E)), ALU.subtract
                                ).then_inc(s["rl_sh"], 1)
                v.memset(probs[:, :, E:E + 2], -1.0)
                v.memset(top6, -1.0)
                dve.wait_ge(s["rl_exp"], b + 1)
                own.link(v.tensor_reduce(den[:], probs[:, :, 0:E], AX, ALU.add))
                own.link(v.reciprocal(rden[:], den[:]))
                own.link(v.tensor_tensor(probs[:, :, 0:E], probs[:, :, 0:E],
                                         rden[:].unsqueeze(2).broadcast_to((P, R, E)), ALU.mult))
                v.memset(idle[:], 0.0)
                for r in range(R):
                    last = v.max(top8[:, r, :], probs[:, r, 0:E])
                own.link(last)
                own.link(v.tensor_copy(top6[:, :, 0:TOPK], top8[:, :, 0:TOPK]))
                v.memset(idle[:], 0.0)
                for r in range(R):
                    last = v.match_replace(rep[:, r, :], top6[:, r, :], probs[:, r, :], -2.0)
                own.link(last)
                own.link(v.tensor_scalar(msk, rep[:, :, 0:E], -1.5, None, ALU.is_lt))
                dve.sem_inc(s["msk_ready"], 1)
                own.link(v.tensor_reduce(den[:], top8[:, :, 0:TOPK], AX, ALU.add))
                own.link(v.tensor_scalar(den[:], den[:], 1e-9, None, ALU.add))
                own.link(v.reciprocal(rden[:], den[:]))
                own.link(v.tensor_tensor(probs[:, :, 0:E], probs[:, :, 0:E], msk, ALU.mult))
                dve.wait_ge(s["pos_ps"], b + 1)
                own.link(v.tensor_tensor(slot, bank(5, P)[:, 0:R * E].rearrange("p (r e) -> p r e", e=E),
                                         carry[:].unsqueeze(1).broadcast_to((P, R, E)), ALU.add))
                v.tensor_scalar(slot, slot, float(CAP), X_SCALE, ALU.is_lt, ALU.mult)
                own.link(v.tensor_tensor(carry[:], carry[:], bank(5, P)[:, R * E:R * E + E], ALU.add))
                own.link(v.tensor_tensor(slot, slot, probs[:, :, 0:E], ALU.mult))
                rb = rden[:].unsqueeze(2).broadcast_to((P, R, E))
                v.tensor_tensor(gate2[:, :, 0:E], slot, rb, ALU.mult)
                own.link(v.tensor_tensor(gate2[:, :, E:2 * E], slot, rb, ALU.mult))
                dve.sem_inc(s["gT_in"], 1)
                dve.wait_ge(s["x3_hi"], b + 1)
                own.link(v.tensor_tensor(q_lo[:, b, :], xnT, q_hi[:, b, :], ALU.subtract))
                dve.wait_ge(s["gT_hi"], b + 1)
                own.link(v.tensor_tensor(halves(gates[E:128, bass.ds(b * T, T)]), ps[E:128, 2:4, 0:HALF],
                                         halves(g_tmp[E:128]), ALU.subtract))
                dve.sem_inc(s["batch_done"], 1)
            stage_end(dve, 5)
            if stop_after < 9:
                return
            with own.loop(NMC, 2) as c:
                dve.wait_ge(s["silu_done"], NSEQ * c + 1)
                dve.wait_ge(s["a_free"], NSEQ * c + 1)
                own.link(v.scalar_tensor_tensor(out=ac[0], in0=sg[0], scalar=X_SCALE * 0.5,
                                                in1=bank(1)[:, 0:MT], op0=ALU.mult, op1=ALU.mult))
                dve.sem_inc(s["up_free"], 1)
                dve.sem_inc(s["a_ready"], 1)
                with dve.Fori(0, PAIRS // 2) as i:
                    for u in (1, 0):
                        n = NSEQ * c + 2 * i + (2 - u)
                        dve.wait_ge(s["silu_done"], n + 1)
                        v.tensor_tensor(su[u], sg[u], bank(3 * u + 1)[:, 0:MT], ALU.mult
                                        ).then_inc(s["su_ready"], 1)
                        dve.wait_ge(s["su_ready"], PAIRS * c + 2 * i + (2 - u))
                        dve.wait_ge(s["a_free"], n + 1)
                        v.tensor_tensor(ac[u], su[u], bank(3 * u + 2)[:, 0:MT], ALU.mult
                                        ).then_inc(s["a_ready"], 1)
                        dve.wait_ge(s["a_ready"], n + 1)
                        dve.sem_inc(s["up_free"], 1)
                dve.wait_ge(s["moe_ps"], c + 1)
                dve.wait_ge(s["fin_out"], 16 * (c + 1))
                own.link(v.scalar_tensor_tensor(out=fin, in0=bank(6, P)[:, 0:4 * C].rearrange("p (r c) -> p r c", c=C),
                                                scalar=1 / (X_SCALE * X_SCALE),
                                                in1=h[:, bass.ds(c * (MT // P), MT // P), :],
                                                op0=ALU.mult, op1=ALU.add))
                dve.sem_inc(s["fin_ready"], 1)
                dve.sem_inc(s["moe_free"], 1)

        @block.tensor
        def _(pe):
            mm = nc.tensor.matmul

            pe.wait_ge(s["const_in"], CONST_IN)
            pe.wait_ge(s["ones_ready"], 1)
            mm(bank(6)[:, 0:128], wq_sb, wk_sb, start=True, stop=True)
            mm(bank(6)[:, 128:256], wv_sb, wo_sb, start=True, stop=True)
            mm(bank(6)[:, 256:384], w1_sb, w1_sb, start=True, stop=True)
            mm(bank(6)[:, 384:512], w1_sb, fc_sb, start=True, stop=True).then_inc(s["wprod_ps"], 1)
            with pe.Fori(0, B) as b:
                for u in range(2):
                    pe.wait_ge(s_xt[u], 16 * (b + 1))
                    pe.wait_ge(s["logits_free"], 2 * b + u + 1)
                    for j in range(GW):
                        o = bank(u, WT)[:, j * HEADS * TAPS:(j + 1) * HEADS * TAPS]
                        mm(o, xt[u][:, j * WT:(j + 1) * WT], wl_sb, start=True, stop=False)
                        last = mm(o, ones[0:1, 0:WT], bl_sb, start=False, stop=True)
                    last.then_inc(s["logits_ready"], 1)
            with pe.Fori(0, B) as b:
                for j in range(NW):
                    n = NW * b + j
                    pe.wait_ge(s_band[j % 4], 32 * (2 * b + j // 4 + 1))
                    pe.wait_ge(s["bandT_ps_free"], n + 1)
                    for g in range(HEADS):
                        last = nc.tensor.transpose(bank(2 + j % 2, WIN)[:, g * WT:(g + 1) * WT],
                                                   band[j % 4][:, g * WIN:(g + 1) * WIN], ident[0:WT, 0:WT])
                    last.then_inc(s["bandT_ready"], 1)
                    pe.wait_ge(s["bandT_sb"], n + 1)
                    pe.sem_inc(s["bandT_ps_free"], 1)
                    pe.wait_ge(s["yps_free"], n + 1)
                    mm(bank(4 + j % 2)[:, 0:HEADS * WT], xw[j % 4], bandT[j % 2], start=True, stop=True
                       ).then_inc(s["yps_ready"], 1)
                    pe.wait_ge(s["yps_ready"], n + 1)
                    pe.sem_inc(s["bandT_free"], 1)
                    pe.sem_inc(s["band_free"], 1)
            stage_end(pe, 1)
            with pe.Fori(0, B) as b:
                for u in range(2):
                    if u == 0:
                        pe.wait_ge(s["h_done"], b + 1)
                    for k in range(TAPS):
                        yh = y_hi[:, b, u * HALF + k:u * HALF + k + HALF]
                        yl = y_lo[:, b, u * HALF + k:u * HALF + k + HALF]
                        for m in range(MC):
                            o = bank(4 * u + m)[:, 0:HALF]
                            wh = wc_hi[:, k, m * 128:(m + 1) * 128]
                            mm(o, wh, yh, start=(k == 0), stop=False)
                            mm(o, wh, yl, start=False, stop=False)
                            last = mm(o, wc_lo[:, k, m * 128:(m + 1) * 128], yh, start=False, stop=(k == TAPS - 1))
                    last.then_inc(s["conv_done"], 1)
                for u in range(2):
                    pe.wait_ge(s["z_ready"], 2 * b + u + 1)
                    for r in range(3):
                        for m in range(MC):
                            last = mm(bank(4 * u, P)[:, r * C:(r + 1) * C], zz[u][:, m, r * P:(r + 1) * P],
                                      w2_sb[:, m, :], start=(m == 0), stop=(m == MC - 1))
                    last.then_inc(s["h_ps_ready"], 1)
            stage_end(pe, 2)

            def transposes():
                for r in range(R):
                    last = nc.tensor.transpose(bank(r // 3)[:, (r % 3) * P:(r % 3 + 1) * P], xn[:, r, :],
                                               ident[0:P, 0:P])
                last.then_inc(s["xT_ps"], 1)

            with pe.Fori(0, B) as b:
                pe.wait_ge(s["xn_ready"], 2 * b + 1)
                transposes()
                pe.wait_ge(s["xT_sb"], 2 * b + 1)
                for u in range(2):
                    last = mm(bank(2 + u)[:, 0:HALF], g0[:], xnT[:, u * HALF:(u + 1) * HALF], start=True, stop=True)
                last.then_inc(s["qg_ps"], 1)
                for r in range(R):
                    last = mm(bank(4 + r // 3, P)[:, (r % 3) * C:(r % 3 + 1) * C], xnT[:, r * P:(r + 1) * P],
                              m0[:], start=True, stop=True)
                last.then_inc(s["v_ps"], 1)
                pe.wait_ge(s["qg_sb"], b + 1)
                pe.wait_ge(s["v_sb"], b + 1)

                def scores(r):
                    o = bank(2 * (r % 2), P)
                    last = mm(o[:, 0:min(r + 1, 3) * P], qg[:, r * P:(r + 1) * P], xnT[:, 0:min(r + 1, 3) * P],
                              start=True, stop=True)
                    if r >= 3:
                        last = mm(bank(2 * (r % 2) + 1, P)[:, 0:(r - 2) * P], qg[:, r * P:(r + 1) * P],
                                  xnT[:, HALF:HALF + (r - 2) * P], start=True, stop=True)
                    last.then_inc(s["s_ps"], 1)

                scores(0)
                for r in range(R):
                    if r + 1 < R:
                        scores(r + 1)
                    pe.wait_ge(s["s_exp"], R * b + r + 1)
                    for t in range(r + 1):
                        last = nc.tensor.transpose(bank(4 + t // 3, P)[:, (t % 3) * P:(t % 3 + 1) * P],
                                                   pr[r % 2][:, t * P:(t + 1) * P], ident[0:P, 0:P])
                    last.then_inc(s["pT_ps"], 1)
                    pe.wait_ge(s["pT_sb"], R * b + r + 1)
                    if r >= 2:
                        pe.wait_ge(s["o_free"], R * b + r - 1)
                    for t in range(r + 1):
                        last = mm(bank(6 + r % 2, P)[:, 0:C], prT[r % 2][:, t * P:(t + 1) * P], v0[:, t, :],
                                  start=(t == 0), stop=(t == r))
                    last.then_inc(s["o_ps"], 1)
                pe.wait_ge(s["xn_ready"], 2 * b + 2)
                transposes()
                pe.wait_ge(s["xT_sb"], 2 * b + 2)
                for u in range(2):
                    last = mm(bank(2 + u)[:, 0:HALF], g1[:], xnT[:, u * HALF:(u + 1) * HALF], start=True, stop=True)
                last.then_inc(s["q1_ps"], 1)
                pe.wait_ge(s["q1_done"], b + 1)
            stage_end(pe, 3)
            stage_end(pe, 4)
            if stop_after < 4:
                stage_end(pe, 5)
                return

            with pe.Fori(0, B) as b:
                with pe.Fori(0, NCH // 2) as c2:
                    for u in range(2):
                        n = NCH * b + 2 * c2 + u
                        pe.wait_ge(s_vf[u], 16 * ((NCH // 2) * b + c2 + 1))
                        pe.wait_ge(s["vps_free"], n + 1)
                        for t in range(6):
                            last = mm(bank(4 + t // 3, P)[:, (t % 3) * C:(t % 3 + 1) * C],
                                      vf[u][:, t * P:(t + 1) * P], m1[:], start=True, stop=True)
                        last.then_inc(s["vps_ready"], 1)
                        pe.wait_ge(s["khi_ready"], n + 1)
                        for r in range(R):
                            pe.wait_ge(s["mx_free"], R * n + r + 1)
                            for w in range(2):
                                last = mm(bank(2 * (r % 2) + w, P)[:, 0:HALF], q_hi[:, b, r * P:(r + 1) * P],
                                          k_hi[:, bass.ds(c2 * (2 * CH) + u * CH + w * HALF, HALF)],
                                          start=True, stop=True)
                            last.then_inc(s["mx_ps"], 1)
                        pe.wait_ge(s["vps_ready"], n + 1)
                        pe.sem_inc(s["vf_free"], 1)
                pe.wait_ge(s["shift_ready"], b + 1)
                pe.wait_ge(s["klo_ready"], NCH * (b + 1))
                pe.wait_ge(s["vp_ready"], NCH * (b + 1))
                for w in range(2):
                    mm(bank(6 + w, P)[:, 0:3 * (C + 1)], ones16[0:1, 0:P], zrow[:, 0:3 * (C + 1)], start=True, stop=False,
                       skip_group_check=True)

                def scores(kt, u, n):
                    if n is not None:
                        pe.wait_ge(s["st_free"], n)
                    kh, kl = k_hi[:, bass.ds(kt * P, P)], k_lo[:, bass.ds(kt * P, P)]
                    for w in range(2):
                        q = slice(w * HALF, (w + 1) * HALF)
                        o = bank(2 * u + w, P)[:, 0:HALF]
                        mm(o, kh, qb_hi[:, q], start=True, stop=False)
                        mm(o, kh, qb_lo[:, q], start=False, stop=False)
                    for w in range(2):
                        q = slice(w * HALF, (w + 1) * HALF)
                        mm(bank(2 * u + w, P)[:, 0:HALF], kl, qb_hi[:, q], start=False, stop=False)
                    for w in range(2):
                        last = mm(bank(2 * u + w, P)[:, 0:HALF], ones16[0:P, 0:P],
                                  shift.rearrange("p r q -> p (r q)")[:, w * HALF:(w + 1) * HALF],
                                  start=False, stop=True)
                    last.then_inc(s["st_ps"], 1)

                def weigh(kt, u, n):
                    pe.wait_ge(s["pt_ready"], n)
                    for r in range(R):
                        o = (r % 3) * (C + 1)
                        last = mm(ps[0:P, 6 + r // 3, o:o + C + 1], pt[u][:, r * P:(r + 1) * P],
                                  vp[:, bass.ds(kt, 1), :].rearrange("p a c -> p (a c)"),
                                  start=False, stop=False, skip_group_check=True)
                    last.then_inc(s["pt_free"], 1)

                scores(0, 0, None)
                with pe.Fori(0, KT // 2 - 1) as i:
                    scores(2 * i + 1, 1, KT * b + 2 * i + 2)
                    weigh(2 * i, 0, KT * b + 2 * i + 1)
                    scores(2 * i + 2, 0, KT * b + 2 * i + 3)
                    weigh(2 * i + 1, 1, KT * b + 2 * i + 2)
                scores(KT - 1, 1, KT * b + KT)
                weigh(KT - 2, 0, KT * b + KT - 1)
                weigh(KT - 1, 1, KT * b + KT)
                for w in range(2):
                    last = mm(bank(6 + w, P)[:, 0:3 * (C + 1)], ones16[0:1, 0:P], zrow[:, 0:3 * (C + 1)], start=False, stop=True,
                              skip_group_check=True)
                last.then_inc(s["acc_ps"], 1)
                pe.wait_ge(s["xn_ready"], 2 * B + b + 1)
                transposes()
                pe.wait_ge(s["xT_sb"], 2 * B + b + 1)
                for r in range(R):
                    o = bank(4, P)[:, r * E:(r + 1) * E]
                    mm(o, xnT[:, r * P:(r + 1) * P], rw_sb[:], start=True, stop=False)
                    last = mm(o, ones[0:1, 0:P], rb_sb[:], start=False, stop=True)
                last.then_inc(s["rl_ps"], 1)
                pe.wait_ge(s["msk_ready"], b + 1)
                for r in range(R + 1):
                    o = bank(5, P)[:, r * E:(r + 1) * E]
                    for t in range(min(r + 1, R)):
                        w = before if t == r else ones[0:P, 0:P]
                        last = mm(o, w[:] if t == r else w, msk[:, t, :], start=(t == 0), stop=(t == min(r, R - 1)))
                last.then_inc(s["pos_ps"], 1)
                pe.wait_ge(s["gT_in"], b + 1)
                for r in range(R):
                    last = nc.tensor.transpose(bank(2 + r // 3)[:, (r % 3) * P:(r % 3 + 1) * P], gate2[:, r, :],
                                               ident[0:P, 0:P])
                last.then_inc(s["gT_ps"], 1)
                pe.wait_ge(s["batch_done"], b + 1)
            stage_end(pe, 5)
            if stop_after < 9:
                return

            with pe.Fori(0, NMC) as c:
                xh, xl = x_hi[:, bass.ds(c * MT, MT)], x_lo[:, bass.ds(c * MT, MT)]
                gt = gates[:, bass.ds(c * MT, MT)]

                def up(sq, pair, u, n):
                    pe.wait_ge(s["up_free"], n)
                    for k, (wh, wl) in enumerate(((wg_hi, wg_lo), (wu_hi, wu_lo))):
                        o = bank(3 * u + k)[:, 0:MT]
                        mm(o, wh[:, bass.ds(sq * 128, 128)], xh, start=True, stop=False)
                        mm(o, wh[:, bass.ds(sq * 128, 128)], xl, start=False, stop=False)
                        last = mm(o, wl[:, bass.ds(sq * 128, 128)], xh, start=False, stop=True)
                    if pair is not None:
                        last = mm(bank(3 * u + 2)[:, 0:MT], sel_sb[:, bass.ds(pair * 128, 128)], gt,
                                  start=True, stop=True)
                    last.then_inc(s["up_ps"], 1)

                def down(sq, u, n):
                    pe.wait_ge(s["a_ready"], n)
                    for r in range(MT // P):
                        last = mm(bank(6, P)[:, r * C:(r + 1) * C], ac[u][:, r * P:(r + 1) * P],
                                  wd_sb[:, bass.ds(sq * C, C)], start=False, stop=False, skip_group_check=True)
                    last.then_inc(s["a_free"], 1)

                n0 = NSEQ * c
                pe.wait_ge(s["moe_free"], c + 1)
                mm(bank(6, P)[:, 0:4 * C], ones16[0:1, 0:P], zrow[:, 0:4 * C], start=True, stop=False,
                   skip_group_check=True)
                up(0, None, 0, n0 + 1)
                with pe.Fori(0, PAIRS // 2) as i:
                    up(2 * i + 1, 2 * i, 1, n0 + 2 * i + 2)
                    down(2 * i, 0, n0 + 2 * i + 1)
                    up(2 * i + 2, 2 * i + 1, 0, n0 + 2 * i + 3)
                    down(2 * i + 1, 1, n0 + 2 * i + 2)
                down(PAIRS, 0, n0 + NSEQ)
                mm(bank(6, P)[:, 0:4 * C], ones16[0:1, 0:P], zrow[:, 0:4 * C], start=False, stop=True,
                   skip_group_check=True).then_inc(s["moe_ps"], 1)


_STOP = 9


def _laid_out(i):
    f = lambda a: np.ascontiguousarray(np.asarray(a))
    x = f(i["x"])
    xp = np.zeros((B, LEFT + TP + TAPS - 1 - LEFT, C), x.dtype)
    xp[:, LEFT:LEFT + T_IN] = x
    half = GW * WT
    d = {
        "xT": f([xp[b, LEFT + half * u:LEFT + half * (u + 1)].T for b in range(B) for u in range(2)]),
        "xw": f([xp[b, WT * j:WT * j + WIN] for b in range(B) for j in range(NW)]),
        "WlT": f(np.asarray(i["L0_tok_Wl"]).T),
        "bl": f(i["L0_tok_bl"]).reshape(1, -1),
        "tok_bias": f(i["L0_tok_bias"]).reshape(-1, 1),
        "WcT": f(np.asarray(i["L0_tok_Wc"]).transpose(1, 2, 0).reshape(C, 8, WCH).transpose(1, 0, 2)),
        "bc": f(np.asarray(i["L0_tok_bc"]).reshape(MC, 128).T),
        "W2T": f(np.asarray(i["L0_tok_W2"]).T.reshape(MC, 128, C).transpose(1, 0, 2)),
        "b2": f(i["L0_tok_b2"]),
        "bo": f(i["L0_attn_b_out"]),
        "Wo": f(i["L0_attn_W_out"]),
        "k": f(i["L1_attn_k"]).reshape(B, C, KEYS),
        "v": f(i["L1_attn_v"]).reshape(B, C, KEYS),
        "W1": f(i["L1_attn_w_qkvs"]),
        "fcT": f(np.asarray(i["L1_attn_fc_w"]).T),
        "fcb": f(i["L1_attn_fc_b"]),
        "gamma": f(i["L1_attn_gamma"]),
        "beta": f(i["L1_attn_beta"]),
        "rwT": f(np.asarray(i["L1_ffn_router_w"]).T),
        "rb": f(i["L1_ffn_bias"]).reshape(1, -1),
    }
    qkv = np.asarray(i["L0_attn_W_qkv"])
    for n, name in enumerate(("WqT", "WkT", "WvT")):
        d[name] = f(qkv[:, 64 * n:64 * (n + 1)].T)

    def projection(shared, experts):
        w = np.concatenate([np.asarray(shared), np.asarray(experts)]).reshape(NSEQ * 128, C)
        return w.T.reshape(C, 3, NSEQ * 128 // 3).transpose(1, 0, 2)

    d["wgu"] = f(np.concatenate([projection(i["L1_ffn_shared_w_gate"], i["L1_ffn_w_gate"]),
                                 projection(i["L1_ffn_shared_w_up"], i["L1_ffn_w_up"])]))
    down = np.concatenate([np.asarray(i["L1_ffn_shared_w_down"]), np.asarray(i["L1_ffn_w_down"])])
    d["wdT"] = f(down.reshape(NSEQ, 2, C, FF).transpose(1, 3, 0, 2).reshape(128, NSEQ * C))

    t = (half * np.arange(2)[None, :, None, None] + WT * np.arange(GW)[None, None, :, None]
         + np.arange(WT)[:, None, None, None])
    at = t + np.arange(TAPS) - LEFT
    m = np.where((at >= 0) & (at < T_IN), 0.0, -3e38).astype(np.float32)
    d["mask"] = f(np.broadcast_to(m[:, :, :, None, :], (WT, 2, GW, HEADS, TAPS)).reshape(WT, 2, -1))
    d["ident"] = np.eye(128, dtype=np.float32)
    d["causal"] = np.triu(np.full((P, P), -1e30, np.float32), 1)
    d["before"] = np.triu(np.ones((P, P), np.float32), 1)
    r, c = np.arange(128)[:, None] % E, np.arange(PAIRS * 128)[None, :]
    d["sel"] = (r == 2 * (c // 128) + c % 128 // FF).astype(np.float16)
    return d


def kernel(**inputs):
    import concourse.bacc as bacc
    from concourse.bass_utils import run_bass_kernel_spmd

    arrays = _laid_out(inputs)
    nc = bacc.Bacc("TRN2", target_bir_lowering=False, num_devices=1)
    d = {n: nc.dram_tensor(f"in_{n}", a.shape, mybir.dt.from_np(a.dtype), kind="ExternalInput").ap()
         for n, a in arrays.items()}
    out = nc.dram_tensor("out", (B, T, C), F32, kind="ExternalOutput").ap()
    tower(nc, d, out, _STOP)
    r = run_bass_kernel_spmd(nc, [{f"in_{n}": a for n, a in arrays.items()}], core_ids=[0])
    return r.results[0]["out"]
```

```python
from contextlib import ExitStack, contextmanager

import numpy as np
import concourse.bass as bass
from concourse import mybir

F32 = mybir.dt.float32
F16 = mybir.dt.float16
ALU = mybir.AluOpType
ACT = mybir.ActivationFunctionType
AX = mybir.AxisListType.X

B, T_IN, C = 4, 750, 128
HEADS, TAPS = 4, 31
HID = 512
MC = HID // 128
T = T_IN - TAPS + 1
P = 120
R = T // P
HALF = T // 2
LEFT = (TAPS - 1) // 2
WT = 94
WIN = WT + TAPS - 1
NW = 8
GW = 4
TP = NW * WT
KEYS = 7200
KW = 128
KT = KEYS // KW
TAIL = KEYS - KT * KW
CH = 4 * KW
NCH = KEYS // CH
TILES = KT + 1
CHUNKS = NCH + 1
MAXIMA = NCH * R + 1
E, FF, TOPK = 64, 64, 6
CAP = int(B * T * TOPK * 2.0 / E)
PAIRS = E // 2
NSEQ = PAIRS + 1
MT = 480
NMC = B * T // MT
EPS = 1e-5
SELU_SCALE = 1.0507009873554804934193349852946
SELU_ALPHA = 1.6732632423543772848170429916717
W_SCALE = 256.0
X_SCALE = 16.0
A_SCALE = 4.0
NWP = 6
EV, OD = (TAPS + 1) // 2, TAPS // 2
XP = TP // 2
WPIECE = 2 * (EV // 2) * 128



DOWN, ATTN, MIX = "down", "attn", "mix"
ATTN_STEPS = ([("norm", 0), ("transpose", 0), ("query", 0), ("value", 0), ("score", 0), ("turn", 0)]
              + [x for r in range(R - 1) for x in (("score", r + 1), ("weigh", r), ("turn", r + 1))]
              + [("weigh", R - 1), ("norm", 1), ("norm", 2), ("transpose", 1), ("query", 1)])
MIX_STEPS = ([("logits", 0), ("logits", 1)]
             + [x for j in range(NW) for x in (("band", j), ("apply", j))] + [("split", 0)])


def side_steps(b):
    down = [(DOWN, b - 1, "h", k) for k in range(2)] if b else []
    attn = [(ATTN, b - 1, *x) for x in ATTN_STEPS] if b else []
    mix = [(MIX, b + 1, *x) for x in MIX_STEPS] if b + 1 < B else []
    steps, attn, mix = down + mix[:2] + attn[:3], attn[3:], mix[2:]
    while attn or mix:
        steps += mix[:1] + attn[:1]
        attn, mix = attn[1:], mix[1:]
    return steps


def layer_order(b):
    steps = side_steps(b)
    slots = 3 * MC * 4
    for i in range(slots):
        first, last = 2, slots
        now = [x for n, x in enumerate(steps) if first + n * (last - first) // max(len(steps), 1) == i]
        yield i // 12, i // 4 % 3, i % 4, now


def shared_turns():
    turns = {}
    steps = [(MIX, 0, *x) for x in MIX_STEPS]
    for b in range(B + 1):
        for kind, at, what, k in steps:
            if kind == DOWN or (kind == MIX and what != "split"):
                turns[kind, at, what, k] = len(turns) + 1
        steps = side_steps(b) if b < B else []
    for k in range(2):
        turns[DOWN, B - 1, "h", k] = len(turns) + 1
    return turns


SHARED = shared_turns()
PAIR_S = {x: n + 1 for n, x in enumerate([("transpose", 0), ("value", 0)] + [("score", r) for r in range(R)]
                                         + [("transpose", 1)])}
PAIR_T = {x: n + 1 for n, x in enumerate([("query", 0)] + [x for r in range(R) for x in (("turn", r), ("weigh", r))]
                                         + [("query", 1)])}
NS, NT = len(PAIR_S), len(PAIR_T)


class Order:

    def __init__(self, eng, sem):
        self.eng, self.sem, self.base, self.n = eng, sem, 0, 0

    def link(self, ins):
        ins.then_inc(self.sem, 1)
        self.n += 1
        self.eng.wait_ge(self.sem, self.base + self.n)

    @contextmanager
    def loop(self, count, per):
        before = self.base + self.n
        with self.eng.Fori(0, count) as i:
            self.base, self.n = before + i * per, 0
            yield i
            assert self.n == per, f"the body links {self.n} times, not {per}"
        self.base, self.n = before + count * per, 0


class Region:

    def __init__(self, tensor, words):
        self.tensor, self.words, self.at = tensor, words, 0

    def take(self, *shape, dtype=F32):
        n = int(np.prod(shape))
        words = n if dtype == F32 else (n + 1) // 2
        assert self.at + words <= self.words, (self.at + words, self.words)
        piece = self.tensor[:, self.at:self.at + words]
        self.at += words
        if dtype != F32:
            piece = piece.bitcast(dtype)[:, 0:n]
        if len(shape) == 2:
            piece = piece.rearrange("p (a b) -> p a b", a=shape[0])
        if len(shape) == 3:
            piece = piece.rearrange("p (a b c) -> p a b c", a=shape[0], b=shape[1])
        return piece


def tower(nc, d, out, stop_after=9):
    ctx = ExitStack()
    with ctx:
        def sb(name, shape, dt=F32):
            return ctx.enter_context(nc.sbuf_tensor(name, shape, dt))

        def sem(name):
            return ctx.enter_context(nc.semaphore(name))

        ps = ctx.enter_context(nc.psum_tensor("ps", [128, 8, 512], F32))

        h = sb("h", [P, B * R, C])
        xres = sb("xres", [P, B * R, C])
        gates = sb("gates", [128, B * T], F16)

        ident = sb("ident", [128, 128])
        ones = sb("ones", [128, 128])
        ones16 = sb("ones16", [128, 128], F16)
        causal = sb("causal", [P, P])
        before = sb("before", [P, P], F16)
        bc_sb = sb("bc_sb", [128, MC])
        tokb = sb("tokb", [128, 1])
        w2_sb = sb("w2_sb", [128, MC, C])
        rows = sb("rows", [P, 6, C])
        rw_sb = sb("rw_sb", [128, E])
        rb_sb = sb("rb_sb", [1, E])
        g0 = sb("g0", [128, 128])
        m0 = sb("m0", [128, 128])
        g1 = sb("g1", [128, 128])
        m1 = sb("m1", [128, 128])
        zrow = sb("zrow", [1, 512], F16)
        carry = sb("carry", [P, E])
        stats = sb("stats", [P, R, 6])
        mv = sb("mv", [P, R, 2])
        rstd = sb("rstd", [P, R])
        vare = sb("vare", [P, R])
        power = sb("power", [P, R])
        eps = sb("eps", [P, R])
        idle = sb("idle", [P, 1])
        mx2 = sb("mx2", [P, 2])
        nm = sb("nm", [P, R])
        sums = sb("sums", [P, R, 2])
        den = sb("den", [P, R])
        rden = sb("rden", [P, R])

        KSET = 14720
        region_k = Region(sb("region_k", [128, 2 * KSET]), 2 * KSET)
        wc = [[region_k.take(MC, n, 128, dtype=F16) for _ in range(2)] for n in (EV, OD, EV)]
        ys = [[[region_k.take(XP, dtype=F16) for _ in range(2)] for _ in range(3)] for _ in range(2)]
        zz = region_k.take(MC, T)
        k_hi, k_lo, v_hi, v_lo = [], [], [], []
        for n in range(2):
            region_k.at = n * KSET
            k_hi.append(region_k.take(KEYS, dtype=F16))
            k_lo.append(region_k.take(KEYS, dtype=F16))
            v_hi.append(region_k.take(TILES, C + 1, dtype=F16))
            v_lo.append(region_k.take(TILES, C + 1, dtype=F16))
        region_k.at = 0
        wg_hi, wg_lo, wu_hi, wu_lo, wd_hi, wd_lo = (region_k.take(NSEQ * 128, dtype=F16) for _ in range(6))
        sel_sb = region_k.take(PAIRS * 128, dtype=F16)
        assert region_k.at <= KSET

        region_b = Region(sb("region_b", [128, B * T]), B * T)
        q_hi = region_b.take(B, T, dtype=F16)
        q_lo = region_b.take(B, T, dtype=F16)
        x_hi = q_hi.rearrange("p b t -> p (b t)")
        x_lo = q_lo.rearrange("p b t -> p (b t)")

        gates32 = gates[:, :].bitcast(F32)
        taps = [gates32[0:WT, n * 496:(n + 1) * 496].rearrange("p (a k) -> p a k", k=TAPS) for n in range(2)]
        band = [gates32[0:WT, n * 496:(n + 1) * 496] for n in range(2)]
        bandT = gates32[0:WIN, 992:992 + HEADS * WT]
        xsum = gates32[:, 992:992 + XP]

        region_c = Region(sb("region_c", [128, 8060]), 8060)
        wq_sb = region_c.take(128)[0:64]
        wk_sb = region_c.take(128)[0:64]
        wv_sb = region_c.take(128)[0:64]
        wo_sb = region_c.take(128)[0:64]
        w1_sb = region_c.take(128)
        fc_sb = region_c.take(128)
        region_c.at = 0
        xn = region_c.take(R, C)[0:P]
        xnT = region_c.take(T)
        qg = region_c.take(T)
        v0 = region_c.take(R, C)[0:P]
        pr = region_c.take(T)[0:P]
        prT = region_c.take(T)[0:P]
        at_c = region_c.at
        region_c.at = 0
        wc_f = [region_c.take(WPIECE) for _ in range(2)]
        region_c.at = 0
        p_hi = [region_c.take(T, dtype=F16) for _ in range(2)]
        p_lo = [region_c.take(T, dtype=F16) for _ in range(2)]
        region_c.at = at_c
        even_sb = region_c.take(HALF + 1)
        z_even = region_c.take(HALF)
        z_odd = region_c.take(HALF)
        zn = region_c.take(HALF)
        wq_sb = region_c.take(128)[0:64]
        wk_sb = region_c.take(128)[0:64]
        wv_sb = region_c.take(128)[0:64]
        wo_sb = region_c.take(128)[0:64]
        w1_sb = region_c.take(128)
        fc_sb = region_c.take(128)
        ytmp = region_c.take(TP)
        xt = ytmp
        mask = region_c.take(2, TAPS)[0:WT]
        wmx = region_c.take(GW * HEADS)[0:WT]
        wsum = region_c.take(GW * HEADS)[0:WT]
        wrs = region_c.take(GW * HEADS)[0:WT]
        wl_sb = region_c.take(HEADS * TAPS)
        bl_sb = region_c.take(HEADS * TAPS)[0:1]
        xw = [region_c.take(C)[0:WIN] for _ in range(2)]
        region_c.at = at_c
        kf = [region_c.take(CH) for _ in range(2)]
        vf = [region_c.take(CH) for _ in range(2)]
        kf_tail = region_c.take(TAIL)
        vf_tail = region_c.take(TAIL)
        shift = [region_c.take(R, P, dtype=F16)[0:P] for _ in range(2)]
        mxk = region_c.take(R, CHUNKS)[0:P]
        region_c.at = at_c
        wf = [region_c.take(NSEQ * 128 // NWP) for _ in range(2)]
        region_c.at = 0
        region_c.take(R, C)
        region_c.take(T)
        hb = region_c.take(R, C)[0:P]
        lg = region_c.take(R, E)[0:P]
        probs = region_c.take(R, E + 2)[0:P]
        rep = region_c.take(R, E + 2)[0:P]
        top8 = region_c.take(R, 8)[0:P]
        top6 = region_c.take(R, 8)[0:P]
        msk = region_c.take(R, E, dtype=F16)[0:P]
        gate2 = region_c.take(R, 2 * E)[0:P]
        slot = region_c.take(R, E)[0:P]
        g_tmp = region_c.take(T, dtype=F16)
        region_c.at = 0
        sg = [region_c.take(MT) for _ in range(2)]
        su = [region_c.take(MT) for _ in range(2)]
        ac = [region_c.take(MT) for _ in range(2)]
        a_hi = [region_c.take(MT, dtype=F16) for _ in range(2)]
        a_lo = [region_c.take(MT, dtype=F16) for _ in range(2)]
        out_cm = region_c.take(MT)
        fin = region_c.take(MT // P, C)[0:P]

        band_dram = nc.dram_tensor("band_dram", [NW, WT, HEADS * WIN], F32).ap()

        names = """mix_in const_in ones_ready su_ready dve_own pool_own wprod_ps wprod_sb zero_ready zero_out
            x_in shifted exp_done w_ready band_written ysum_ready y_hi_done y_ready
            shared_full shared_free wc_hi_ready wc_lo_ready wc_sum wc_sum_hi wc_ready
            prod_full prod_free zneg_ready zexp_done z_ready h_ready
            s_full s_free t_full t_free nmax_ready xn_ready var_ready rstd_ready q_hi_done q_done
            xT_ps xT_sb
            klo_ready vps_ready vh_ready vl_ready mx_ps mx_free shift_ready
            st_ps p_hi_ready exp_sum lo_ready pv_done acc_ps acc_free wf_done
            rl_ps rl_sh rl_exp pos_ps msk_ready gT_in gT_ps gT_hi gT_done x3_hi xm_done batch_done
            gate_ps up_ps up_free silu_done a_ready a_hi_ready a_lo_ready down_done moe_ps
            out_cm_ready out_ps fin_ready fin_out
            stage""".split()
        s = {n: sem(n) for n in names}
        s_wc = [sem(f"wc_in{u}") for u in range(2)]
        s_band = [sem(f"band_in{u}") for u in range(2)]
        s_kf = [sem(f"kf_in{u}") for u in range(2)]
        s_vf = [sem(f"vf_in{u}") for u in range(2)]
        s_wf = [sem(f"wf_in{u}") for u in range(2)]
        s_tail = sem("tail_in")

        def bank(n, parts=128):
            return ps[0:parts, n]

        def two(n, parts=128):
            return ps[0:parts, n:n + 2, 0:HALF]

        def halves(ap):
            return ap.rearrange("p (a b) -> p a b", a=2)

        def stage_end(eng, n):
            eng.drain()
            eng.sem_inc(s["stage"], 1)
            eng.wait_ge(s["stage"], 5 * n)

        row = HEADS * WIN

        def band_taps(i):
            return bass.AP(tensor=band_dram.tensor, offset=i * (WT * row),
                           ap=[[row + 1, WT], [WIN, HEADS], [1, TAPS]])

        def taps_of(n):
            odd = 8 - n % 2
            piece = wc_f[n % 2][:, 0:(8 + odd) * 128].rearrange("p (t c) -> p t c", c=128)
            return piece[:, 0:8], piece[:, 8:8 + odd]

        def attn_banks(b):
            return 4 if b + 1 < B else 0

        SB = 3

        mix_loads = [(ident, "ident"), (wl_sb, "WlT"), (bl_sb, "bl"), (mask, "mask"), (tokb, "tok_bias")]
        const_loads = [
            (wq_sb, "WqT"), (wk_sb, "WkT"), (wv_sb, "WvT"), (wo_sb, "Wo"),
            (w1_sb, "W1"), (fc_sb, "fcT"), (bc_sb, "bc"), (w2_sb, "W2T"), (causal, "causal"),
            (before, "before"), (rw_sb, "rwT"), (rb_sb, "rb"),
        ]
        row_loads = ["b2", "bo", "fcb", "gamma", "beta"]
        MIX_IN = 16 * len(mix_loads)
        CONST_IN = 16 * (len(const_loads) + len(row_loads))

        block = ctx.enter_context(nc.Block())

        @block.sync
        def _(sp):
            sp.dma_start(xt, d["xT"][0]).then_inc(s["x_in"], 16)
            for dst, name in mix_loads:
                sp.dma_start(dst[:], d[name]).then_inc(s["mix_in"], 16)
            for dst, name in const_loads:
                sp.dma_start(dst[:], d[name]).then_inc(s["const_in"], 16)
            for n, name in enumerate(row_loads):
                sp.dma_start(rows[:, n, :], d[name].partition_broadcast(P)).then_inc(s["const_in"], 16)
            for b in range(B):
                if b:
                    sp.wait_ge(s["y_ready"], b)
                    sp.dma_start(xt, d["xT"][b]).then_inc(s["x_in"], 16)
                for j in range(NW):
                    if j == 0:
                        sp.wait_ge(s["band_written"], 16 * NW * (b + 1))
                    if j >= 2:
                        sp.wait_ge(s["shared_full"], SHARED[MIX, b, "apply", j - 2])
                    sp.dma_start(band[j % 2], band_dram[j]).then_inc(s_band[j % 2], 16)
                    sp.dma_start(xw[j % 2], d["xw"][NW * b + j]).then_inc(s_band[j % 2], 16)
            sp.wait_ge(s["z_ready"], 2 * MC * B)
            for b in range(B):
                if b >= 1:
                    sp.wait_ge(s["klo_ready"], 2 + CHUNKS * (b - 1) + 1)
                    sp.wait_ge(s["vps_ready"], 2 + CHUNKS * (b - 1) + 1)
                sp.dma_start(kf_tail, d["k"][b, :, KT * KW:]).then_inc(s_tail, 16)
                sp.dma_start(vf_tail, d["v"][b, :, KT * KW:]).then_inc(s_tail, 16)
                with sp.Fori(0, NCH // 2) as c2:
                    for u in range(2):
                        c = 2 * c2 + u
                        at = bass.ds(sp.snap(c2 * (2 * CH) + u * CH), CH)
                        sp.wait_ge(s["klo_ready"], 2 + CHUNKS * b + c)
                        sp.dma_start(kf[u], d["k"][b, :, at]).then_inc(s_kf[u], 16)
                        sp.wait_ge(s["vps_ready"], 2 + CHUNKS * b + c)
                        sp.dma_start(vf[u], d["v"][b, :, at]).then_inc(s_vf[u], 16)
            sp.wait_ge(s["klo_ready"], 2 + CHUNKS * B)
            sp.wait_ge(s["vps_ready"], 2 + CHUNKS * B)
            sp.wait_ge(s["acc_ps"], B - 1)
            sp.dma_start(sel_sb, d["sel"]).then_inc(s["const_in"], 16)
            for n in range(3 * NWP):
                if n >= 2:
                    sp.wait_ge(s["wf_done"], n - 1)
                sp.dma_start(wf[n % 2], d["experts"][n]).then_inc(s_wf[n % 2], 16)
            stage_end(sp, 1)
            stage_end(sp, 2)
            out_t = out.rearrange("b (r p) c -> p (b r) c", p=P)
            if stop_after < 9:
                sp.dma_start(out_t, h[:]).then_inc(s["fin_out"], 16)
                sp.wait_ge(s["fin_out"], 32)
                return
            with sp.Fori(0, NMC) as c:
                sp.wait_ge(s["fin_ready"], c + 1)
                sp.dma_start(out_t[:, bass.ds(c * (MT // P), MT // P), :], fin).then_inc(s["fin_out"], 16)
            sp.wait_ge(s["fin_out"], 16 * (NMC + 1))

        @block.gpsimd
        def _(pool):
            g = nc.gpsimd
            for name, n in (("klo_ready", 2), ("vps_ready", 2), ("vl_ready", 1), ("mx_free", 1),
                            ("up_free", 2), ("down_done", 2), ("fin_out", 16)):
                if n:
                    pool.sem_inc(s[name], n)
            g.memset(xsum, 0.0).then_inc(s["zero_ready"], 1)
            for n in range(2):
                pool.dma_start(wc_f[n][:, 0:(2048, 1920)[n % 2]], d["WcT"][n][:, 0:(2048, 1920)[n % 2]]
                               ).then_inc(s_wc[n % 2], 16)
            g.memset(power[:], -0.5)
            g.memset(eps[:], EPS)
            g.memset(carry[:], 0.0)
            g.memset(ones16[:], 1.0)
            g.memset(zrow[:], 0.0)
            g.memset(ones[:], 1.0).then_inc(s["ones_ready"], 1)
            own = Order(pool, s["pool_own"])

            for n in range(2 * MC):
                m, half = divmod(n, 2)
                e, o = taps_of(n)
                pool.wait_ge(s["wc_lo_ready"], n + 1)
                own.link(g.tensor_tensor(e[:, 0:o.shape[1]], e[:, 0:o.shape[1]], o, ALU.add))
                own.link(g.tensor_scalar(e, e, W_SCALE, None, ALU.mult))
                pool.sem_inc(s["wc_sum"], 1)
                pool.wait_ge(s["wc_sum_hi"], n + 1)
                at = slice(8 * half, 8 * half + 8)
                g.tensor_tensor(wc[2][1][:, m, at], e, wc[2][0][:, m, at], ALU.subtract
                                ).then_inc(s["wc_ready"], 1)
                if n + 2 < 2 * MC:
                    pool.wait_ge(s["wc_ready"], n + 1)
                    w = (2048, 1920)[n % 2]
                    pool.dma_start(wc_f[n % 2][:, 0:w], d["WcT"][n + 2][:, 0:w]).then_inc(s_wc[n % 2], 16)

            def power_of_variance(n):
                pool.wait_ge(s["var_ready"], n)
                own.link(g.tensor_tensor(vare[:], mv[:, :, 1], eps[:], ALU.add))
                g.tensor_tensor(rstd[:], vare[:], power[:], ALU.pow).then_inc(s["rstd_ready"], 1)

            for n in range(3 * (B - 1)):
                power_of_variance(n + 1)
            pool.wait_ge(s["prod_full"], 3 * MC * B)
            for b in range(B):
                kh, kl = k_hi[b % 2], k_lo[b % 2]
                if b < 2:
                    g.memset(v_hi[b][:, :, C:C + 1], 1.0)
                    g.memset(v_lo[b][:, :, C:C + 1], 0.0)
                if b >= 2:
                    pool.wait_ge(s["acc_ps"], b - 1)
                pool.wait_ge(s_tail, 32 * (b + 1))
                own.link(g.tensor_copy(kh[:, KT * KW:], kf_tail))
                g.tensor_tensor(kl[:, KT * KW:], kf_tail, kh[:, KT * KW:], ALU.subtract
                                ).then_inc(s["klo_ready"], 1)

                def split(c2, u):
                    at = bass.ds(c2 * (2 * CH) + u * CH, CH)
                    pool.wait_ge(s_kf[u], 16 * ((NCH // 2) * b + c2 + 1))
                    pool.wait_ge(s["ones_ready"], 1)
                    own.link(g.tensor_copy(kh[:, at], kf[u]))
                    g.tensor_tensor(kl[:, at], kf[u], kh[:, at], ALU.subtract).then_inc(s["klo_ready"], 1)

                if b == 0:
                    for c in range(NCH):
                        for k, (what, r) in enumerate(ATTN_STEPS):
                            if what == "norm" and k // 2 == c - 1:
                                power_of_variance(3 * (B - 1) + r + 1)
                        split(c // 2, c % 2)
                else:
                    with own.loop(NCH // 2, 2) as c2:
                        for u in range(2):
                            split(c2, u)
            pool.wait_ge(s["acc_ps"], B - 1)
            for n in range(3 * NWP):
                part = slice((n % NWP) * (NSEQ * 128 // NWP), (n % NWP + 1) * (NSEQ * 128 // NWP))
                hi, lo = ((wg_hi, wg_lo), (wu_hi, wu_lo), (wd_hi, wd_lo))[n // NWP]
                pool.wait_ge(s_wf[n % 2], 16 * (n // 2 + 1))
                own.link(g.tensor_scalar(wf[n % 2], wf[n % 2], X_SCALE, None, ALU.mult))
                own.link(g.tensor_copy(hi[:, part], wf[n % 2]))
                g.tensor_tensor(lo[:, part], wf[n % 2], hi[:, part], ALU.subtract).then_inc(s["wf_done"], 1)
            stage_end(pool, 1)
            with own.loop(B, 2) as b:
                for n in range(2):
                    power_of_variance(3 * B + 2 * b + n + 1)
            stage_end(pool, 2)
            if stop_after < 9:
                return
            def low_part(n, u):
                pool.wait_ge(s["a_hi_ready"], n + 1)
                g.tensor_tensor(a_lo[u], ac[u], a_hi[u], ALU.subtract).then_inc(s["a_lo_ready"], 1)

            with pool.Fori(0, NMC) as c:
                low_part(NSEQ * c, 0)
                with pool.Fori(0, PAIRS // 2) as i:
                    low_part(NSEQ * c + 2 * i + 1, 1)
                    low_part(NSEQ * c + 2 * i + 2, 0)

        @block.scalar
        def _(act):
            a = nc.scalar

            act.wait_ge(s["zero_ready"], 1)
            for n in range(2):
                act.dma_start(band_dram.rearrange("i p (a n) -> p i a n", a=2)[:, :, n],
                              xsum[0:WT, 0:HEADS * WIN // 2].unsqueeze(1).broadcast_to((WT, NW, HEADS * WIN // 2))
                              ).then_inc(s["zero_out"], 16)

            def mix(b, what, k):
                if what == "logits":
                    act.wait_ge(s["shifted"], 2 * b + k + 1)
                    a.activation(taps[k], taps[k], ACT.Exp).then_inc(s["exp_done"], 1)
                    act.wait_ge(s["w_ready"], 2 * b + k + 1)
                    for j in range(GW):
                        act.dma_start(band_taps(GW * k + j), taps[k][:, HEADS * j:HEADS * (j + 1), :]
                                      ).then_inc(s["band_written"], 16)
                elif what == "band":
                    act.wait_ge(s["shared_full"], SHARED[MIX, b, what, k])
                    a.activation(bandT, bank(SB, WIN)[:, 0:HEADS * WT], ACT.Copy).then_inc(s["shared_free"], 1)
                elif what == "split":
                    act.wait_ge(s["ysum_ready"], b + 1)
                    y = ytmp.rearrange("p (n two) -> p n two", two=2)
                    a.activation(ys[b % 2][0][0], y[:, :, 0], ACT.Copy)
                    a.activation(ys[b % 2][1][0], y[:, :, 1], ACT.Copy)
                    a.activation(ys[b % 2][2][0], xsum, ACT.Copy).then_inc(s["y_hi_done"], 1)

            def attn(b, what, k):
                bk = attn_banks(b)
                if (what, k) in PAIR_S and what != "value":
                    if what == "score":
                        act.wait_ge(s["nmax_ready"], R * b + k + 1)
                        n1 = min(k + 1, 3) * P
                        last = a.activation(pr[:, 0:n1], bank(bk, P)[:, 0:n1], ACT.Exp, bias=nm[:, k:k + 1],
                                            accum_out=sums[:, k, 0:1])
                        if k >= 3:
                            last = a.activation(pr[:, HALF:(k + 1) * P], bank(bk + 1, P)[:, 0:(k - 2) * P],
                                                ACT.Exp, bias=nm[:, k:k + 1], accum_out=sums[:, k, 1:2])
                    else:
                        act.wait_ge(s["s_full"], NS * b + PAIR_S[what, k])
                        last = a.activation(halves(xnT), two(bk), ACT.Copy)
                    last.then_inc(s["s_free"], 1)
                elif (what, k) == ("query", 0):
                    act.wait_ge(s["t_full"], NT * b + PAIR_T[what, k])
                    a.activation(halves(qg), two(bk + 2), ACT.Copy).then_inc(s["t_free"], 1)
                elif (what, k) == ("query", 1):
                    act.wait_ge(s["t_full"], NT * b + PAIR_T[what, k])
                    a.activation(halves(q_hi[:, b, :]), two(bk + 2), ACT.Copy).then_inc(s["q_hi_done"], 1)
                elif what == "turn":
                    act.wait_ge(s["t_full"], NT * b + PAIR_T[what, k])
                    last = a.activation(prT[:, 0:min(k + 1, 3) * P], bank(bk + 2, P)[:, 0:min(k + 1, 3) * P], ACT.Copy)
                    if k >= 3:
                        last = a.activation(prT[:, HALF:(k + 1) * P], bank(bk + 3, P)[:, 0:(k - 2) * P], ACT.Copy)
                    last.then_inc(s["t_free"], 1)

            def weights(n):
                m, half = divmod(n, 2)
                e, o = taps_of(n)
                act.wait_ge(s_wc[n % 2], 16 * (n // 2 + 1))
                a.activation(wc[0][0][:, m, 8 * half:8 * half + 8], e, ACT.Copy, scale=W_SCALE)
                a.activation(wc[1][0][:, m, 8 * half:8 * half + o.shape[1]], o, ACT.Copy, scale=W_SCALE
                             ).then_inc(s["wc_hi_ready"], 1)
                act.wait_ge(s["wc_sum"], n + 1)
                a.activation(wc[2][0][:, m, 8 * half:8 * half + 8], e, ACT.Copy).then_inc(s["wc_sum_hi"], 1)

            def product_done(b, m, p):
                if p:
                    act.wait_ge(s["zneg_ready"], 2 * (MC * b + m) + p)
                    a.activation(zn, zn, ACT.Exp).then_inc(s["zexp_done"], 1)

            act.wait_ge(s["zero_out"], 32)
            for n, (what, k) in enumerate(MIX_STEPS):
                mix(0, what, k)
                if n % 2 == 0 and n // 2 < 2 * MC:
                    weights(n // 2)
            act.wait_ge(s["wprod_ps"], 1)
            for n, (dst, scale) in enumerate(((g0, 64 ** -0.5), (m0, 1.0), (g1, C ** -0.5), (m1, 1.0))):
                last = a.activation(dst[:], bank(6)[:, 128 * n:128 * (n + 1)], ACT.Copy, scale=scale)
            last.then_inc(s["wprod_sb"], 1)
            for b in range(B):
                for m, p, quarter, steps in layer_order(b):
                    if quarter == 3:
                        product_done(b, m, p)
                    for kind, at, what, k in steps:
                        if kind == MIX:
                            mix(at, what, k)
                        if kind == ATTN:
                            attn(at, what, k)

            def exponentials(b, t, u, parts=KW):
                act.wait_ge(s["st_ps"], TILES * b + t + 1)
                if not isinstance(t, int) or t > 1:
                    act.wait_ge(s["pv_done"], TILES * b + t - 1)
                elif b:
                    act.wait_ge(s["pv_done"], TILES * b)
                st = two(2 * u, parts)
                a.activation(halves(p_hi[u][0:parts]), st, ACT.Exp).then_inc(s["p_hi_ready"], 1)
                a.activation(st, st, ACT.Exp).then_inc(s["exp_sum"], 1)

            def values_high(b, c, parts=KW):
                n = CHUNKS * b + 1 + c
                act.wait_ge(s["vps_ready"], 2 + n + 1)
                if isinstance(c, int) and c < 0:
                    a.activation(v_hi[b % 2][0:TAIL, KT, 0:C], bank(5, TAIL)[:, 0:C], ACT.Copy
                                 ).then_inc(s["vh_ready"], 1)
                else:
                    act.wait_ge(s["ones_ready"], 1)
                    a.activation(v_hi[b % 2][:, bass.ds(c * 4, 4), 0:C],
                                 bank(5).rearrange("p (t c) -> p t c", c=C), ACT.Copy).then_inc(s["vh_ready"], 1)

            values_high(0, -1)
            for c in range(NCH):
                for what, k in ATTN_STEPS[2 * c:2 * c + 2]:
                    attn(B - 1, what, k)
                values_high(0, c)
            for b in range(B):
                exponentials(b, 0, 0)
                if b + 1 < B:
                    values_high(b + 1, -1)
                exponentials(b, 1, 1)

                def eight(i, ts):
                    for t in ts:
                        exponentials(b, 8 * i + t, t % 2)
                        if t % 4 == 2 and b + 1 < B:
                            values_high(b + 1, 2 * i + t // 4)

                eight(0, range(2, 8))
                with act.Fori(1, NCH // 2) as i:
                    eight(i, range(8))
                exponentials(b, KT, 0, TAIL)
            stage_end(act, 1)
            with act.Fori(0, B) as b:
                act.wait_ge(s["xT_ps"], b + 1)
                a.activation(halves(xnT), two(0), ACT.Copy).then_inc(s["xT_sb"], 1)
                act.wait_ge(s["rl_sh"], b + 1)
                a.activation(probs[:, :, 0:E], lg, ACT.Exp).then_inc(s["rl_exp"], 1)
                act.wait_ge(s["xT_sb"], b + 1)
                a.activation(q_hi[:, b, :], xnT, ACT.Copy).then_inc(s["x3_hi"], 1)
                act.wait_ge(s["gT_ps"], b + 1)
                a.activation(halves(gates[0:E, bass.ds(b * T, T)]), two(2, E), ACT.Copy)
                a.activation(halves(g_tmp[E:128]), ps[E:128, 2:4, 0:HALF], ACT.Copy
                             ).then_inc(s["gT_hi"], 1)
            stage_end(act, 2)
            if stop_after < 9:
                return

            def silu(n, u):
                act.wait_ge(s["gate_ps"], n + 1)
                act.wait_ge(s["up_free"], n + 1)
                a.activation(sg[u], bank(3 * u)[:, 0:MT], ACT.Silu, scale=1 / X_SCALE).then_inc(s["silu_done"], 1)

            def high_part(n, u):
                act.wait_ge(s["a_ready"], n + 1)
                act.wait_ge(s["down_done"], n + 1)
                a.activation(a_hi[u], ac[u], ACT.Copy).then_inc(s["a_hi_ready"], 1)

            with act.Fori(0, NMC) as c:
                n0 = NSEQ * c
                silu(n0, 0)
                with act.Fori(0, PAIRS // 2) as i:
                    silu(n0 + 2 * i + 1, 1)
                    high_part(n0 + 2 * i, 0)
                    silu(n0 + 2 * i + 2, 0)
                    high_part(n0 + 2 * i + 1, 1)
                high_part(n0 + PAIRS, 0)
                act.wait_ge(s["down_done"], 2 + NSEQ * (c + 1))
                a.activation(out_cm, bank(6)[:, 0:MT], ACT.Copy, scale=1 / (A_SCALE * X_SCALE)
                             ).then_inc(s["out_cm_ready"], 1)

        @block.vector
        def _(dve):
            v = nc.vector
            own = Order(dve, s["dve_own"])

            dve.wait_ge(s["mix_in"], MIX_IN)

            def mix(b, what, k):
                if what == "logits":
                    dve.wait_ge(s["shared_full"], SHARED[MIX, b, what, k])
                    raw = bank(SB, WT)[:, 0:GW * HEADS * TAPS].rearrange("p (a k) -> p a k", k=TAPS)
                    edge = raw[:, 0:HEADS] if k == 0 else raw[:, (GW - 1) * HEADS:]
                    own.link(v.tensor_tensor(edge, edge, mask[:, k:k + 1, :].broadcast_to((WT, HEADS, TAPS)),
                                             ALU.add))
                    own.link(v.tensor_reduce(wmx, raw, AX, ALU.max))
                    v.tensor_tensor(taps[k], raw, wmx.unsqueeze(2).broadcast_to((WT, GW * HEADS, TAPS)),
                                    ALU.subtract).then_inc(s["shifted"], 1)
                    dve.wait_ge(s["shifted"], 2 * b + k + 1)
                    dve.sem_inc(s["shared_free"], 1)
                    dve.wait_ge(s["exp_done"], 2 * b + k + 1)
                    own.link(v.tensor_reduce(wsum, taps[k], AX, ALU.add))
                    own.link(v.reciprocal(wrs, wsum))
                    v.tensor_tensor(taps[k], taps[k], wrs.unsqueeze(2).broadcast_to((WT, GW * HEADS, TAPS)),
                                    ALU.mult).then_inc(s["w_ready"], 1)
                elif what == "apply":
                    dve.wait_ge(s["shared_full"], SHARED[MIX, b, what, k])
                    for g in range(HEADS):
                        lo, hi = g * 32, (g + 1) * 32
                        last = v.tensor_scalar(ytmp[lo:hi, k * WT:(k + 1) * WT], ps[lo:hi, SB, g * WT:(g + 1) * WT],
                                               tokb[lo:hi, :], None, ALU.add)
                    own.link(last)
                    dve.sem_inc(s["shared_free"], 1)
                elif what == "split":
                    own.link(v.memset(ytmp[:, T_IN:TP], 0.0))
                    y = ytmp.rearrange("p (n two) -> p n two", two=2)
                    own.link(v.tensor_tensor(xsum[:, 0:XP - 1], y[:, 0:XP - 1, 1], y[:, 1:XP, 0], ALU.add))
                    own.link(v.tensor_copy(xsum[:, XP - 1:XP], y[:, XP - 1:XP, 1]))
                    dve.sem_inc(s["ysum_ready"], 1)
                    dve.wait_ge(s["y_hi_done"], b + 1)
                    for n, src in enumerate((y[:, :, 0], y[:, :, 1], xsum)):
                        last = v.tensor_tensor(ys[b % 2][n][1], src, ys[b % 2][n][0], ALU.subtract)
                    last.then_inc(s["y_ready"], 1)

            def weights(n):
                m, half = divmod(n, 2)
                dve.wait_ge(s["wc_hi_ready"], n + 1)
                for k, src in enumerate(taps_of(n)):
                    at = slice(8 * half, 8 * half + src.shape[1])
                    last = v.scalar_tensor_tensor(
                        out=wc[k][1][:, m, at].rearrange("p t c -> p (t c)"), in0=src.rearrange("p t c -> p (t c)"),
                        scalar=W_SCALE, in1=wc[k][0][:, m, at].rearrange("p t c -> p (t c)"),
                        op0=ALU.mult, op1=ALU.subtract)
                last.then_inc(s["wc_lo_ready"], 1)

            def selu(b, m, odd, z):
                n = 2 * (MC * b + m) + odd
                bias = bc_sb[:, m:m + 1]
                v.tensor_scalar(zn, z, bias, 0.0, ALU.add, ALU.min).then_inc(s["zneg_ready"], 1)
                own.link(v.tensor_scalar(z, z, bias, 0.0, ALU.add, ALU.max))
                dve.wait_ge(s["zexp_done"], n + 1)
                own.link(v.tensor_scalar(zn, zn, -1.0, SELU_SCALE * SELU_ALPHA, ALU.add, ALU.mult))
                v.scalar_tensor_tensor(out=zz[:, m, :].rearrange("p (n two) -> p n two", two=2)[:, :, odd], in0=z,
                                       scalar=SELU_SCALE, in1=zn, op0=ALU.mult, op1=ALU.add
                                       ).then_inc(s["z_ready"], 1)
                dve.wait_ge(s["z_ready"], n + 1)

            def product_done(b, m, p):
                dve.wait_ge(s["prod_full"], 3 * (MC * b + m) + p + 1)
                if p == 0:
                    own.link(v.tensor_scalar(even_sb, bank(0)[:, 0:HALF + 1], 1 / W_SCALE, None, ALU.mult))
                    dve.sem_inc(s["prod_free"], 1)
                elif p == 1:
                    v.scalar_tensor_tensor(out=z_even, in0=bank(1)[:, 0:HALF], scalar=1 / W_SCALE,
                                           in1=even_sb[:, 0:HALF], op0=ALU.mult, op1=ALU.add)
                    own.link(v.scalar_tensor_tensor(out=z_odd, in0=bank(1)[:, 0:HALF], scalar=-1 / W_SCALE,
                                                    in1=even_sb[:, 1:HALF + 1], op0=ALU.mult, op1=ALU.subtract))
                    dve.sem_inc(s["prod_free"], 1)
                    selu(b, m, 0, z_even)
                else:
                    own.link(v.scalar_tensor_tensor(out=z_odd, in0=bank(2)[:, 0:HALF], scalar=1 / W_SCALE,
                                                    in1=z_odd, op0=ALU.mult, op1=ALU.add))
                    dve.sem_inc(s["prod_free"], 1)
                    selu(b, m, 1, z_odd)

            def down(b, k):
                dve.wait_ge(s["shared_full"], SHARED[DOWN, b, "h", k])
                own.link(v.tensor_tensor(h[:, b * R + 3 * k:b * R + 3 * k + 3, :],
                                         bank(SB, P)[:, 0:3 * C].rearrange("p (r c) -> p r c", c=C),
                                         rows[:, 0:1, :].broadcast_to((P, 3, C)), ALU.add))
                dve.sem_inc(s["shared_free"], 1)

            def layer_norm(dst, src, n):
                for r in range(R):
                    last = v.bn_stats(stats[:, r, :], src[:, r, :])
                own.link(last)
                v.memset(idle[:], 0.0)
                for r in range(R):
                    last = v.bn_aggr(mv[:, r, :], stats[:, r, :])
                last.then_inc(s["var_ready"], 1)
                dve.wait_ge(s["var_ready"], n)
                dve.wait_ge(s["rstd_ready"], n)
                for r in range(R):
                    last = v.tensor_scalar(dst[:, r, :], src[:, r, :], mv[:, r, 0:1], rstd[:, r:r + 1],
                                           ALU.subtract, ALU.mult)
                own.link(last)

            def attn(b, what, k):
                bk = attn_banks(b)
                x = h[:, b * R:(b + 1) * R, :]
                if (what, k) == ("norm", 0):
                    layer_norm(xn, x, 3 * b + 1)
                    dve.sem_inc(s["xn_ready"], 1)
                elif what == "value":
                    dve.wait_ge(s["s_full"], NS * b + PAIR_S[what, k])
                    v.tensor_copy(v0.rearrange("p (a r) c -> p a r c", a=2),
                                  ps[0:P, bk:bk + 2, 0:3 * C].rearrange("p a (r c) -> p a r c", c=C)
                                  ).then_inc(s["s_free"], 1)
                elif what == "score":
                    dve.wait_ge(s["s_full"], NS * b + PAIR_S[what, k])
                    diag = bank(bk + k // 3, P)[:, (k % 3) * P:(k % 3 + 1) * P]
                    own.link(v.tensor_tensor(diag, diag, causal[:], ALU.add))
                    last = v.tensor_reduce(mx2[:, 0:1], bank(bk, P)[:, 0:min(k + 1, 3) * P], AX, ALU.max)
                    if k >= 3:
                        last = v.tensor_reduce(mx2[:, 1:2], bank(bk + 1, P)[:, 0:(k - 2) * P], AX, ALU.max)
                    own.link(last)
                    own.link(v.tensor_reduce(nm[:, k:k + 1], mx2[:, 0:1 + k // 3], AX, ALU.max, negate=True))
                    dve.sem_inc(s["nmax_ready"], 1)
                elif what == "weigh":
                    own.link(v.tensor_reduce(den[:, k:k + 1], sums[:, k, 0:1 + k // 3], AX, ALU.add))
                    own.link(v.reciprocal(rden[:, k:k + 1], den[:, k:k + 1]))
                    dve.wait_ge(s["t_full"], NT * b + PAIR_T[what, k])
                    own.link(v.scalar_tensor_tensor(out=x[:, k, :], in0=bank(bk + 2, P)[:, 0:C],
                                                    scalar=rden[:, k:k + 1], in1=x[:, k, :],
                                                    op0=ALU.mult, op1=ALU.add))
                    dve.sem_inc(s["t_free"], 1)
                elif (what, k) == ("norm", 1):
                    own.link(v.tensor_tensor(x, x, rows[:, 1:2, :].broadcast_to((P, R, C)), ALU.add))
                    layer_norm(xn, x, 3 * b + 2)
                elif (what, k) == ("norm", 2):
                    own.link(v.tensor_tensor(x, x, xn, ALU.add))
                    layer_norm(xres[:, b * R:(b + 1) * R, :], x, 3 * b + 3)
                    dve.sem_inc(s["xn_ready"], 1)
                elif (what, k) == ("query", 1):
                    dve.wait_ge(s["q_hi_done"], b + 1)
                    own.link(v.tensor_tensor(halves(q_lo[:, b, :]), two(bk + 2), halves(q_hi[:, b, :]), ALU.subtract))
                    dve.sem_inc(s["t_free"], 1)
                    dve.sem_inc(s["q_done"], 1)

            for n, (what, k) in enumerate(MIX_STEPS):
                mix(0, what, k)
                if n % 2 == 0 and n // 2 < 2 * MC:
                    weights(n // 2)
            dve.wait_ge(s["const_in"], CONST_IN)
            for b in range(B):
                for m, p, quarter, steps in layer_order(b):
                    if quarter == 3:
                        product_done(b, m, p)
                    for kind, at, what, k in steps:
                        if kind == MIX:
                            mix(at, what, k)
                        if kind == ATTN:
                            attn(at, what, k)
                        if kind == DOWN:
                            down(at, k)
            for k in range(2):
                down(B - 1, k)

            def low_part(b, t, u, parts=KW):
                dve.wait_ge(s["exp_sum"], TILES * b + t + 1)
                v.tensor_tensor(halves(p_lo[u][0:parts]), two(2 * u, parts), halves(p_hi[u][0:parts]),
                                ALU.subtract).then_inc(s["lo_ready"], 1)

            def maximum_of(b, c, r):
                dve.wait_ge(s["mx_ps"], MAXIMA * b + 1 + R * c + r + 1)
                bk = 7 if b == 0 and r % 2 == 0 else 4
                v.tensor_reduce(mxk[:, r, bass.ds(c + 1, 1)], bank(bk, P), AX, ALU.max).then_inc(s["mx_free"], 1)

            def values_low(b, c):
                dve.wait_ge(s["vh_ready"], CHUNKS * b + 1 + c + 1)
                v.tensor_tensor(v_lo[b % 2][:, bass.ds(c * 4, 4), 0:C], bank(5).rearrange("p (t c) -> p t c", c=C),
                                v_hi[b % 2][:, bass.ds(c * 4, 4), 0:C], ALU.subtract).then_inc(s["vl_ready"], 1)

            def prepare(b, c, part):
                for r in ((0, 1), (2,), (3, 4), (5,))[part]:
                    maximum_of(b, c, r)
                if part == 2:
                    values_low(b, c)

            def prepare_tail(b):
                dve.wait_ge(s["vh_ready"], CHUNKS * b + 1)
                v.tensor_tensor(v_lo[b % 2][0:TAIL, KT, 0:C], bank(5, TAIL)[:, 0:C], v_hi[b % 2][0:TAIL, KT, 0:C],
                                ALU.subtract).then_inc(s["vl_ready"], 1)
                dve.wait_ge(s["mx_ps"], MAXIMA * b + 1)
                v.tensor_reduce(mxk[:, :, 0], bank(4, P)[:, 0:R * TAIL].rearrange("p (r k) -> p r k", r=R),
                                AX, ALU.max).then_inc(s["mx_free"], 1)

            def shifts(b):
                dve.wait_ge(s["mx_free"], 1 + MAXIMA * (b + 1))
                own.link(v.tensor_reduce(nm[:], mxk, AX, ALU.max, negate=True))
                for r in range(R):
                    last = v.tensor_scalar(shift[b % 2][:, r, :], ident[0:P, 0:P], nm[:, r:r + 1], None, ALU.mult)
                last.then_inc(s["shift_ready"], 1)

            prepare_tail(0)
            for c in range(NCH):
                for r in range(3):
                    maximum_of(0, c, r)
                for what, k in ATTN_STEPS[2 * c:2 * c + 2]:
                    attn(B - 1, what, k)
                for r in range(3, R):
                    maximum_of(0, c, r)
                values_low(0, c)
            shifts(0)
            for b in range(B):
                if b + 1 < B:
                    prepare_tail(b + 1)
                with dve.Fori(0, NCH // 2) as i:
                    for t in range(8):
                        low_part(b, 8 * i + t, t % 2)
                        if b + 1 < B:
                            prepare(b + 1, 2 * i + t // 4, t % 4)
                if b + 1 < B:
                    shifts(b + 1)
                low_part(b, KT, 0, TAIL)
                dve.wait_ge(s["acc_ps"], b + 1)
                for r in range(R):
                    o = (r % 3) * (C + 1)
                    last = v.reciprocal(rden[:, r:r + 1], ps[0:P, 6 + r // 3, o + C:o + C + 1])
                own.link(last)
                for r in range(R):
                    o = (r % 3) * (C + 1)
                    x = xres[:, b * R + r, :]
                    last = v.scalar_tensor_tensor(out=x, in0=ps[0:P, 6 + r // 3, o:o + C],
                                                  scalar=rden[:, r:r + 1], in1=x, op0=ALU.mult, op1=ALU.add)
                last.then_inc(s["acc_free"], 1)
            stage_end(dve, 1)
            f_links = 28
            with own.loop(B, f_links) as b:
                at = bass.ds(b * R, R)
                own.link(v.tensor_copy(hb, xres[:, at, :]))
                own.link(v.tensor_tensor(hb, hb, rows[:, 2:3, :].broadcast_to((P, R, C)), ALU.add))
                layer_norm(xn, hb, 3 * B + 2 * b + 1)
                own.link(v.tensor_tensor(xn, xn, rows[:, 3:4, :].broadcast_to((P, R, C)), ALU.mult))
                own.link(v.tensor_tensor(xn, xn, rows[:, 4:5, :].broadcast_to((P, R, C)), ALU.add))
                own.link(v.tensor_tensor(hb, xn, h[:, at, :], ALU.add))
                layer_norm(xn, hb, 3 * B + 2 * b + 2)
                dve.sem_inc(s["xn_ready"], 1)
                own.link(v.tensor_copy(h[:, at, :], hb))
                dve.wait_ge(s["rl_ps"], b + 1)
                rl = bank(4, P)[:, 0:R * E].rearrange("p (r e) -> p r e", e=E)
                own.link(v.tensor_reduce(den[:], rl, AX, ALU.max))
                v.tensor_tensor(lg, rl, den[:].unsqueeze(2).broadcast_to((P, R, E)), ALU.subtract
                                ).then_inc(s["rl_sh"], 1)
                v.memset(probs[:, :, E:E + 2], -1.0)
                v.memset(top6, -1.0)
                dve.wait_ge(s["rl_exp"], b + 1)
                own.link(v.tensor_reduce(den[:], probs[:, :, 0:E], AX, ALU.add))
                own.link(v.reciprocal(rden[:], den[:]))
                own.link(v.tensor_tensor(probs[:, :, 0:E], probs[:, :, 0:E],
                                         rden[:].unsqueeze(2).broadcast_to((P, R, E)), ALU.mult))
                v.memset(idle[:], 0.0)
                for r in range(R):
                    last = v.max(top8[:, r, :], probs[:, r, 0:E])
                own.link(last)
                own.link(v.tensor_copy(top6[:, :, 0:TOPK], top8[:, :, 0:TOPK]))
                v.memset(idle[:], 0.0)
                for r in range(R):
                    last = v.match_replace(rep[:, r, :], top6[:, r, :], probs[:, r, :], -2.0)
                own.link(last)
                own.link(v.tensor_scalar(msk, rep[:, :, 0:E], -1.5, None, ALU.is_lt))
                dve.sem_inc(s["msk_ready"], 1)
                own.link(v.tensor_reduce(den[:], top8[:, :, 0:TOPK], AX, ALU.add))
                own.link(v.tensor_scalar(den[:], den[:], 1e-9, None, ALU.add))
                own.link(v.reciprocal(rden[:], den[:]))
                own.link(v.tensor_tensor(probs[:, :, 0:E], probs[:, :, 0:E], msk, ALU.mult))
                dve.wait_ge(s["pos_ps"], b + 1)
                own.link(v.tensor_tensor(slot, bank(5, P)[:, 0:R * E].rearrange("p (r e) -> p r e", e=E),
                                         carry[:].unsqueeze(1).broadcast_to((P, R, E)), ALU.add))
                v.tensor_scalar(slot, slot, float(CAP), X_SCALE, ALU.is_lt, ALU.mult)
                own.link(v.tensor_tensor(carry[:], carry[:], bank(5, P)[:, R * E:R * E + E], ALU.add))
                own.link(v.tensor_tensor(slot, slot, probs[:, :, 0:E], ALU.mult))
                rb = rden[:].unsqueeze(2).broadcast_to((P, R, E))
                v.tensor_tensor(gate2[:, :, 0:E], slot, rb, ALU.mult)
                own.link(v.tensor_tensor(gate2[:, :, E:2 * E], slot, rb, ALU.mult))
                dve.sem_inc(s["gT_in"], 1)
                dve.wait_ge(s["x3_hi"], b + 1)
                own.link(v.tensor_tensor(q_lo[:, b, :], xnT, q_hi[:, b, :], ALU.subtract))
                dve.wait_ge(s["gT_hi"], b + 1)
                own.link(v.tensor_tensor(halves(gates[E:128, bass.ds(b * T, T)]), ps[E:128, 2:4, 0:HALF],
                                         halves(g_tmp[E:128]), ALU.subtract))
                dve.sem_inc(s["batch_done"], 1)
            stage_end(dve, 2)
            if stop_after < 9:
                return
            def product(n, u, m):
                dve.wait_ge(s["silu_done"], n + 1)
                dve.wait_ge(s["up_ps"], n + 1)
                v.scalar_tensor_tensor(out=su[u], in0=sg[u], scalar=A_SCALE / X_SCALE ** 2,
                                       in1=bank(3 * u + 1)[:, 0:MT], op0=ALU.mult, op1=ALU.mult
                                       ).then_inc(s["su_ready"], 1)
                dve.wait_ge(s["su_ready"], m)
                dve.wait_ge(s["down_done"], n + 1)
                v.tensor_tensor(ac[u], su[u], bank(3 * u + 2)[:, 0:MT], ALU.mult).then_inc(s["a_ready"], 1)
                dve.wait_ge(s["a_ready"], n + 1)
                dve.sem_inc(s["up_free"], 1)

            with own.loop(NMC, 2) as c:
                n0 = NSEQ * c
                dve.wait_ge(s["silu_done"], n0 + 1)
                dve.wait_ge(s["up_ps"], n0 + 1)
                own.link(v.scalar_tensor_tensor(out=ac[0], in0=sg[0], scalar=A_SCALE * 0.5 / X_SCALE,
                                                in1=bank(1)[:, 0:MT], op0=ALU.mult, op1=ALU.mult))
                dve.sem_inc(s["up_free"], 1)
                dve.sem_inc(s["a_ready"], 1)
                with dve.Fori(0, PAIRS // 2) as i:
                    product(n0 + 2 * i + 1, 1, PAIRS * c + 2 * i + 1)
                    product(n0 + 2 * i + 2, 0, PAIRS * c + 2 * i + 2)
                dve.wait_ge(s["out_ps"], c + 1)
                dve.wait_ge(s["fin_out"], 16 * (c + 1))
                own.link(v.tensor_tensor(fin, bank(7, P).rearrange("p (r c) -> p r c", c=C),
                                         h[:, bass.ds(c * (MT // P), MT // P), :], ALU.add))
                dve.sem_inc(s["fin_ready"], 1)

        @block.tensor
        def _(pe):
            mm = nc.tensor.matmul

            def mix(b, what, k):
                if what == "split":
                    return
                turn = SHARED[MIX, b, what, k]
                if what == "logits":
                    pe.wait_ge(s["x_in"], 16 * (b + 1))
                elif what == "band":
                    pe.wait_ge(s_band[k % 2], 32 * (NW // 2 * b + k // 2 + 1))
                if turn > 1:
                    pe.wait_ge(s["shared_free"], turn - 1)
                if what == "logits":
                    for j in range(GW):
                        o = bank(SB, WT)[:, j * HEADS * TAPS:(j + 1) * HEADS * TAPS]
                        mm(o, xt[:, (GW * k + j) * WT:(GW * k + j + 1) * WT], wl_sb, start=True, stop=False)
                        last = mm(o, ones[0:1, 0:WT], bl_sb, start=False, stop=True)
                elif what == "band":
                    for g in range(HEADS):
                        last = nc.tensor.transpose(bank(SB, WIN)[:, g * WT:(g + 1) * WT],
                                                   band[k % 2][:, g * WIN:(g + 1) * WIN], ident[0:WT, 0:WT])
                else:
                    last = mm(bank(SB)[:, 0:HEADS * WT], xw[k % 2], bandT, start=True, stop=True)
                last.then_inc(s["shared_full"], 1)

            def down(b, k):
                pe.wait_ge(s["z_ready"], 2 * MC * (b + 1))
                pe.wait_ge(s["shared_free"], SHARED[DOWN, b, "h", k] - 1)
                for r in range(3):
                    t = (3 * k + r) * P
                    for m in range(MC):
                        last = mm(bank(SB, P)[:, r * C:(r + 1) * C], zz[:, m, t:t + P], w2_sb[:, m, :],
                                  start=(m == 0), stop=(m == MC - 1))
                last.then_inc(s["shared_full"], 1)

            def attn(b, what, k):
                bk = attn_banks(b)
                if what == "norm":
                    return
                if (what, k) in PAIR_S:
                    full = s["s_full"]
                    if NS * b + PAIR_S[what, k] > 1:
                        pe.wait_ge(s["s_free"], NS * b + PAIR_S[what, k] - 1)
                else:
                    full = s["t_full"]
                    if NT * b + PAIR_T[what, k] > 1:
                        pe.wait_ge(s["t_free"], NT * b + PAIR_T[what, k] - 1)
                if what == "transpose":
                    pe.wait_ge(s["xn_ready"], 2 * b + k + 1)
                    src = xn if k == 0 else xres[:, b * R:(b + 1) * R, :]
                    for r in range(R):
                        last = nc.tensor.transpose(bank(bk + r // 3)[:, (r % 3) * P:(r % 3 + 1) * P], src[:, r, :],
                                                   ident[0:P, 0:P])
                elif what == "query":
                    pe.wait_ge(s["s_free"], NS * b + PAIR_S["transpose", k])
                    for u in range(2):
                        last = mm(bank(bk + 2 + u)[:, 0:HALF], (g0, g1)[k][:], xnT[:, u * HALF:(u + 1) * HALF],
                                  start=True, stop=True)
                elif what == "value":
                    for r in range(R):
                        last = mm(bank(bk + r // 3, P)[:, (r % 3) * C:(r % 3 + 1) * C], xnT[:, r * P:(r + 1) * P],
                                  m0[:], start=True, stop=True)
                elif what == "score":
                    pe.wait_ge(s["t_free"], NT * b + PAIR_T["query", 0])
                    q = qg[:, k * P:(k + 1) * P]
                    last = mm(bank(bk, P)[:, 0:min(k + 1, 3) * P], q, xnT[:, 0:min(k + 1, 3) * P],
                              start=True, stop=True)
                    if k >= 3:
                        last = mm(bank(bk + 1, P)[:, 0:(k - 2) * P], q, xnT[:, HALF:(k + 1) * P],
                                  start=True, stop=True)
                elif what == "turn":
                    pe.wait_ge(s["s_free"], NS * b + PAIR_S["score", k])
                    for t in range(k + 1):
                        last = nc.tensor.transpose(bank(bk + 2 + t // 3, P)[:, (t % 3) * P:(t % 3 + 1) * P],
                                                   pr[:, t * P:(t + 1) * P], ident[0:P, 0:P])
                elif what == "weigh":
                    for t in range(k + 1):
                        last = mm(bank(bk + 2, P)[:, 0:C], prT[:, t * P:(t + 1) * P], v0[:, t, :],
                                  start=(t == 0), stop=(t == k))
                last.then_inc(full, 1)

            def conv(b, m, p, quarter):
                n = (EV, OD, EV)[p]
                if quarter == 0:
                    turn = 3 * (MC * b + m) + p
                    if turn >= 3:
                        pe.wait_ge(s["prod_free"], turn - 2)
                    if m == 0 and p == 0:
                        pe.wait_ge(s["y_ready"], b + 1)
                    if b == 0 and p == 0:
                        pe.wait_ge(s["wc_ready"], 2 * (m + 1))
                w = HALF + (p == 0)
                o = bank(p)[:, 0:w]
                xh, xl = ys[b % 2][p]
                wh, wl = wc[p]
                for j in range(4 * quarter, min(4 * quarter + 4, n)):
                    mm(o, wh[:, m, j], xh[:, j:j + w], start=(j == 0), stop=False)
                    mm(o, wh[:, m, j], xl[:, j:j + w], start=False, stop=False)
                    last = mm(o, wl[:, m, j], xh[:, j:j + w], start=False, stop=(j == n - 1))
                if quarter == 3:
                    last.then_inc(s["prod_full"], 1)

            pe.wait_ge(s["mix_in"], MIX_IN)
            pe.wait_ge(s["ones_ready"], 1)
            for n, (what, k) in enumerate(MIX_STEPS):
                mix(0, what, k)
                if n == 1:
                    pe.wait_ge(s["const_in"], CONST_IN)
                    mm(bank(6)[:, 0:128], wq_sb, wk_sb, start=True, stop=True)
                    mm(bank(6)[:, 128:256], wv_sb, wo_sb, start=True, stop=True)
                    mm(bank(6)[:, 256:384], w1_sb, w1_sb, start=True, stop=True)
                    mm(bank(6)[:, 384:512], w1_sb, fc_sb, start=True, stop=True).then_inc(s["wprod_ps"], 1)
            pe.wait_ge(s["wprod_sb"], 1)
            for b in range(B):
                for m, p, quarter, steps in layer_order(b):
                    conv(b, m, p, quarter)
                    for kind, at, what, k in steps:
                        if kind == MIX:
                            mix(at, what, k)
                        if kind == ATTN:
                            attn(at, what, k)
                        if kind == DOWN:
                            down(at, k)
            for k in range(2):
                down(B - 1, k)

            def transposes():
                for r in range(R):
                    last = nc.tensor.transpose(bank(r // 3)[:, (r % 3) * P:(r % 3 + 1) * P], xn[:, r, :],
                                               ident[0:P, 0:P])
                last.then_inc(s["xT_ps"], 1)

            def project(b, c2, u):
                pe.wait_ge(s_vf[u], 16 * ((NCH // 2) * b + c2 + 1))
                pe.wait_ge(s["vl_ready"], CHUNKS * b + 2 * c2 + u + 2)
                for t in range(4):
                    last = mm(bank(5)[:, t * C:(t + 1) * C], vf[u][:, t * KW:(t + 1) * KW], m1[:],
                              start=True, stop=True)
                last.then_inc(s["vps_ready"], 1)

            def maximum_of(b, c2, u, r):
                pe.wait_ge(s["klo_ready"], 2 + CHUNKS * b + 2 * c2 + u + 2)
                pe.wait_ge(s["mx_free"], MAXIMA * b + 1 + R * (2 * c2 + u) + r + (b > 0))
                bk = 7 if b == 0 and r % 2 == 0 else 4
                mm(bank(bk, P), q_hi[:, b, r * P:(r + 1) * P], k_hi[b % 2][:, bass.ds(c2 * (2 * CH) + u * CH, CH)],
                   start=True, stop=True).then_inc(s["mx_ps"], 1)

            def prepare_tail(b):
                pe.wait_ge(s_tail, 32 * (b + 1))
                pe.wait_ge(s["vl_ready"], CHUNKS * b + 1)
                mm(bank(5, TAIL)[:, 0:C], vf_tail, m1[:], start=True, stop=True).then_inc(s["vps_ready"], 1)
                pe.wait_ge(s["klo_ready"], 2 + CHUNKS * b + 1)
                pe.wait_ge(s["mx_free"], MAXIMA * b + 1)
                for r in range(R):
                    last = mm(bank(4, P)[:, r * TAIL:(r + 1) * TAIL], q_hi[:, b, r * P:(r + 1) * P],
                              k_hi[b % 2][:, KT * KW:], start=True, stop=True)
                last.then_inc(s["mx_ps"], 1)

            def key_scores(b, t, u, parts=KW):
                first = isinstance(t, int) and t < 2
                if b or not first:
                    pe.wait_ge(s["lo_ready"], TILES * b + (0 if first else t - 1))
                at = slice(t * KW, t * KW + parts) if isinstance(t, int) else bass.ds(t * KW, parts)
                kh, kl = k_hi[b % 2][:, at], k_lo[b % 2][:, at]
                for w in range(2):
                    q = slice(w * HALF, (w + 1) * HALF)
                    mm(bank(2 * u + w, parts)[:, 0:HALF], kh, q_hi[:, b, q], start=True, stop=False)
                    mm(bank(2 * u + w, parts)[:, 0:HALF], kh, q_lo[:, b, q], start=False, stop=False)
                for w in range(2):
                    q = slice(w * HALF, (w + 1) * HALF)
                    mm(bank(2 * u + w, parts)[:, 0:HALF], kl, q_hi[:, b, q], start=False, stop=False)
                sh = shift[b % 2].rearrange("p r q -> p (r q)")
                for w in range(2):
                    last = mm(bank(2 * u + w, parts)[:, 0:HALF], ones16[0:P, 0:parts],
                              sh[:, w * HALF:(w + 1) * HALF], start=False, stop=True)
                last.then_inc(s["st_ps"], 1)

            def weigh(b, t, u, parts=KW):
                at = slice(t, t + 1) if isinstance(t, int) else bass.ds(t, 1)
                vh = v_hi[b % 2][0:parts, at, :].rearrange("p a c -> p (a c)")
                vl = v_lo[b % 2][0:parts, at, :].rearrange("p a c -> p (a c)")

                def sums(r):
                    o = (r % 3) * (C + 1)
                    return ps[0:P, 6 + r // 3, o:o + C + 1]

                pe.wait_ge(s["p_hi_ready"], TILES * b + t + 1)
                for r in range(R):
                    ph = p_hi[u][0:parts, r * P:(r + 1) * P]
                    mm(sums(r), ph, vh, start=False, stop=False, skip_group_check=True)
                    mm(sums(r), ph, vl, start=False, stop=False, skip_group_check=True)
                pe.wait_ge(s["lo_ready"], TILES * b + t + 1)
                for r in range(R):
                    last = mm(sums(r), p_lo[u][0:parts, r * P:(r + 1) * P], vh, start=False, stop=False,
                              skip_group_check=True)
                last.then_inc(s["pv_done"], 1)

            def zero_sums(start):
                for w in range(2):
                    last = mm(bank(6 + w, P)[:, 0:3 * (C + 1)], ones16[0:1, 0:P], zrow[:, 0:3 * (C + 1)],
                              start=start, stop=not start, skip_group_check=True)
                return last

            pe.wait_ge(s["s_free"], NS * (B - 1))
            pe.wait_ge(s["t_free"], NT * (B - 1))
            prepare_tail(0)
            for c in range(NCH):
                for r in range(3):
                    maximum_of(0, c // 2, c % 2, r)
                project(0, c // 2, c % 2)
                for what, k in ATTN_STEPS[2 * c:2 * c + 2]:
                    attn(B - 1, what, k)
                for r in range(3, R):
                    maximum_of(0, c // 2, c % 2, r)
            pe.wait_ge(s["q_done"], B)
            for b in range(B):
                pe.wait_ge(s["klo_ready"], 2 + CHUNKS * (b + 1))
                pe.wait_ge(s["vl_ready"], 1 + CHUNKS * (b + 1))
                pe.wait_ge(s["shift_ready"], b + 1)
                key_scores(b, 0, 0)
                if b:
                    pe.wait_ge(s["acc_free"], b)
                zero_sums(True)
                if b + 1 < B:
                    prepare_tail(b + 1)

                def eight(i, last):
                    for t in range(8):
                        if last and t == 7:
                            key_scores(b, KT, 0, TAIL)
                        else:
                            key_scores(b, 8 * i + t + 1, (t + 1) % 2)
                        u = t // 4
                        if b + 1 < B:
                            maximum_of(b + 1, i, u, (0, 2, 3, 5)[t % 4])
                        weigh(b, 8 * i + t, t % 2)
                        if b + 1 < B:
                            if t % 4 == 1:
                                project(b + 1, i, u)
                            elif t % 4 != 3:
                                maximum_of(b + 1, i, u, (1, None, 4)[t % 4])

                eight(0, False)
                with pe.Fori(1, NCH // 2 - 1) as i:
                    eight(i, False)
                eight(NCH // 2 - 1, True)
                weigh(b, KT, 0, TAIL)
                zero_sums(False).then_inc(s["acc_ps"], 1)
            stage_end(pe, 1)
            with pe.Fori(0, B) as b:
                pe.wait_ge(s["xn_ready"], 2 * B + b + 1)
                transposes()
                pe.wait_ge(s["xT_sb"], b + 1)
                for r in range(R):
                    o = bank(4, P)[:, r * E:(r + 1) * E]
                    mm(o, xnT[:, r * P:(r + 1) * P], rw_sb[:], start=True, stop=False)
                    last = mm(o, ones[0:1, 0:P], rb_sb[:], start=False, stop=True)
                last.then_inc(s["rl_ps"], 1)
                pe.wait_ge(s["msk_ready"], b + 1)
                for r in range(R + 1):
                    o = bank(5, P)[:, r * E:(r + 1) * E]
                    for t in range(min(r + 1, R)):
                        w = before if t == r else ones16[0:P, 0:P]
                        last = mm(o, w[:] if t == r else w, msk[:, t, :], start=(t == 0), stop=(t == min(r, R - 1)))
                last.then_inc(s["pos_ps"], 1)
                pe.wait_ge(s["gT_in"], b + 1)
                for r in range(R):
                    last = nc.tensor.transpose(bank(2 + r // 3)[:, (r % 3) * P:(r % 3 + 1) * P], gate2[:, r, :],
                                               ident[0:P, 0:P])
                last.then_inc(s["gT_ps"], 1)
                pe.wait_ge(s["batch_done"], b + 1)
            stage_end(pe, 2)
            if stop_after < 9:
                return

            with pe.Fori(0, NMC) as c:
                xh, xl = x_hi[:, bass.ds(c * MT, MT)], x_lo[:, bass.ds(c * MT, MT)]
                gt = gates[:, bass.ds(c * MT, MT)]

                def up(sq, pair, u, n):
                    pe.wait_ge(s["up_free"], n + 1)
                    for k, (wh, wl) in enumerate(((wg_hi, wg_lo), (wu_hi, wu_lo))):
                        o = bank(3 * u + k)[:, 0:MT]
                        mm(o, wh[:, bass.ds(sq * 128, 128)], xh, start=True, stop=False)
                        mm(o, wh[:, bass.ds(sq * 128, 128)], xl, start=False, stop=False)
                        last = mm(o, wl[:, bass.ds(sq * 128, 128)], xh, start=False, stop=True)
                        if k == 0:
                            last.then_inc(s["gate_ps"], 1)
                    if pair is not None:
                        last = mm(bank(3 * u + 2)[:, 0:MT], sel_sb[:, bass.ds(pair * 128, 128)], gt,
                                  start=True, stop=True)
                    last.then_inc(s["up_ps"], 1)

                def down(sq, u, n, start=False, stop=False):
                    pe.wait_ge(s["a_lo_ready"], n + 1)
                    o = bank(6)[:, 0:MT]
                    mm(o, wd_hi[:, bass.ds(sq * C, C)], a_hi[u], start=start, stop=False)
                    mm(o, wd_hi[:, bass.ds(sq * C, C)], a_lo[u], start=False, stop=False)
                    mm(o, wd_lo[:, bass.ds(sq * C, C)], a_hi[u], start=False, stop=stop
                       ).then_inc(s["down_done"], 1)

                n0 = NSEQ * c
                up(0, None, 0, n0)
                up(1, 0, 1, n0 + 1)
                up(2, 1, 0, n0 + 2)
                down(0, 0, n0, start=True)
                with pe.Fori(0, PAIRS // 2 - 1) as i:
                    up(2 * i + 3, 2 * i + 2, 1, n0 + 2 * i + 3)
                    down(2 * i + 1, 1, n0 + 2 * i + 1)
                    up(2 * i + 4, 2 * i + 3, 0, n0 + 2 * i + 4)
                    down(2 * i + 2, 0, n0 + 2 * i + 2)
                down(PAIRS - 1, 1, n0 + PAIRS - 1)
                down(PAIRS, 0, n0 + PAIRS, stop=True)
                pe.wait_ge(s["out_cm_ready"], c + 1)
                for r in range(MT // P):
                    last = nc.tensor.transpose(bank(7, P)[:, r * C:(r + 1) * C], out_cm[:, r * P:(r + 1) * P],
                                               ident[:])
                last.then_inc(s["out_ps"], 1)


_STOP = 9


def _pieces(w):
    w = w.reshape(MC, 128, C, TAPS).transpose(0, 2, 3, 1)
    out = np.zeros((2 * MC, C, WPIECE // 128, 128), w.dtype)
    for n in range(2 * MC):
        part = w[n // 2, :, 16 * (n % 2):16 * (n % 2) + 16]
        both = np.concatenate([part[:, 0::2], part[:, 1::2]], axis=1)
        out[n, :, :both.shape[1]] = both
    return out.reshape(2 * MC, C, WPIECE)


def _laid_out(i):
    f = lambda a: np.ascontiguousarray(np.asarray(a))
    x = f(i["x"])
    xp = np.zeros((B, TP + TAPS - 1, C), x.dtype)
    xp[:, LEFT:LEFT + T_IN] = x
    half = GW * WT
    d = {
        "xT": f([xp[b, LEFT:LEFT + TP].T for b in range(B)]),
        "xw": f([xp[b, WT * j:WT * j + WIN] for b in range(B) for j in range(NW)]),
        "WlT": f(np.asarray(i["L0_tok_Wl"]).T),
        "bl": f(i["L0_tok_bl"]).reshape(1, -1),
        "tok_bias": f(i["L0_tok_bias"]).reshape(-1, 1),
        "WcT": _pieces(np.asarray(i["L0_tok_Wc"])),
        "bc": f(np.asarray(i["L0_tok_bc"]).reshape(MC, 128).T),
        "W2T": f(np.asarray(i["L0_tok_W2"]).T.reshape(MC, 128, C).transpose(1, 0, 2)),
        "b2": f(i["L0_tok_b2"]),
        "bo": f(i["L0_attn_b_out"]),
        "Wo": f(i["L0_attn_W_out"]),
        "k": f(i["L1_attn_k"]).reshape(B, C, KEYS),
        "v": f(i["L1_attn_v"]).reshape(B, C, KEYS),
        "W1": f(i["L1_attn_w_qkvs"]),
        "fcT": f(np.asarray(i["L1_attn_fc_w"]).T),
        "fcb": f(i["L1_attn_fc_b"]),
        "gamma": f(i["L1_attn_gamma"]),
        "beta": f(i["L1_attn_beta"]),
        "rwT": f(np.asarray(i["L1_ffn_router_w"]).T),
        "rb": f(i["L1_ffn_bias"]).reshape(1, -1),
    }
    qkv = np.asarray(i["L0_attn_W_qkv"])
    for n, name in enumerate(("WqT", "WkT", "WvT")):
        d[name] = f(qkv[:, 64 * n:64 * (n + 1)].T)

    def pieces(w):
        return w.reshape(128, NWP, NSEQ * 128 // NWP).transpose(1, 0, 2)

    def projection(shared, experts):
        return pieces(np.concatenate([np.asarray(shared), np.asarray(experts)]).reshape(NSEQ * 128, C).T)

    down = np.concatenate([np.asarray(i["L1_ffn_shared_w_down"]), np.asarray(i["L1_ffn_w_down"])])
    d["experts"] = f(np.concatenate([
        projection(i["L1_ffn_shared_w_gate"], i["L1_ffn_w_gate"]),
        projection(i["L1_ffn_shared_w_up"], i["L1_ffn_w_up"]),
        pieces(down.reshape(NSEQ, 2, C, FF).transpose(1, 3, 0, 2).reshape(128, NSEQ * C))]))

    t = (half * np.arange(2)[None, :, None, None] + WT * np.arange(GW)[None, None, :, None]
         + np.arange(WT)[:, None, None, None])
    at = t + np.arange(TAPS) - LEFT
    m = np.where((at >= 0) & (at < T_IN), 0.0, -3e38).astype(np.float32)
    d["mask"] = f(np.stack([m[:, 0, 0], m[:, 1, GW - 1]], axis=1))
    d["ident"] = np.eye(128, dtype=np.float32)
    d["causal"] = np.triu(np.full((P, P), -1e30, np.float32), 1)
    d["before"] = np.triu(np.ones((P, P), np.float16), 1)
    r, c = np.arange(128)[:, None] % E, np.arange(PAIRS * 128)[None, :]
    d["sel"] = (r == 2 * (c // 128) + c % 128 // FF).astype(np.float16)
    return d


def kernel(**inputs):
    import concourse.bacc as bacc
    from concourse.bass_utils import run_bass_kernel_spmd

    arrays = _laid_out(inputs)
    nc = bacc.Bacc("TRN2", target_bir_lowering=False, num_devices=1)
    d = {n: nc.dram_tensor(f"in_{n}", a.shape, mybir.dt.from_np(a.dtype), kind="ExternalInput").ap()
         for n, a in arrays.items()}
    out = nc.dram_tensor("out", (B, T, C), F32, kind="ExternalOutput").ap()
    tower(nc, d, out, _STOP)
    r = run_bass_kernel_spmd(nc, [{f"in_{n}": a for n, a in arrays.items()}], core_ids=[0])
    return r.results[0]["out"]
```

```python
from contextlib import ExitStack, contextmanager

import numpy as np
import concourse.bass as bass
from concourse import mybir

F32 = mybir.dt.float32
F16 = mybir.dt.float16
ALU = mybir.AluOpType
ACT = mybir.ActivationFunctionType
AX = mybir.AxisListType.X

B, T_IN, C = 4, 750, 128
HEADS, TAPS = 4, 31
HID = 512
MC = HID // 128
T = T_IN - TAPS + 1
P = 120
R = T // P
HALF = T // 2
LEFT = (TAPS - 1) // 2
WT = 94
WIN = WT + TAPS - 1
NW = 8
GW = 4
TP = NW * WT
KEYS = 7200
KW = 128
KT = KEYS // KW
TAIL = KEYS - KT * KW
CH = 4 * KW
NCH = KEYS // CH
TILES = KT + 1
CHUNKS = NCH + 1
MAXIMA = NCH * R + 1
E, FF, TOPK = 64, 64, 6
CAP = int(B * T * TOPK * 2.0 / E)
PAIRS = E // 2
NSEQ = PAIRS + 1
MT = 480
NMC = B * T // MT
EPS = 1e-5
SELU_SCALE = 1.0507009873554804934193349852946
SELU_ALPHA = 1.6732632423543772848170429916717
W_SCALE = 256.0
X_SCALE = 16.0
A_SCALE = 4.0
NWP = 6
EV, OD = (TAPS + 1) // 2, TAPS // 2
XP = TP // 2
WPIECE = 2 * (EV // 2) * 128



DOWN, ATTN, MIX = "down", "attn", "mix"
MIX_SPAN, ATTN_SPAN = (1, 43), (3, 48)
ATTN_STEPS = ([("stats", 0), ("norm", 0), ("transpose", 0), ("query", 0), ("value", 0), ("score", 0), ("turn", 0)]
              + [x for r in range(R - 1) for x in (("score", r + 1), ("weigh", r), ("turn", r + 1))]
              + [("weigh", R - 1), ("norm", 1), ("norm", 2), ("transpose", 1), ("query", 1)])
LAST_ATTN_STEPS = ATTN_STEPS[1:-4]
MIX_STEPS = ([("logits", 0), ("logits", 1), ("taps", 0), ("taps", 1)]
             + [x for j in range(NW) for x in (("band", j), ("apply", j))] + [("split", 0)])
MIX_ALONE = ([("logits", 0), ("logits", 1), ("taps", 0), ("taps", 1), ("high", 0), ("low", 0), ("high", 1),
              ("low", 1), ("band", 0), ("sums", 0)]
             + [x for j in range(NW - 1) for x in (("band", j + 1), ("apply", j)) + (("sums", 1),) * (j == 4)]
             + [("apply", NW - 1), ("split", 0)])
WEIGHTS_AT = {12 * (m - 1) + at: (what, 2 * m + half) for m in range(1, MC)
              for half in range(2) for at, what in ((4 * half, "high"), (4 * half + 1, "low"), (4 * half + 3, "sums"))}


LONG = {("taps", 1): 4, ("norm", 0): 2, ("norm", 1): 3, ("norm", 2): 3}
NBAND = 6
QUARTERS = 3 * MC * 4


def side_steps(b):
    down = [(DOWN, b - 1, "h", k) for k in range(2)] if b else []
    attn = [(ATTN, b - 1, *x) for x in ATTN_STEPS] if b else []
    mix = [(MIX, b + 1, *x) for x in MIX_STEPS] if b + 1 < B else []
    steps = [(at, (MIX, 0, *x)) for at, x in WEIGHTS_AT.items()] if b == 0 else []
    for row, (first, last) in ((mix, MIX_SPAN), (down + attn, ATTN_SPAN)):
        times = [LONG.get(x[2:], 1) for x in row]
        steps += [(first + sum(times[:n]) * (last - first) // sum(times), x) for n, x in enumerate(row)]
    return sorted(steps, key=lambda x: x[0])


def layer_order(b):
    steps = side_steps(b)
    for i in range(QUARTERS):
        yield i // 12, i // 4 % 3, i % 4, [x for at, x in steps if at == i]


def shared_turns():
    turns, left, read = {}, {}, {"act_read": 0, "dve_read": 0}
    steps = [(MIX, 0, *x) for x in MIX_ALONE]
    for b in range(B + 1):
        for x in steps + [(DOWN, B - 1, "h", k) for k in range(2)] * (b == B):
            kind, at, what, k = x
            if what not in ("logits", "band", "apply", "h"):
                continue
            bank = 3
            if kind == MIX and at == 0:
                bank = ((1, 2) if what == "band" else (3, 0))[k % 2]
            reader = "act_read" if what == "band" else "dve_read"
            read[reader] += 1
            turns[x] = (len(turns) + 1, bank, left.get(bank), read[reader])
            left[bank] = (reader, read[reader])
        steps = [x for _, x in side_steps(b)] if b < B else []
    return turns


SHARED = shared_turns()
PAIR_S = {x: n + 1 for n, x in enumerate([("transpose", 0), ("value", 0)] + [("score", r) for r in range(R)]
                                         + [("transpose", 1)])}
PAIR_T = {x: n + 1 for n, x in enumerate([("query", 0)] + [x for r in range(R) for x in (("turn", r), ("weigh", r))]
                                         + [("query", 1)])}
NS, NT = len(PAIR_S), len(PAIR_T)

EIGHTS = KEYS // KW // 8
FIRST, LAST = 3, EIGHTS - 1
POST_STEPS = [("dve", "sum", 0, 1, 1), ("dve", "stats", 0, 2, 1), ("dve", "gamma", 0, 3, 2),
              ("dve", "beta", 0, 4, 3), ("dve", "add", 0, 5, 4), ("dve", "stats", 1, 6, 5), ("dve", "norm", 0, 7, 6),
              ("pe", "x", 0, 8, 7), ("act", "x", 0, 9, 9), ("pe", "x", 1, 11, 10), ("act", "x", 1, 12, 12),
              ("dve", "low", 0, 13, 13), ("pe", "logits", 0, 15, 13), ("dve", "logits", 0, 16, 15),
              ("act", "exp", 0, 17, 16), ("dve", "exp", 0, 17, 17), ("dve", "top", 0, 19, 18),
              ("dve", "choose", 0, 21, 19), ("dve", "share", 0, 48, 20), ("pe", "place", 0, 23, 20),
              ("dve", "place", 0, 23, 22), ("dve", "gates", 0, 50, 23), ("pe", "gates", 0, 51, 24),
              ("act", "gates", 0, 52, 26), ("dve", "gates", 1, 53, 27), ("pe", "gates", 1, 55, 28),
              ("act", "gates", 1, 56, 30), ("dve", "gates", 2, 56, 31)]
END_STEPS = [("dve", "stats", 0, 1), ("dve", "norm", 0, 3), ("dve", "add", 0, 4), ("dve", "stats", 1, 5),
             ("dve", "norm", 1, 6), ("pe", "x", 0, 7), ("act", "x", 0, 8), ("pe", "x", 1, 11), ("act", "x", 1, 12),
             ("pe", "query", 0, 15), ("act", "query", 0, 16), ("dve", "query", 0, 17),
             ("pe", "query", 1, 19), ("act", "query", 1, 20), ("dve", "query", 1, 21)]
END, POST = "end", "post"


def beside(b, engine=None, tile=None, pair=None):
    steps = [(0, e, t, None, (END, B - 1, what, k)) for e, what, k, t in END_STEPS]
    for n in range(B):
        last = n + 1 == B
        steps += [(n + 1, e, None if last else t, i if last else None, (POST, n, what, k))
                  for e, what, k, t, i in POST_STEPS]
    return [x for n, e, t, i, x in steps if (b is None or n == b) and e == engine
            and (tile is None or t == tile) and (pair is None or i == pair)]


USE = {x: n + 1 for n, x in enumerate(beside(None, "pe"))}


def uses(b, tile):
    return len([0 for n in range(b) for _ in beside(n, "pe")]) + len(
        [0 for n in range(tile) for _ in beside(b, "pe", n)])


class Order:

    def __init__(self, eng, sem):
        self.eng, self.sem, self.base, self.n = eng, sem, 0, 0

    def link(self, ins):
        ins.then_inc(self.sem, 1)
        self.n += 1
        self.eng.wait_ge(self.sem, self.base + self.n)

    @contextmanager
    def loop(self, first, end, per):
        before = self.base + self.n - first * per
        with self.eng.Fori(first, end) as i:
            self.base, self.n = before + i * per, 0
            yield i
            assert self.n == per, f"the body links {self.n} times, not {per}"
        self.base, self.n = before + end * per, 0


class Region:

    def __init__(self, tensor, words):
        self.tensor, self.words, self.at = tensor, words, 0

    def take(self, *shape, dtype=F32):
        n = int(np.prod(shape))
        words = n if dtype == F32 else (n + 1) // 2
        assert self.at + words <= self.words, (self.at + words, self.words)
        piece = self.tensor[:, self.at:self.at + words]
        self.at += words
        if dtype != F32:
            piece = piece.bitcast(dtype)[:, 0:n]
        if len(shape) == 2:
            piece = piece.rearrange("p (a b) -> p a b", a=shape[0])
        if len(shape) == 3:
            piece = piece.rearrange("p (a b c) -> p a b c", a=shape[0], b=shape[1])
        return piece


def tower(nc, d, out):
    ctx = ExitStack()
    with ctx:
        def sb(name, shape, dt=F32):
            return ctx.enter_context(nc.sbuf_tensor(name, shape, dt))

        def sem(name):
            return ctx.enter_context(nc.semaphore(name))

        ps = ctx.enter_context(nc.psum_tensor("ps", [128, 8, 512], F32))

        h = sb("h", [P, B * R, C])
        xres = sb("xres", [P, B * R, C])
        gates = sb("gates", [128, B * T], F16)

        ident = sb("ident", [128, 128])
        ones = sb("ones", [128, 128])
        ones16 = sb("ones16", [128, 128], F16)
        causal = sb("causal", [P, P])
        before = sb("before", [P, P], F16)
        bc_sb = sb("bc_sb", [128, MC])
        tokb = sb("tokb", [128, 1])
        w2_sb = sb("w2_sb", [128, MC, C])
        rows = sb("rows", [P, 6, C])
        rw_sb = sb("rw_sb", [128, E])
        rb_sb = sb("rb_sb", [1, E])
        g0 = sb("g0", [128, 128])
        m0 = sb("m0", [128, 128])
        g1 = sb("g1", [128, 128])
        m1 = sb("m1", [128, 128])
        zrow = sb("zrow", [1, 512], F16)
        carry = sb("carry", [P, E])
        stats = sb("stats", [P, R, 6])
        mv = sb("mv", [P, R, 2])
        rstd = sb("rstd", [P, R])
        vare = sb("vare", [P, R])
        power = sb("power", [P, R])
        eps = sb("eps", [P, R])
        idle = sb("idle", [P, 1])
        mx2 = sb("mx2", [P, 2])
        nm = sb("nm", [P, R])
        sums = sb("sums", [P, R, 2])
        den = sb("den", [P, R])
        rden = sb("rden", [P, R])

        KSET = 14720
        region_k = Region(sb("region_k", [128, 2 * KSET]), 2 * KSET)
        wc = [[region_k.take(MC, n, 128, dtype=F16) for _ in range(2)] for n in (EV, OD, EV)]
        ys = [[[region_k.take(XP, dtype=F16) for _ in range(2)] for _ in range(3)] for _ in range(2)]
        zz_at = region_k.at
        zz = region_k.take(MC, T)
        k_hi, k_lo, v_hi, v_lo = [], [], [], []
        for n in range(2):
            region_k.at = n * KSET
            k_hi.append(region_k.take(KEYS, dtype=F16))
            k_lo.append(region_k.take(KEYS, dtype=F16))
            v_hi.append(region_k.take(TILES, C + 1, dtype=F16))
            v_lo.append(region_k.take(TILES, C + 1, dtype=F16))
        region_k.at = 0
        wg_hi, wg_lo, wu_hi, wu_lo, wd_hi, wd_lo = (region_k.take(NSEQ * 128, dtype=F16) for _ in range(6))
        sel_sb = region_k.take(PAIRS * 128, dtype=F16)
        assert region_k.at <= KSET

        region_b = Region(sb("region_b", [128, B * T]), B * T)
        q_hi = region_b.take(B, T, dtype=F16)
        q_lo = region_b.take(B, T, dtype=F16)
        x_hi = q_hi.rearrange("p b t -> p (b t)")
        x_lo = q_lo.rearrange("p b t -> p (b t)")

        gates32 = gates[:, :].bitcast(F32)
        taps = [gates32[0:WT, n * 496:(n + 1) * 496].rearrange("p (a k) -> p a k", k=TAPS) for n in range(2)]
        band = [gates32[0:WT, n * 496:(n + 1) * 496] for n in range(2)]
        xsum = gates32[:, 992:992 + XP]

        region_c = Region(sb("region_c", [128, 8060]), 8060)
        wq_sb = region_c.take(128)[0:64]
        wk_sb = region_c.take(128)[0:64]
        wv_sb = region_c.take(128)[0:64]
        wo_sb = region_c.take(128)[0:64]
        w1_sb = region_c.take(128)
        fc_sb = region_c.take(128)
        region_c.at = 0
        xn = region_c.take(R, C)[0:P]
        yT = region_c.take(T)
        qg = region_c.take(T)
        v0 = region_c.take(R, C)[0:P]
        pr = region_c.take(T)[0:P]
        prT = region_c.take(T)[0:P]
        at_c = region_c.at
        region_c.at = 0
        wc_f = [region_c.take(WPIECE) for _ in range(2)]
        region_c.at = 0
        p_hi = [region_c.take(T, dtype=F16) for _ in range(2)]
        p_lo = [region_c.take(T, dtype=F16) for _ in range(2)]
        region_c.at = at_c
        even_sb = region_c.take(HALF + 1)
        z_even = region_c.take(HALF)
        z_odd = region_c.take(HALF)
        zn = region_c.take(HALF)
        bandT = [gates32[0:WIN, 992:992 + HEADS * WT]]
        wq_sb = region_c.take(128)[0:64]
        wk_sb = region_c.take(128)[0:64]
        wv_sb = region_c.take(128)[0:64]
        wo_sb = region_c.take(128)[0:64]
        w1_sb = region_c.take(128)
        fc_sb = region_c.take(128)
        keys_at = region_c.at - 6 * 128
        ytmp = region_c.take(TP)
        xt = ytmp
        mask = region_c.take(2, TAPS)[0:WT]
        wmx = region_c.take(GW * HEADS)[0:WT]
        wsum = region_c.take(GW * HEADS)[0:WT]
        wrs = region_c.take(GW * HEADS)[0:WT]
        wl_sb = region_c.take(HEADS * TAPS)
        bl_sb = region_c.take(HEADS * TAPS)[0:WT]
        xw = [region_c.take(C)[0:WIN] for _ in range(2)]
        region_k.at = zz_at
        bandT.append(region_k.take(HEADS * WT)[0:WIN])
        band += [region_k.take(496)[0:WT] for _ in range(NBAND - 2)]
        xw += [region_k.take(C)[0:WIN] for _ in range(NBAND - 2)]
        assert region_k.at <= zz_at + MC * T
        region_c.at = keys_at
        kf = [region_c.take(CH) for _ in range(2)]
        vf = [region_c.take(CH) for _ in range(2)]
        kf_tail = region_c.take(TAIL)
        vf_tail = region_c.take(TAIL)
        region_c.at = keys_at
        wf = [region_c.take(NSEQ * 128 // NWP) for _ in range(2)]
        region_c.at = 2 * T
        xnT = region_c.take(T)
        probs = region_c.take(R, E + 2)[0:P]
        rep = region_c.take(R, E + 2)[0:P]
        slot = rep
        top8 = region_c.take(R, 8)[0:P]
        top6 = region_c.take(R, 8)[0:P]
        msk = region_c.take(R, E, dtype=F16)[0:P]
        gate2 = region_c.take(R, 2 * E)[0:P]
        g_tmp = region_c.take(T, dtype=F16)
        router_end = region_c.at
        shift = [region_c.take(R, P, dtype=F16)[0:P] for _ in range(2)]
        mxk = region_c.take(R, CHUNKS)[0:P]
        assert region_c.at <= keys_at
        region_c.at = 0
        ac = [region_c.take(MT) for _ in range(2)]
        out_cm = region_c.take(MT)
        assert region_c.at <= 2 * T
        region_c.at = router_end
        sg = [region_c.take(MT) for _ in range(2)]
        su = [region_c.take(MT) for _ in range(2)]
        a_hi = [region_c.take(MT, dtype=F16) for _ in range(2)]
        a_lo = [region_c.take(MT, dtype=F16) for _ in range(2)]
        fin = region_c.take(MT // P, C)[0:P]

        band_dram = nc.dram_tensor("band_dram", [WT, NW, HEADS * WIN], F32).ap()

        names = """mix_in const_in ones_ready su_ready dve_own pool_own wprod_ps wprod_sb zero_ready zero_out
            x_in shifted exp_done w_ready band_written ysum_ready y_hi_done y_ready
            shared_full act_read dve_read wc_hi_ready wc_lo_ready wc_sum wc_sum_hi wc_ready
            prod_full prod_free zneg_ready zexp_done z_ready
            s_full s_free t_full t_free nmax_ready xn_ready var_ready rstd_ready q_hi_done q_done
            post_full post_free klo_ready vps_ready vh_ready vl_ready mx_ps mx_free shift_ready
            st_ps p_hi_ready exp_sum lo_ready pv_done acc_ps acc_free wf_done
            shifted_logits logits_exp msk_ready gates_ready gates_hi
            gate_ps up_ps up_free silu_done a_ready a_hi_ready a_lo_ready down_done
            out_cm_ready out_ps fin_ready fin_out
            stage""".split()
        s = {n: sem(n) for n in names}
        s_wc = [sem(f"wc_in{u}") for u in range(2)]
        s_band = [sem(f"band_in{u}") for u in range(NBAND)]
        s_kf = [sem(f"kf_in{u}") for u in range(2)]
        s_vf = [sem(f"vf_in{u}") for u in range(2)]
        s_wf = [sem(f"wf_in{u}") for u in range(2)]
        s_tail = sem("tail_in")

        def bank(n, parts=128):
            return ps[0:parts, n]

        def two(n, parts=128):
            return ps[0:parts, n:n + 2, 0:HALF]

        def halves(ap):
            return ap.rearrange("p (a b) -> p a b", a=2)

        def stage_end(eng, n):
            eng.drain()
            eng.sem_inc(s["stage"], 1)
            eng.wait_ge(s["stage"], 5 * n)

        row = HEADS * WIN

        def band_taps(i):
            return bass.AP(tensor=band_dram.tensor, offset=i * row,
                           ap=[[NW * row + 1, WT], [WIN, GW * HEADS], [1, TAPS]])

        def taps_of(n):
            odd = 8 - n % 2
            piece = wc_f[n % 2][:, 0:(8 + odd) * 128].rearrange("p (t c) -> p t c", c=128)
            return piece[:, 0:8], piece[:, 8:8 + odd]

        def attn_banks(b):
            return 4 if b + 1 < B else 0

        def band_buffer(b, j):
            if b == 0:
                return j % NBAND, j // NBAND + 1
            return j % 2, (NW - 1 - j % 2) // NBAND + 1 + NW // 2 * (b - 1) + j // 2 + 1

        def post_bank(b):
            return 5 if b + 1 < B else 7

        def shared(b, what, k, kind=MIX):
            return SHARED[kind, b, what, k][:2]

        mix_loads = [(wl_sb, "WlT"), (mask, "mask"), (ident, "ident"), (tokb, "tok_bias")]
        const_loads = [
            (wq_sb, "WqT"), (wk_sb, "WkT"), (wv_sb, "WvT"), (wo_sb, "Wo"),
            (w1_sb, "W1"), (fc_sb, "fcT"), (bc_sb, "bc"), (w2_sb, "W2T"), (causal, "causal"),
            (before, "before"), (rw_sb, "rwT"), (rb_sb, "rb"),
        ]
        row_loads = ["b2", "bo", "fcb", "gamma", "beta"]
        MIX_IN = 16 * (len(mix_loads) + 1)
        CONST_IN = 16 * (len(const_loads) + len(row_loads))

        block = ctx.enter_context(nc.Block())

        @block.sync
        def _(sp):
            sp.dma_start(xt, d["xT"][0]).then_inc(s["x_in"], 16)
            for dst, name in mix_loads:
                sp.dma_start(dst[:], d[name]).then_inc(s["mix_in"], 16)
            sp.dma_start(bl_sb, d["bl"].partition_broadcast(WT)).then_inc(s["mix_in"], 16)
            for dst, name in const_loads:
                sp.dma_start(dst[:], d[name]).then_inc(s["const_in"], 16)
            for n, name in enumerate(row_loads):
                sp.dma_start(rows[:, n, :], d[name].partition_broadcast(P)).then_inc(s["const_in"], 16)
            for b in range(B):
                if b:
                    sp.wait_ge(s["y_ready"], 3 * b)
                    sp.dma_start(xt, d["xT"][b]).then_inc(s["x_in"], 16)
                for j in range(NW):
                    if j == 0:
                        sp.wait_ge(s["band_written"], 32 * (b + 1))
                    depth = 2 if b else NBAND
                    if j >= depth:
                        sp.wait_ge(s["shared_full"], shared(b, "apply", j - depth)[0])
                    u, _ = band_buffer(b, j)
                    sp.dma_start(band[u], band_dram[:, j]).then_inc(s_band[u], 16)
                    sp.dma_start(xw[u], d["xw"][NW * b + j]).then_inc(s_band[u], 16)
            sp.wait_ge(s["y_ready"], 3 * B)
            for b in range(B):
                if b >= 1:
                    sp.wait_ge(s["klo_ready"], 2 + CHUNKS * (b - 1) + 1)
                    sp.wait_ge(s["vps_ready"], 2 + CHUNKS * (b - 1) + 1)
                sp.dma_start(kf_tail, d["k"][b, :, KT * KW:]).then_inc(s_tail, 16)
                sp.dma_start(vf_tail, d["v"][b, :, KT * KW:]).then_inc(s_tail, 16)
                with sp.Fori(0, NCH // 2) as c2:
                    for u in range(2):
                        c = 2 * c2 + u
                        at = bass.ds(sp.snap(c2 * (2 * CH) + u * CH), CH)
                        sp.wait_ge(s["klo_ready"], 2 + CHUNKS * b + c)
                        sp.dma_start(kf[u], d["k"][b, :, at]).then_inc(s_kf[u], 16)
                        sp.wait_ge(s["vps_ready"], 2 + CHUNKS * b + c)
                        sp.dma_start(vf[u], d["v"][b, :, at]).then_inc(s_vf[u], 16)
            sp.wait_ge(s["klo_ready"], 2 + CHUNKS * B)
            sp.wait_ge(s["vps_ready"], 2 + CHUNKS * B)
            sp.wait_ge(s["acc_ps"], B - 1)
            sp.dma_start(sel_sb, d["sel"]).then_inc(s["const_in"], 16)
            for n in range(3 * NWP):
                if n >= 2:
                    sp.wait_ge(s["wf_done"], n - 1)
                sp.dma_start(wf[n % 2], d["experts"][n]).then_inc(s_wf[n % 2], 16)
            stage_end(sp, 1)
            out_t = out.rearrange("b (r p) c -> p (b r) c", p=P)
            with sp.Fori(0, NMC) as c:
                sp.wait_ge(s["fin_ready"], c + 1)
                sp.dma_start(out_t[:, bass.ds(c * (MT // P), MT // P), :], fin).then_inc(s["fin_out"], 16)
            sp.wait_ge(s["fin_out"], 16 * (NMC + 1))

        @block.gpsimd
        def _(pool):
            g = nc.gpsimd
            for name, n in (("klo_ready", 2), ("vps_ready", 2), ("vl_ready", 1), ("mx_free", 1),
                            ("up_free", 2), ("down_done", 2), ("fin_out", 16)):
                if n:
                    pool.sem_inc(s[name], n)
            g.memset(xsum, 0.0).then_inc(s["zero_ready"], 1)
            g.memset(power[:], -0.5)
            g.memset(eps[:], EPS)
            g.memset(carry[:], 0.0)
            g.memset(ones16[:], 1.0)
            g.memset(zrow[:], 0.0)
            g.memset(ones[:], 1.0).then_inc(s["ones_ready"], 1)
            pool.wait_ge(s["zero_out"], 32)
            for n in range(2):
                pool.dma_start(wc_f[n][:, 0:(2048, 1920)[n % 2]], d["WcT"][n][:, 0:(2048, 1920)[n % 2]]
                               ).then_inc(s_wc[n % 2], 16)
            own = Order(pool, s["pool_own"])

            for n in range(2 * MC):
                m, half = divmod(n, 2)
                e, o = taps_of(n)
                pool.wait_ge(s["wc_lo_ready"], n + 1)
                own.link(g.tensor_tensor(e[:, 0:o.shape[1]], e[:, 0:o.shape[1]], o, ALU.add))
                own.link(g.tensor_scalar(e, e, W_SCALE, None, ALU.mult))
                pool.sem_inc(s["wc_sum"], 1)
                pool.wait_ge(s["wc_sum_hi"], n + 1)
                at = slice(8 * half, 8 * half + 8)
                g.tensor_tensor(wc[2][1][:, m, at], e, wc[2][0][:, m, at], ALU.subtract
                                ).then_inc(s["wc_ready"], 1)
                if n + 2 < 2 * MC:
                    pool.wait_ge(s["wc_ready"], n + 1)
                    w = (2048, 1920)[n % 2]
                    pool.dma_start(wc_f[n % 2][:, 0:w], d["WcT"][n + 2][:, 0:w]).then_inc(s_wc[n % 2], 16)

            def power_of_variance(n):
                pool.wait_ge(s["var_ready"], n)
                own.link(g.tensor_tensor(vare[:], mv[:, :, 1], eps[:], ALU.add))
                g.tensor_tensor(rstd[:], vare[:], power[:], ALU.pow).then_inc(s["rstd_ready"], 1)

            def ones_columns(n):
                g.memset(v_hi[n][:, :, C:C + 1], 1.0)
                g.memset(v_lo[n][:, :, C:C + 1], 0.0)

            for n in range(3 * (B - 1)):
                power_of_variance(n + 1)
            pool.wait_ge(s["prod_full"], 3 * MC * B - 2)
            for b in range(B):
                kh, kl = k_hi[b % 2], k_lo[b % 2]
                if b == 1:
                    ones_columns(b)
                if b >= 2:
                    pool.wait_ge(s["acc_ps"], b - 1)
                pool.wait_ge(s_tail, 32 * (b + 1))
                own.link(g.tensor_copy(kh[:, KT * KW:], kf_tail))
                g.tensor_tensor(kl[:, KT * KW:], kf_tail, kh[:, KT * KW:], ALU.subtract
                                ).then_inc(s["klo_ready"], 1)

                def split(c2, u):
                    at = bass.ds(c2 * (2 * CH) + u * CH, CH)
                    pool.wait_ge(s_kf[u], 16 * ((NCH // 2) * b + c2 + 1))
                    pool.wait_ge(s["ones_ready"], 1)
                    own.link(g.tensor_copy(kh[:, at], kf[u]))
                    g.tensor_tensor(kl[:, at], kf[u], kh[:, at], ALU.subtract).then_inc(s["klo_ready"], 1)

                if b == 0:
                    for c in range(NCH):
                        split(c // 2, c % 2)
                        if c == 1:
                            power_of_variance(3 * (B - 1) + 1)
                            pool.wait_ge(s["prod_full"], 3 * MC * B)
                            ones_columns(0)
                else:
                    for c in range(4):
                        split(c // 2, c % 2)
                        if c % 2 == 0:
                            first = 3 * (B - 1) + 1 if b == 1 else 3 * B + 2 * (b - 2)
                            power_of_variance(first + c // 2 + 1)
                    with own.loop(2, NCH // 2, 2) as c2:
                        for u in range(2):
                            split(c2, u)
            for n in range(2):
                power_of_variance(3 * B + 2 * (B - 2) + n + 1)
            pool.wait_ge(s["acc_ps"], B - 1)
            for n in range(3 * NWP):
                part = slice((n % NWP) * (NSEQ * 128 // NWP), (n % NWP + 1) * (NSEQ * 128 // NWP))
                hi, lo = ((wg_hi, wg_lo), (wu_hi, wu_lo), (wd_hi, wd_lo))[n // NWP]
                pool.wait_ge(s_wf[n % 2], 16 * (n // 2 + 1))
                own.link(g.tensor_scalar(wf[n % 2], wf[n % 2], X_SCALE, None, ALU.mult))
                own.link(g.tensor_copy(hi[:, part], wf[n % 2]))
                g.tensor_tensor(lo[:, part], wf[n % 2], hi[:, part], ALU.subtract).then_inc(s["wf_done"], 1)
            stage_end(pool, 1)
            def low_part(n, u):
                pool.wait_ge(s["a_hi_ready"], n + 1)
                g.tensor_tensor(a_lo[u], ac[u], a_hi[u], ALU.subtract).then_inc(s["a_lo_ready"], 1)

            for n in range(NSEQ):
                low_part(n, n % 2)
                for k in range(2):
                    if (POST, B - 1, "stats", k) in beside(B, "dve", pair=n):
                        power_of_variance(3 * B + 2 * (B - 1) + k + 1)
            with pool.Fori(1, NMC) as c:
                low_part(NSEQ * c, 0)
                with pool.Fori(0, PAIRS // 2) as i:
                    low_part(NSEQ * c + 2 * i + 1, 1)
                    low_part(NSEQ * c + 2 * i + 2, 0)

        @block.scalar
        def _(act):
            a = nc.scalar

            act.wait_ge(s["zero_ready"], 1)
            act.wait_ge(s["mix_in"], MIX_IN)
            for n in range(2):
                act.dma_start(band_dram.rearrange("p i (a n) -> p i a n", a=2)[:, :, n],
                              xsum[0:WT, 0:HEADS * WIN // 2].unsqueeze(1).broadcast_to((WT, NW, HEADS * WIN // 2))
                              ).then_inc(s["zero_out"], 16)

            def mix(b, what, k):
                if what == "logits":
                    act.wait_ge(s["shifted"], 2 * b + k + 1)
                    a.activation(taps[k], taps[k], ACT.Exp).then_inc(s["exp_done"], 1)
                elif what == "taps":
                    act.wait_ge(s["zero_out"], 32)
                    act.wait_ge(s["w_ready"], 2 * b + k + 1)
                    act.dma_start(band_taps(GW * k), taps[k]).then_inc(s["band_written"], 16)
                elif what == "band":
                    turn, bk = shared(b, what, k)
                    act.wait_ge(s["shared_full"], turn)
                    a.activation(bandT[k % 2 * (b == 0)], bank(bk, WIN)[:, 0:HEADS * WT], ACT.Copy
                                 ).then_inc(s["act_read"], 1)
                elif what == "split":
                    act.wait_ge(s["ysum_ready"], b + 1)
                    y = ytmp.rearrange("p (n two) -> p n two", two=2)
                    for n, src in enumerate((y[:, :, 0], y[:, :, 1], xsum)):
                        a.activation(ys[b % 2][n][0], src, ACT.Copy).then_inc(s["y_hi_done"], 1)

                elif what == "high":
                    e, o = taps_of(k)
                    at = 8 * (k % 2)
                    act.wait_ge(s_wc[k % 2], 16 * (k // 2 + 1))
                    a.activation(wc[0][0][:, k // 2, at:at + 8], e, ACT.Copy, scale=W_SCALE)
                    a.activation(wc[1][0][:, k // 2, at:at + o.shape[1]], o, ACT.Copy, scale=W_SCALE
                                 ).then_inc(s["wc_hi_ready"], 1)
                elif what == "sums":
                    act.wait_ge(s["wc_sum"], k + 1)
                    a.activation(wc[2][0][:, k // 2, 8 * (k % 2):8 * (k % 2) + 8], taps_of(k)[0], ACT.Copy
                                 ).then_inc(s["wc_sum_hi"], 1)

            def attn(b, what, k):
                bk = attn_banks(b)
                if (what, k) in PAIR_S and what != "value":
                    if what == "score":
                        act.wait_ge(s["nmax_ready"], R * b + k + 1)
                        n1 = min(k + 1, 3) * P
                        last = a.activation(pr[:, 0:n1], bank(bk, P)[:, 0:n1], ACT.Exp, bias=nm[:, k:k + 1],
                                            accum_out=sums[:, k, 0:1])
                        if k >= 3:
                            last = a.activation(pr[:, HALF:(k + 1) * P], bank(bk + 1, P)[:, 0:(k - 2) * P],
                                                ACT.Exp, bias=nm[:, k:k + 1], accum_out=sums[:, k, 1:2])
                    else:
                        act.wait_ge(s["s_full"], NS * b + PAIR_S[what, k])
                        last = a.activation(halves(yT), two(bk), ACT.Copy)
                    last.then_inc(s["s_free"], 1)
                elif (what, k) == ("query", 0):
                    act.wait_ge(s["t_full"], NT * b + PAIR_T[what, k])
                    a.activation(halves(qg), two(bk + 2), ACT.Copy).then_inc(s["t_free"], 1)
                elif (what, k) == ("query", 1):
                    act.wait_ge(s["t_full"], NT * b + PAIR_T[what, k])
                    a.activation(halves(q_hi[:, b, :]), two(bk + 2), ACT.Copy).then_inc(s["q_hi_done"], 1)
                elif what == "turn":
                    act.wait_ge(s["t_full"], NT * b + PAIR_T[what, k])
                    last = a.activation(prT[:, 0:min(k + 1, 3) * P], bank(bk + 2, P)[:, 0:min(k + 1, 3) * P], ACT.Copy)
                    if k >= 3:
                        last = a.activation(prT[:, HALF:(k + 1) * P], bank(bk + 3, P)[:, 0:(k - 2) * P], ACT.Copy)
                    last.then_inc(s["t_free"], 1)

            def product_done(b, m, p):
                if p:
                    act.wait_ge(s["zneg_ready"], 2 * (MC * b + m) + p)
                    a.activation(zn, zn, ACT.Exp).then_inc(s["zexp_done"], 1)

            for what, k in MIX_ALONE:
                mix(0, what, k)
            act.wait_ge(s["wprod_ps"], 1)
            for n, (dst, scale) in enumerate(((g0, 64 ** -0.5), (m0, 1.0), (g1, C ** -0.5), (m1, 1.0))):
                last = a.activation(dst[:], bank(6)[:, 128 * n:128 * (n + 1)], ACT.Copy, scale=scale)
            last.then_inc(s["wprod_sb"], 1)
            for b in range(B):
                for m, p, quarter, steps in layer_order(b):
                    if quarter == 3:
                        product_done(b, m, p)
                    for kind, at, what, k in steps:
                        if kind == MIX:
                            mix(at, what, k)
                        if kind == ATTN:
                            attn(at, what, k)

            def exponentials(b, t, u, parts=KW):
                act.wait_ge(s["st_ps"], TILES * b + t + 1)
                if not isinstance(t, int) or t > 1:
                    act.wait_ge(s["pv_done"], TILES * b + t - 1)
                elif b:
                    act.wait_ge(s["pv_done"], TILES * b)
                st = two(2 * u, parts)
                a.activation(halves(p_hi[u][0:parts]), st, ACT.Exp).then_inc(s["p_hi_ready"], 1)
                a.activation(st, st, ACT.Exp).then_inc(s["exp_sum"], 1)

            def values_high(b, c, parts=KW):
                n = CHUNKS * b + 1 + c
                act.wait_ge(s["vps_ready"], 2 + n + 1)
                if isinstance(c, int) and c < 0:
                    a.activation(v_hi[b % 2][0:TAIL, KT, 0:C], bank(5, TAIL)[:, 0:C], ACT.Copy
                                 ).then_inc(s["vh_ready"], 1)
                else:
                    act.wait_ge(s["ones_ready"], 1)
                    a.activation(v_hi[b % 2][:, bass.ds(c * 4, 4), 0:C],
                                 bank(5).rearrange("p (t c) -> p t c", c=C), ACT.Copy).then_inc(s["vh_ready"], 1)

            def step(kind, b, what, k):
                (end if kind == END else post)(b, what, k)

            def end(b, what, k):
                half = slice(k * HALF, (k + 1) * HALF)
                act.wait_ge(s["post_full"], USE[END, b, what, k])
                if what == "x":
                    a.activation(xnT[:, half], bank(5)[:, 0:HALF], ACT.Copy).then_inc(s["post_free"], 1)
                else:
                    a.activation(q_hi[:, b, half], bank(5)[:, 0:HALF], ACT.Copy).then_inc(s["q_hi_done"], 1)

            def post(b, what, k):
                bk = post_bank(b)
                half = slice(k * HALF, (k + 1) * HALF)
                if what == "x":
                    act.wait_ge(s["post_full"], USE[POST, b, what, k])
                    a.activation(xnT[:, half], bank(bk)[:, 0:HALF], ACT.Copy)
                    a.activation(q_hi[:, b, half], bank(bk)[:, 0:HALF], ACT.Copy).then_inc(s["post_free"], 1)
                elif what == "exp":
                    act.wait_ge(s["shifted_logits"], b + 1)
                    a.activation(probs[:, :, 0:E], probs[:, :, 0:E], ACT.Exp).then_inc(s["logits_exp"], 1)
                elif what == "gates":
                    act.wait_ge(s["post_full"], USE[POST, b, what, k])
                    a.activation(gates[0:E, b * T + k * HALF:b * T + (k + 1) * HALF], bank(bk, E)[:, 0:HALF], ACT.Copy)
                    a.activation(g_tmp[E:128, half], ps[E:128, bk, 0:HALF], ACT.Copy).then_inc(s["gates_hi"], 1)

            values_high(0, -1)
            for c in range(NCH):
                for what, k in LAST_ATTN_STEPS[2 * c:2 * c + 2]:
                    attn(B - 1, what, k)
                values_high(0, c)
            for b in range(B):
                exponentials(b, 0, 0)
                if b + 1 < B:
                    values_high(b + 1, -1)
                exponentials(b, 1, 1)

                def eight(i, ts=range(8)):
                    for t in ts:
                        exponentials(b, 8 * i + t, t % 2)
                        if t % 4 == 2 and b + 1 < B:
                            values_high(b + 1, 2 * i + t // 4)
                        if isinstance(i, int):
                            for x in beside(b, "act", 8 * i + t):
                                step(*x)

                eight(0, range(2, 8))
                for i in range(1, FIRST):
                    eight(i)
                with act.Fori(FIRST, LAST) as i:
                    eight(i)
                eight(LAST)
                exponentials(b, KT, 0, TAIL)
                for x in beside(b, "act", KT):
                    step(*x)
            stage_end(act, 1)

            def silu(n, u):
                act.wait_ge(s["gate_ps"], n + 1)
                act.wait_ge(s["up_free"], n + 1)
                a.activation(sg[u], bank(3 * u)[:, 0:MT], ACT.Silu, scale=1 / X_SCALE).then_inc(s["silu_done"], 1)

            def high_part(n, u):
                act.wait_ge(s["a_ready"], n + 1)
                act.wait_ge(s["down_done"], n + 1)
                a.activation(a_hi[u], ac[u], ACT.Copy).then_inc(s["a_hi_ready"], 1)

            def chunk_done(c):
                act.wait_ge(s["down_done"], 2 + NSEQ * (c + 1))
                a.activation(out_cm, bank(6)[:, 0:MT], ACT.Copy, scale=1 / (A_SCALE * X_SCALE)
                             ).then_inc(s["out_cm_ready"], 1)

            silu(0, 0)
            for n in range(NSEQ):
                if n + 1 < NSEQ:
                    silu(n + 1, (n + 1) % 2)
                high_part(n, n % 2)
                for x in beside(B, "act", pair=n):
                    step(*x)
            chunk_done(0)
            with act.Fori(1, NMC) as c:
                n0 = NSEQ * c
                silu(n0, 0)
                with act.Fori(0, PAIRS // 2) as i:
                    silu(n0 + 2 * i + 1, 1)
                    high_part(n0 + 2 * i, 0)
                    silu(n0 + 2 * i + 2, 0)
                    high_part(n0 + 2 * i + 1, 1)
                high_part(n0 + PAIRS, 0)
                chunk_done(c)

        @block.vector
        def _(dve):
            v = nc.vector
            own = Order(dve, s["dve_own"])

            dve.wait_ge(s["mix_in"], MIX_IN)

            def mix(b, what, k):
                if what == "logits":
                    turn, bk = shared(b, what, k)
                    dve.wait_ge(s["shared_full"], turn)
                    n = GW * HEADS * TAPS
                    own.link(v.tensor_tensor(taps[k].rearrange("p (j h) k -> p j (h k)", j=GW),
                                             bank(bk, WT)[:, 0:n].rearrange("p (j n) -> p j n", j=GW),
                                             bl_sb.unsqueeze(1).broadcast_to((WT, GW, HEADS * TAPS)), ALU.add))
                    dve.sem_inc(s["dve_read"], 1)
                    edge = taps[k][:, 0:HEADS] if k == 0 else taps[k][:, (GW - 1) * HEADS:]
                    own.link(v.tensor_tensor(edge, edge, mask[:, k:k + 1, :].broadcast_to((WT, HEADS, TAPS)),
                                             ALU.add))
                    own.link(v.tensor_reduce(wmx, taps[k], AX, ALU.max))
                    v.tensor_tensor(taps[k], taps[k], wmx.unsqueeze(2).broadcast_to((WT, GW * HEADS, TAPS)),
                                    ALU.subtract).then_inc(s["shifted"], 1)
                    dve.wait_ge(s["shifted"], 2 * b + k + 1)
                elif what == "taps":
                    dve.wait_ge(s["exp_done"], 2 * b + k + 1)
                    own.link(v.tensor_reduce(wsum, taps[k], AX, ALU.add))
                    own.link(v.reciprocal(wrs, wsum))
                    v.tensor_tensor(taps[k], taps[k], wrs.unsqueeze(2).broadcast_to((WT, GW * HEADS, TAPS)),
                                    ALU.mult).then_inc(s["w_ready"], 1)
                elif what == "apply":
                    turn, bk = shared(b, what, k)
                    dve.wait_ge(s["shared_full"], turn)
                    for g in range(HEADS):
                        lo, hi = g * 32, (g + 1) * 32
                        last = v.tensor_scalar(ytmp[lo:hi, k * WT:(k + 1) * WT], ps[lo:hi, bk, g * WT:(g + 1) * WT],
                                               tokb[lo:hi, :], None, ALU.add)
                    own.link(last)
                    dve.sem_inc(s["dve_read"], 1)
                elif what == "split":
                    own.link(v.memset(ytmp[:, T_IN:TP], 0.0))
                    y = ytmp.rearrange("p (n two) -> p n two", two=2)
                    own.link(v.tensor_tensor(xsum[:, 0:XP - 1], y[:, 0:XP - 1, 1], y[:, 1:XP, 0], ALU.add))
                    own.link(v.tensor_copy(xsum[:, XP - 1:XP], y[:, XP - 1:XP, 1]))
                    dve.sem_inc(s["ysum_ready"], 1)
                    for n, src in enumerate((y[:, :, 0], y[:, :, 1], xsum)):
                        dve.wait_ge(s["y_hi_done"], 3 * b + n + 1)
                        v.tensor_tensor(ys[b % 2][n][1], src, ys[b % 2][n][0], ALU.subtract
                                        ).then_inc(s["y_ready"], 1)
                elif what == "low":
                    dve.wait_ge(s["wc_hi_ready"], k + 1)
                    for p, src in enumerate(taps_of(k)):
                        at = slice(8 * (k % 2), 8 * (k % 2) + src.shape[1])
                        last = v.scalar_tensor_tensor(
                            out=wc[p][1][:, k // 2, at].rearrange("p t c -> p (t c)"),
                            in0=src.rearrange("p t c -> p (t c)"), scalar=W_SCALE,
                            in1=wc[p][0][:, k // 2, at].rearrange("p t c -> p (t c)"),
                            op0=ALU.mult, op1=ALU.subtract)
                    last.then_inc(s["wc_lo_ready"], 1)

            def selu(b, m, odd, z):
                n = 2 * (MC * b + m) + odd
                bias = bc_sb[:, m:m + 1]
                v.tensor_scalar(zn, z, bias, 0.0, ALU.add, ALU.min).then_inc(s["zneg_ready"], 1)
                own.link(v.tensor_scalar(z, z, bias, 0.0, ALU.add, ALU.max))
                dve.wait_ge(s["zexp_done"], n + 1)
                own.link(v.tensor_scalar(zn, zn, -1.0, SELU_SCALE * SELU_ALPHA, ALU.add, ALU.mult))
                v.scalar_tensor_tensor(out=zz[:, m, :].rearrange("p (n two) -> p n two", two=2)[:, :, odd], in0=z,
                                       scalar=SELU_SCALE, in1=zn, op0=ALU.mult, op1=ALU.add
                                       ).then_inc(s["z_ready"], 1)
                dve.wait_ge(s["z_ready"], n + 1)

            def product_done(b, m, p):
                dve.wait_ge(s["prod_full"], 3 * (MC * b + m) + p + 1)
                if p == 0:
                    own.link(v.tensor_scalar(even_sb, bank(0)[:, 0:HALF + 1], 1 / W_SCALE, None, ALU.mult))
                    dve.sem_inc(s["prod_free"], 1)
                elif p == 1:
                    v.scalar_tensor_tensor(out=z_even, in0=bank(1)[:, 0:HALF], scalar=1 / W_SCALE,
                                           in1=even_sb[:, 0:HALF], op0=ALU.mult, op1=ALU.add)
                    own.link(v.scalar_tensor_tensor(out=z_odd, in0=bank(1)[:, 0:HALF], scalar=-1 / W_SCALE,
                                                    in1=even_sb[:, 1:HALF + 1], op0=ALU.mult, op1=ALU.subtract))
                    dve.sem_inc(s["prod_free"], 1)
                    selu(b, m, 0, z_even)
                else:
                    own.link(v.scalar_tensor_tensor(out=z_odd, in0=bank(2)[:, 0:HALF], scalar=1 / W_SCALE,
                                                    in1=z_odd, op0=ALU.mult, op1=ALU.add))
                    dve.sem_inc(s["prod_free"], 1)
                    selu(b, m, 1, z_odd)

            def down(b, k):
                turn, bk = shared(b, "h", k, DOWN)
                dve.wait_ge(s["shared_full"], turn)
                own.link(v.tensor_tensor(h[:, b * R + 3 * k:b * R + 3 * k + 3, :],
                                         bank(bk, P)[:, 0:3 * C].rearrange("p (r c) -> p r c", c=C),
                                         rows[:, 0:1, :].broadcast_to((P, 3, C)), ALU.add))
                dve.sem_inc(s["dve_read"], 1)

            def statistics(src, n):
                for r in range(R):
                    last = v.bn_stats(stats[:, r, :], src[:, r, :])
                own.link(last)
                v.memset(idle[:], 0.0)
                for r in range(R):
                    last = v.bn_aggr(mv[:, r, :], stats[:, r, :])
                last.then_inc(s["var_ready"], 1)
                dve.wait_ge(s["var_ready"], n)

            def normalise(dst, src, n):
                dve.wait_ge(s["rstd_ready"], n)
                for r in range(R):
                    last = v.tensor_scalar(dst[:, r, :], src[:, r, :], mv[:, r, 0:1], rstd[:, r:r + 1],
                                           ALU.subtract, ALU.mult)
                own.link(last)

            def layer_norm(dst, src, n):
                statistics(src, n)
                normalise(dst, src, n)

            def attn(b, what, k):
                bk = attn_banks(b)
                x = h[:, b * R:(b + 1) * R, :]
                if (what, k) == ("stats", 0):
                    statistics(x, 3 * b + 1)
                elif (what, k) == ("norm", 0):
                    normalise(xn, x, 3 * b + 1)
                    dve.sem_inc(s["xn_ready"], 1)
                elif what == "value":
                    dve.wait_ge(s["s_full"], NS * b + PAIR_S[what, k])
                    v.tensor_copy(v0.rearrange("p (a r) c -> p a r c", a=2),
                                  ps[0:P, bk:bk + 2, 0:3 * C].rearrange("p a (r c) -> p a r c", c=C)
                                  ).then_inc(s["s_free"], 1)
                elif what == "score":
                    dve.wait_ge(s["s_full"], NS * b + PAIR_S[what, k])
                    diag = bank(bk + k // 3, P)[:, (k % 3) * P:(k % 3 + 1) * P]
                    own.link(v.tensor_tensor(diag, diag, causal[:], ALU.add))
                    last = v.tensor_reduce(mx2[:, 0:1], bank(bk, P)[:, 0:min(k + 1, 3) * P], AX, ALU.max)
                    if k >= 3:
                        last = v.tensor_reduce(mx2[:, 1:2], bank(bk + 1, P)[:, 0:(k - 2) * P], AX, ALU.max)
                    own.link(last)
                    own.link(v.tensor_reduce(nm[:, k:k + 1], mx2[:, 0:1 + k // 3], AX, ALU.max, negate=True))
                    dve.sem_inc(s["nmax_ready"], 1)
                elif what == "weigh":
                    own.link(v.tensor_reduce(den[:, k:k + 1], sums[:, k, 0:1 + k // 3], AX, ALU.add))
                    own.link(v.reciprocal(rden[:, k:k + 1], den[:, k:k + 1]))
                    dve.wait_ge(s["t_full"], NT * b + PAIR_T[what, k])
                    own.link(v.scalar_tensor_tensor(out=x[:, k, :], in0=bank(bk + 2, P)[:, 0:C],
                                                    scalar=rden[:, k:k + 1], in1=x[:, k, :],
                                                    op0=ALU.mult, op1=ALU.add))
                    dve.sem_inc(s["t_free"], 1)
                elif (what, k) == ("norm", 1):
                    own.link(v.tensor_tensor(x, x, rows[:, 1:2, :].broadcast_to((P, R, C)), ALU.add))
                    layer_norm(xn, x, 3 * b + 2)
                elif (what, k) == ("norm", 2):
                    own.link(v.tensor_tensor(x, x, xn, ALU.add))
                    layer_norm(xres[:, b * R:(b + 1) * R, :], x, 3 * b + 3)
                    dve.sem_inc(s["xn_ready"], 1)
                elif (what, k) == ("query", 1):
                    dve.wait_ge(s["q_hi_done"], b + 1)
                    own.link(v.tensor_tensor(halves(q_lo[:, b, :]), two(bk + 2), halves(q_hi[:, b, :]), ALU.subtract))
                    dve.sem_inc(s["t_free"], 1)
                    dve.sem_inc(s["q_done"], 1)

            for what, k in MIX_ALONE:
                mix(0, what, k)
            dve.wait_ge(s["const_in"], CONST_IN)
            for b in range(B):
                for m, p, quarter, steps in layer_order(b):
                    if quarter == 3:
                        product_done(b, m, p)
                    for kind, at, what, k in steps:
                        if kind == MIX:
                            mix(at, what, k)
                        if kind == ATTN:
                            attn(at, what, k)
                        if kind == DOWN:
                            down(at, k)
            for k in range(2):
                down(B - 1, k)

            def low_part(b, t, u, parts=KW):
                dve.wait_ge(s["exp_sum"], TILES * b + t + 1)
                v.tensor_tensor(halves(p_lo[u][0:parts]), two(2 * u, parts), halves(p_hi[u][0:parts]),
                                ALU.subtract).then_inc(s["lo_ready"], 1)

            def maximum_of(b, c, r):
                dve.wait_ge(s["mx_ps"], MAXIMA * b + 1 + R * c + r + 1)
                bk = (7, 6, 4)[r % 3] if b == 0 else 4
                v.tensor_reduce(mxk[:, r, bass.ds(c + 1, 1)], bank(bk, P), AX, ALU.max).then_inc(s["mx_free"], 1)

            def values_low(b, c):
                dve.wait_ge(s["vh_ready"], CHUNKS * b + 1 + c + 1)
                v.tensor_tensor(v_lo[b % 2][:, bass.ds(c * 4, 4), 0:C], bank(5).rearrange("p (t c) -> p t c", c=C),
                                v_hi[b % 2][:, bass.ds(c * 4, 4), 0:C], ALU.subtract).then_inc(s["vl_ready"], 1)

            def prepare(b, c, part):
                for r in ((0, 1), (2,), (3, 4), (5,))[part]:
                    maximum_of(b, c, r)
                if part == 2:
                    values_low(b, c)

            def prepare_tail(b):
                dve.wait_ge(s["vh_ready"], CHUNKS * b + 1)
                v.tensor_tensor(v_lo[b % 2][0:TAIL, KT, 0:C], bank(5, TAIL)[:, 0:C], v_hi[b % 2][0:TAIL, KT, 0:C],
                                ALU.subtract).then_inc(s["vl_ready"], 1)
                dve.wait_ge(s["mx_ps"], MAXIMA * b + 1)
                v.tensor_reduce(mxk[:, :, 0], bank(4, P)[:, 0:R * TAIL].rearrange("p (r k) -> p r k", r=R),
                                AX, ALU.max).then_inc(s["mx_free"], 1)

            def shifts(b):
                dve.wait_ge(s["mx_free"], 1 + MAXIMA * (b + 1))
                own.link(v.tensor_reduce(nm[:], mxk, AX, ALU.max, negate=True))
                for r in range(R):
                    last = v.tensor_scalar(shift[b % 2][:, r, :], ident[0:P, 0:P], nm[:, r:r + 1], None, ALU.mult)
                last.then_inc(s["shift_ready"], 1)

            def step(kind, b, what, k):
                (end if kind == END else post)(b, what, k)

            def end(b, what, k):
                x, y = h[:, b * R:(b + 1) * R, :], xres[:, b * R:(b + 1) * R, :]
                if what == "stats":
                    if k == 0:
                        own.link(v.tensor_tensor(x, x, rows[:, 1:2, :].broadcast_to((P, R, C)), ALU.add))
                    statistics(x, 3 * b + 2 + k)
                elif what == "norm":
                    normalise(y, x, 3 * b + 2 + k)
                    if k == 1:
                        dve.sem_inc(s["xn_ready"], 1)
                elif what == "add":
                    own.link(v.tensor_tensor(x, x, y, ALU.add))
                else:
                    half = slice(k * HALF, (k + 1) * HALF)
                    dve.wait_ge(s["q_hi_done"], b + k + 1)
                    own.link(v.tensor_tensor(q_lo[:, b, half], bank(5)[:, 0:HALF], q_hi[:, b, half], ALU.subtract))
                    dve.sem_inc(s["post_free"], 1)
                    dve.sem_inc(s["q_done"], 1)

            def post(b, what, k):
                bk = post_bank(b)
                x, y = xres[:, b * R:(b + 1) * R, :], h[:, b * R:(b + 1) * R, :]
                if what == "sum":
                    dve.wait_ge(s["acc_free"], b + 1)
                    own.link(v.tensor_tensor(x, x, rows[:, 2:3, :].broadcast_to((P, R, C)), ALU.add))
                elif what == "stats":
                    statistics(x if k == 0 else y, 3 * B + 2 * b + k + 1)
                elif what == "gamma":
                    for r in range(R):
                        last = v.scalar_tensor_tensor(out=x[:, r, :], in0=x[:, r, :], scalar=mv[:, r, 0:1],
                                                      in1=rows[:, 3, :], op0=ALU.subtract, op1=ALU.mult)
                    own.link(last)
                elif what == "beta":
                    dve.wait_ge(s["rstd_ready"], 3 * B + 2 * b + 1)
                    for r in range(R):
                        last = v.scalar_tensor_tensor(out=x[:, r, :], in0=x[:, r, :], scalar=rstd[:, r:r + 1],
                                                      in1=rows[:, 4, :], op0=ALU.mult, op1=ALU.add)
                    own.link(last)
                elif what == "add":
                    own.link(v.tensor_tensor(y, y, x, ALU.add))
                elif what == "norm":
                    normalise(x, y, 3 * B + 2 * b + 2)
                    dve.sem_inc(s["xn_ready"], 1)
                elif what == "low":
                    dve.wait_ge(s["post_free"], USE[POST, b, "x", 1])
                    own.link(v.tensor_tensor(q_lo[:, b, :], xnT, q_hi[:, b, :], ALU.subtract))
                elif what == "logits":
                    dve.wait_ge(s["post_full"], USE[POST, b, what, k])
                    logits = bank(bk, P)[:, 0:R * E].rearrange("p (r e) -> p r e", e=E)
                    own.link(v.tensor_reduce(den[:], logits, AX, ALU.max))
                    own.link(v.tensor_tensor(probs[:, :, 0:E], logits, den[:].unsqueeze(2).broadcast_to((P, R, E)),
                                             ALU.subtract))
                    dve.sem_inc(s["post_free"], 1)
                    dve.sem_inc(s["shifted_logits"], 1)
                    v.memset(probs[:, :, E:E + 2], -1.0)
                    v.memset(top6, -1.0)
                elif what == "exp":
                    dve.wait_ge(s["logits_exp"], b + 1)
                    own.link(v.tensor_reduce(den[:], probs[:, :, 0:E], AX, ALU.add))
                    own.link(v.reciprocal(rden[:], den[:]))
                    own.link(v.tensor_tensor(probs[:, :, 0:E], probs[:, :, 0:E],
                                             rden[:].unsqueeze(2).broadcast_to((P, R, E)), ALU.mult))
                elif what == "top":
                    v.memset(idle[:], 0.0)
                    for r in range(R):
                        last = v.max(top8[:, r, :], probs[:, r, 0:E])
                    own.link(last)
                    own.link(v.tensor_copy(top6[:, :, 0:TOPK], top8[:, :, 0:TOPK]))
                elif what == "choose":
                    v.memset(idle[:], 0.0)
                    for r in range(R):
                        last = v.match_replace(rep[:, r, :], top6[:, r, :], probs[:, r, :], -2.0)
                    own.link(last)
                    own.link(v.tensor_scalar(msk, rep[:, :, 0:E], -1.5, None, ALU.is_lt))
                    dve.sem_inc(s["msk_ready"], 1)
                elif what == "share":
                    own.link(v.tensor_reduce(den[:], top8[:, :, 0:TOPK], AX, ALU.add))
                    own.link(v.tensor_scalar(den[:], den[:], 1e-9, None, ALU.add))
                    own.link(v.reciprocal(rden[:], den[:]))
                    own.link(v.tensor_tensor(probs[:, :, 0:E], probs[:, :, 0:E], msk, ALU.mult))
                    own.link(v.tensor_tensor(probs[:, :, 0:E], probs[:, :, 0:E],
                                             rden[:].unsqueeze(2).broadcast_to((P, R, E)), ALU.mult))
                elif what == "place":
                    dve.wait_ge(s["post_full"], USE[POST, b, what, k])
                    own.link(v.tensor_tensor(slot[:, :, 0:E], bank(bk, P)[:, 0:R * E].rearrange("p (r e) -> p r e", e=E),
                                             carry[:].unsqueeze(1).broadcast_to((P, R, E)), ALU.add))
                    v.tensor_scalar(slot[:, :, 0:E], slot[:, :, 0:E], float(CAP), X_SCALE, ALU.is_lt, ALU.mult)
                    own.link(v.tensor_tensor(carry[:], carry[:], bank(bk, P)[:, R * E:R * E + E], ALU.add))
                    dve.sem_inc(s["post_free"], 1)
                elif (what, k) == ("gates", 0):
                    for n in range(2):
                        last = v.tensor_tensor(gate2[:, :, n * E:(n + 1) * E], slot[:, :, 0:E], probs[:, :, 0:E],
                                               ALU.mult)
                    own.link(last)
                    dve.sem_inc(s["gates_ready"], 1)
                elif what == "gates":
                    half = slice((k - 1) * HALF, k * HALF)
                    dve.wait_ge(s["gates_hi"], 2 * b + k)
                    own.link(v.tensor_tensor(gates[E:128, b * T + (k - 1) * HALF:b * T + k * HALF],
                                             ps[E:128, bk, 0:HALF], g_tmp[E:128, half], ALU.subtract))
                    dve.sem_inc(s["post_free"], 1)

            prepare_tail(0)
            attn(B - 1, "stats", 0)
            for c in range(NCH):
                for u in range(2):
                    for r in range(3 * u, 3 * u + 3):
                        maximum_of(0, c, r)
                    for what, k in LAST_ATTN_STEPS[2 * c + u:2 * c + u + 1]:
                        attn(B - 1, what, k)
                values_low(0, c)
            shifts(0)
            for b in range(B):
                if b + 1 < B:
                    prepare_tail(b + 1)

                def eight(i):
                    for t in range(8):
                        low_part(b, 8 * i + t, t % 2)
                        if b + 1 < B:
                            prepare(b + 1, 2 * i + t // 4, t % 4)
                        if isinstance(i, int):
                            for x in beside(b, "dve", 8 * i + t):
                                step(*x)

                for i in range(FIRST):
                    eight(i)
                with dve.Fori(FIRST, LAST) as i:
                    eight(i)
                eight(LAST)
                low_part(b, KT, 0, TAIL)
                if b + 1 < B:
                    shifts(b + 1)
                for x in beside(b, "dve", KT):
                    step(*x)
                dve.wait_ge(s["acc_ps"], b + 1)
                for r in range(R):
                    o = (r % 3) * (C + 1)
                    last = v.reciprocal(rden[:, r:r + 1], ps[0:P, 6 + r // 3, o + C:o + C + 1])
                own.link(last)
                for r in range(R):
                    o = (r % 3) * (C + 1)
                    x = xres[:, b * R + r, :]
                    last = v.scalar_tensor_tensor(out=x, in0=ps[0:P, 6 + r // 3, o:o + C],
                                                  scalar=rden[:, r:r + 1], in1=x, op0=ALU.mult, op1=ALU.add)
                last.then_inc(s["acc_free"], 1)
            stage_end(dve, 1)
            def product(n, u, m):
                dve.wait_ge(s["silu_done"], n + 1)
                dve.wait_ge(s["up_ps"], n + 1)
                v.scalar_tensor_tensor(out=su[u], in0=sg[u], scalar=A_SCALE / X_SCALE ** 2,
                                       in1=bank(3 * u + 1)[:, 0:MT], op0=ALU.mult, op1=ALU.mult
                                       ).then_inc(s["su_ready"], 1)
                dve.wait_ge(s["su_ready"], m)
                dve.wait_ge(s["down_done"], n + 1)
                v.tensor_tensor(ac[u], su[u], bank(3 * u + 2)[:, 0:MT], ALU.mult).then_inc(s["a_ready"], 1)
                dve.wait_ge(s["a_ready"], n + 1)
                dve.sem_inc(s["up_free"], 1)

            def shared_product(n):
                dve.wait_ge(s["silu_done"], n + 1)
                dve.wait_ge(s["up_ps"], n + 1)
                own.link(v.scalar_tensor_tensor(out=ac[0], in0=sg[0], scalar=A_SCALE * 0.5 / X_SCALE,
                                                in1=bank(1)[:, 0:MT], op0=ALU.mult, op1=ALU.mult))
                dve.sem_inc(s["up_free"], 1)
                dve.sem_inc(s["a_ready"], 1)

            def chunk_done(c):
                dve.wait_ge(s["out_ps"], c + 1)
                dve.wait_ge(s["fin_out"], 16 * (c + 1))
                own.link(v.tensor_tensor(fin, bank(7, P).rearrange("p (r c) -> p r c", c=C),
                                         h[:, bass.ds(c * (MT // P), MT // P), :], ALU.add))
                dve.sem_inc(s["fin_ready"], 1)

            shared_product(0)
            for n in range(1, NSEQ):
                product(n, n % 2, n)
                for x in beside(B, "dve", pair=n):
                    step(*x)
            with own.loop(1, NMC, 2) as c:
                n0 = NSEQ * c
                shared_product(n0)
                chunk_done(c - 1)
                with dve.Fori(0, PAIRS // 2) as i:
                    product(n0 + 2 * i + 1, 1, PAIRS * c + 2 * i + 1)
                    product(n0 + 2 * i + 2, 0, PAIRS * c + 2 * i + 2)
            chunk_done(NMC - 1)

        @block.tensor
        def _(pe):
            mm = nc.tensor.matmul

            def mix(b, what, k):
                if (MIX, b, what, k) not in SHARED:
                    return
                _, bk, left, _ = SHARED[MIX, b, what, k]
                if what == "logits":
                    pe.wait_ge(s["x_in"], 16 * (b + 1))
                elif what == "band":
                    u, n = band_buffer(b, k)
                    pe.wait_ge(s_band[u], 32 * n)
                elif what == "apply":
                    pe.wait_ge(s["act_read"], SHARED[MIX, b, "band", k][3])
                if left:
                    pe.wait_ge(s[left[0]], left[1])
                if what == "logits":
                    for j in range(GW):
                        o = bank(bk, WT)[:, j * HEADS * TAPS:(j + 1) * HEADS * TAPS]
                        last = mm(o, xt[:, (GW * k + j) * WT:(GW * k + j + 1) * WT], wl_sb, start=True, stop=True)
                elif what == "band":
                    for g in range(HEADS):
                        last = nc.tensor.transpose(bank(bk, WIN)[:, g * WT:(g + 1) * WT],
                                                   band[u][:, g * WIN:(g + 1) * WIN], ident[0:WT, 0:WT])
                else:
                    last = mm(bank(bk)[:, 0:HEADS * WT], xw[band_buffer(b, k)[0]], bandT[k % 2 * (b == 0)], start=True, stop=True)
                last.then_inc(s["shared_full"], 1)

            def down(b, k):
                pe.wait_ge(s["z_ready"], 2 * MC * (b + 1))
                _, bk, left, _ = SHARED[DOWN, b, "h", k]
                pe.wait_ge(s[left[0]], left[1])
                for r in range(3):
                    t = (3 * k + r) * P
                    for m in range(MC):
                        last = mm(bank(bk, P)[:, r * C:(r + 1) * C], zz[:, m, t:t + P], w2_sb[:, m, :],
                                  start=(m == 0), stop=(m == MC - 1))
                last.then_inc(s["shared_full"], 1)

            def attn(b, what, k):
                bk = attn_banks(b)
                if what in ("stats", "norm"):
                    return
                if (what, k) in PAIR_S:
                    full = s["s_full"]
                    if NS * b + PAIR_S[what, k] > 1:
                        pe.wait_ge(s["s_free"], NS * b + PAIR_S[what, k] - 1)
                else:
                    full = s["t_full"]
                    if NT * b + PAIR_T[what, k] > 1:
                        pe.wait_ge(s["t_free"], NT * b + PAIR_T[what, k] - 1)
                if what == "transpose":
                    pe.wait_ge(s["xn_ready"], 2 * b + k + 1)
                    src = xn if k == 0 else xres[:, b * R:(b + 1) * R, :]
                    for r in range(R):
                        last = nc.tensor.transpose(bank(bk + r // 3)[:, (r % 3) * P:(r % 3 + 1) * P], src[:, r, :],
                                                   ident[0:P, 0:P])
                elif what == "query":
                    pe.wait_ge(s["s_free"], NS * b + PAIR_S["transpose", k])
                    for u in range(2):
                        last = mm(bank(bk + 2 + u)[:, 0:HALF], (g0, g1)[k][:], yT[:, u * HALF:(u + 1) * HALF],
                                  start=True, stop=True)
                elif what == "value":
                    for r in range(R):
                        last = mm(bank(bk + r // 3, P)[:, (r % 3) * C:(r % 3 + 1) * C], yT[:, r * P:(r + 1) * P],
                                  m0[:], start=True, stop=True)
                elif what == "score":
                    pe.wait_ge(s["t_free"], NT * b + PAIR_T["query", 0])
                    q = qg[:, k * P:(k + 1) * P]
                    last = mm(bank(bk, P)[:, 0:min(k + 1, 3) * P], q, yT[:, 0:min(k + 1, 3) * P],
                              start=True, stop=True)
                    if k >= 3:
                        last = mm(bank(bk + 1, P)[:, 0:(k - 2) * P], q, yT[:, HALF:(k + 1) * P],
                                  start=True, stop=True)
                elif what == "turn":
                    pe.wait_ge(s["s_free"], NS * b + PAIR_S["score", k])
                    for t in range(k + 1):
                        last = nc.tensor.transpose(bank(bk + 2 + t // 3, P)[:, (t % 3) * P:(t % 3 + 1) * P],
                                                   pr[:, t * P:(t + 1) * P], ident[0:P, 0:P])
                elif what == "weigh":
                    for t in range(k + 1):
                        last = mm(bank(bk + 2, P)[:, 0:C], prT[:, t * P:(t + 1) * P], v0[:, t, :],
                                  start=(t == 0), stop=(t == k))
                last.then_inc(full, 1)

            def conv(b, m, p, quarter):
                n = (EV, OD, EV)[p]
                if quarter == 0:
                    turn = 3 * (MC * b + m) + p
                    if turn >= 3:
                        pe.wait_ge(s["prod_free"], turn - 2)
                    if m == 0:
                        pe.wait_ge(s["y_ready"], 3 * b + p + 1)
                    if b == 0 and p == 0:
                        pe.wait_ge(s["wc_ready"], 2 * (m + 1))
                w = HALF + (p == 0)
                o = bank(p)[:, 0:w]
                xh, xl = ys[b % 2][p]
                wh, wl = wc[p]
                for j in range(4 * quarter, min(4 * quarter + 4, n)):
                    mm(o, wh[:, m, j], xh[:, j:j + w], start=(j == 0), stop=False)
                    mm(o, wh[:, m, j], xl[:, j:j + w], start=False, stop=False)
                    last = mm(o, wl[:, m, j], xh[:, j:j + w], start=False, stop=(j == n - 1))
                if quarter == 3:
                    last.then_inc(s["prod_full"], 1)

            pe.wait_ge(s["mix_in"], MIX_IN)
            pe.wait_ge(s["ones_ready"], 1)
            for what, k in MIX_ALONE:
                mix(0, what, k)
                if (what, k) == ("logits", 1):
                    pe.wait_ge(s["const_in"], CONST_IN)
                    mm(bank(6)[:, 0:128], wq_sb, wk_sb, start=True, stop=True)
                    mm(bank(6)[:, 128:256], wv_sb, wo_sb, start=True, stop=True)
                    mm(bank(6)[:, 256:384], w1_sb, w1_sb, start=True, stop=True)
                    mm(bank(6)[:, 384:512], w1_sb, fc_sb, start=True, stop=True).then_inc(s["wprod_ps"], 1)
            pe.wait_ge(s["wprod_sb"], 1)
            for b in range(B):
                for m, p, quarter, steps in layer_order(b):
                    conv(b, m, p, quarter)
                    for kind, at, what, k in steps:
                        if kind == MIX:
                            mix(at, what, k)
                        if kind == ATTN:
                            attn(at, what, k)
                        if kind == DOWN:
                            down(at, k)

            def step(kind, b, what, k):
                (end if kind == END else post)(b, what, k)

            def end(b, what, k):
                half = slice(k * HALF, (k + 1) * HALF)
                n = USE[END, b, what, k]
                if n > 1:
                    pe.wait_ge(s["post_free"], n - 1)
                if what == "x":
                    pe.wait_ge(s["xn_ready"], 2 * b + 2)
                    for r in range(3):
                        last = nc.tensor.transpose(bank(5)[:, r * P:(r + 1) * P], xres[:, b * R + 3 * k + r, :],
                                                   ident[0:P, 0:P])
                else:
                    last = mm(bank(5)[:, 0:HALF], g1[:], xnT[:, half], start=True, stop=True)
                last.then_inc(s["post_full"], 1)

            def post(b, what, k):
                bk = post_bank(b)
                n = USE[POST, b, what, k]
                if n > 1:
                    pe.wait_ge(s["post_free"], n - 1)
                if what == "x":
                    pe.wait_ge(s["xn_ready"], 2 * B + b + 1)
                    for r in range(3):
                        last = nc.tensor.transpose(bank(bk)[:, r * P:(r + 1) * P], xres[:, b * R + 3 * k + r, :],
                                                   ident[0:P, 0:P])
                elif what == "logits":
                    for r in range(R):
                        o = bank(bk, P)[:, r * E:(r + 1) * E]
                        mm(o, xnT[:, r * P:(r + 1) * P], rw_sb[:], start=True, stop=False)
                        last = mm(o, ones[0:1, 0:P], rb_sb[:], start=False, stop=True)
                elif what == "place":
                    pe.wait_ge(s["msk_ready"], b + 1)
                    for r in range(R + 1):
                        o = bank(bk, P)[:, r * E:(r + 1) * E]
                        for t in range(min(r + 1, R)):
                            w = before if t == r else ones16[0:P, 0:P]
                            last = mm(o, w[:] if t == r else w, msk[:, t, :], start=(t == 0),
                                      stop=(t == min(r, R - 1)))
                elif what == "gates":
                    pe.wait_ge(s["gates_ready"], b + 1)
                    for r in range(3):
                        last = nc.tensor.transpose(bank(bk)[:, r * P:(r + 1) * P], gate2[:, 3 * k + r, :],
                                                   ident[0:P, 0:P])
                last.then_inc(s["post_full"], 1)

            def project(b, c2, u):
                pe.wait_ge(s_vf[u], 16 * ((NCH // 2) * b + c2 + 1))
                pe.wait_ge(s["vl_ready"], CHUNKS * b + 2 * c2 + u + 2)
                for t in range(4):
                    last = mm(bank(5)[:, t * C:(t + 1) * C], vf[u][:, t * KW:(t + 1) * KW], m1[:],
                              start=True, stop=True)
                last.then_inc(s["vps_ready"], 1)

            def maximum_of(b, c2, u, r):
                pe.wait_ge(s["klo_ready"], 2 + CHUNKS * b + 2 * c2 + u + 2)
                n = MAXIMA * b + 2 + R * (2 * c2 + u) + r - 2 * (b == 0)
                if b or n > 0:
                    pe.wait_ge(s["mx_free"], n)
                bk = (7, 6, 4)[r % 3] if b == 0 else 4
                mm(bank(bk, P), q_hi[:, b, r * P:(r + 1) * P], k_hi[b % 2][:, bass.ds(c2 * (2 * CH) + u * CH, CH)],
                   start=True, stop=True).then_inc(s["mx_ps"], 1)

            def prepare_tail(b):
                pe.wait_ge(s_tail, 32 * (b + 1))
                pe.wait_ge(s["vl_ready"], CHUNKS * b + 1)
                mm(bank(5, TAIL)[:, 0:C], vf_tail, m1[:], start=True, stop=True).then_inc(s["vps_ready"], 1)
                pe.wait_ge(s["klo_ready"], 2 + CHUNKS * b + 1)
                pe.wait_ge(s["mx_free"], MAXIMA * b + 1)
                for r in range(R):
                    last = mm(bank(4, P)[:, r * TAIL:(r + 1) * TAIL], q_hi[:, b, r * P:(r + 1) * P],
                              k_hi[b % 2][:, KT * KW:], start=True, stop=True)
                last.then_inc(s["mx_ps"], 1)

            def key_scores(b, t, u, parts=KW):
                first = isinstance(t, int) and t < 2
                if b or not first:
                    pe.wait_ge(s["lo_ready"], TILES * b + (0 if first else t - 1))
                at = slice(t * KW, t * KW + parts) if isinstance(t, int) else bass.ds(t * KW, parts)
                kh, kl = k_hi[b % 2][:, at], k_lo[b % 2][:, at]
                for w in range(2):
                    q = slice(w * HALF, (w + 1) * HALF)
                    mm(bank(2 * u + w, parts)[:, 0:HALF], kh, q_hi[:, b, q], start=True, stop=False)
                    mm(bank(2 * u + w, parts)[:, 0:HALF], kh, q_lo[:, b, q], start=False, stop=False)
                for w in range(2):
                    q = slice(w * HALF, (w + 1) * HALF)
                    mm(bank(2 * u + w, parts)[:, 0:HALF], kl, q_hi[:, b, q], start=False, stop=False)
                if isinstance(t, int) and t == 0:
                    pe.wait_ge(s["shift_ready"], b + 1)
                sh = shift[b % 2].rearrange("p r q -> p (r q)")
                for w in range(2):
                    last = mm(bank(2 * u + w, parts)[:, 0:HALF], ones16[0:P, 0:parts],
                              sh[:, w * HALF:(w + 1) * HALF], start=False, stop=True)
                last.then_inc(s["st_ps"], 1)

            def weigh(b, t, u, parts=KW):
                at = slice(t, t + 1) if isinstance(t, int) else bass.ds(t, 1)
                vh = v_hi[b % 2][0:parts, at, :].rearrange("p a c -> p (a c)")
                vl = v_lo[b % 2][0:parts, at, :].rearrange("p a c -> p (a c)")

                def sums(r):
                    o = (r % 3) * (C + 1)
                    return ps[0:P, 6 + r // 3, o:o + C + 1]

                pe.wait_ge(s["p_hi_ready"], TILES * b + t + 1)
                for r in range(R):
                    ph = p_hi[u][0:parts, r * P:(r + 1) * P]
                    mm(sums(r), ph, vh, start=False, stop=False, skip_group_check=True)
                    mm(sums(r), ph, vl, start=False, stop=False, skip_group_check=True)
                pe.wait_ge(s["lo_ready"], TILES * b + t + 1)
                for r in range(R):
                    last = mm(sums(r), p_lo[u][0:parts, r * P:(r + 1) * P], vh, start=False, stop=False,
                              skip_group_check=True)
                last.then_inc(s["pv_done"], 1)

            def zero_sums(start):
                for w in range(2):
                    last = mm(bank(6 + w, P)[:, 0:3 * (C + 1)], ones16[0:1, 0:P], zrow[:, 0:3 * (C + 1)],
                              start=start, stop=not start, skip_group_check=True)
                return last

            pe.wait_ge(s["s_free"], NS * (B - 1))
            pe.wait_ge(s["t_free"], NT * (B - 1))
            prepare_tail(0)
            for k in range(2):
                down(B - 1, k)
            for c in range(NCH):
                for u in range(2):
                    for r in range(3 * u, 3 * u + 3):
                        maximum_of(0, c // 2, c % 2, r)
                    if u == 0:
                        project(0, c // 2, c % 2)
                    for what, k in LAST_ATTN_STEPS[2 * c + u:2 * c + u + 1]:
                        attn(B - 1, what, k)
            pe.wait_ge(s["mx_free"], MAXIMA + 1)
            pe.wait_ge(s["q_done"], B - 1)
            for b in range(B):
                pe.wait_ge(s["klo_ready"], 2 + CHUNKS * (b + 1))
                pe.wait_ge(s["vl_ready"], 1 + CHUNKS * (b + 1))
                key_scores(b, 0, 0)
                if b:
                    pe.wait_ge(s["acc_free"], b)
                zero_sums(True)
                if b:
                    pe.wait_ge(s["post_free"], uses(b, 0))
                if b + 2 == B:
                    pe.wait_ge(s["q_done"], B + 1)
                if b + 1 < B:
                    prepare_tail(b + 1)

                def eight(i, last):
                    for t in range(8):
                        if last and t == 7:
                            key_scores(b, KT, 0, TAIL)
                        else:
                            key_scores(b, 8 * i + t + 1, (t + 1) % 2)
                        u = t // 4
                        if b + 1 < B:
                            maximum_of(b + 1, i, u, (0, 2, 3, 5)[t % 4])
                        weigh(b, 8 * i + t, t % 2)
                        if b + 1 < B:
                            if t % 4 == 1:
                                if isinstance(i, int) and uses(b, 8 * i + t):
                                    pe.wait_ge(s["post_free"], uses(b, 8 * i + t))
                                project(b + 1, i, u)
                            elif t % 4 != 3:
                                maximum_of(b + 1, i, u, (1, None, 4)[t % 4])
                        if isinstance(i, int):
                            for x in beside(b, "pe", 8 * i + t):
                                if b + 1 < B:
                                    pe.wait_ge(s["vl_ready"], CHUNKS * (b + 1) + 2 * i + u + 2 + (t % 4 > 0))
                                step(*x)

                for i in range(FIRST):
                    eight(i, False)
                pe.wait_ge(s["post_free"], uses(b, 8 * FIRST))
                with pe.Fori(FIRST, LAST) as i:
                    eight(i, False)
                eight(LAST, True)
                weigh(b, KT, 0, TAIL)
                zero_sums(False).then_inc(s["acc_ps"], 1)
            stage_end(pe, 1)

            def up(c, sq, pair, u, n):
                at = bass.ds(c * MT, MT)
                xh, xl = x_hi[:, at], x_lo[:, at]
                pe.wait_ge(s["up_free"], n + 1)
                for k, (wh, wl) in enumerate(((wg_hi, wg_lo), (wu_hi, wu_lo))):
                    o = bank(3 * u + k)[:, 0:MT]
                    mm(o, wh[:, bass.ds(sq * 128, 128)], xh, start=True, stop=False)
                    mm(o, wh[:, bass.ds(sq * 128, 128)], xl, start=False, stop=False)
                    last = mm(o, wl[:, bass.ds(sq * 128, 128)], xh, start=False, stop=True)
                    if k == 0:
                        last.then_inc(s["gate_ps"], 1)
                if pair is not None:
                    last = mm(bank(3 * u + 2)[:, 0:MT], sel_sb[:, bass.ds(pair * 128, 128)], gates[:, at],
                              start=True, stop=True)
                last.then_inc(s["up_ps"], 1)

            def down(sq, u, n, start=False, stop=False):
                pe.wait_ge(s["a_lo_ready"], n + 1)
                o = bank(6)[:, 0:MT]
                mm(o, wd_hi[:, bass.ds(sq * C, C)], a_hi[u], start=start, stop=False)
                mm(o, wd_hi[:, bass.ds(sq * C, C)], a_lo[u], start=False, stop=False)
                mm(o, wd_lo[:, bass.ds(sq * C, C)], a_hi[u], start=False, stop=stop
                   ).then_inc(s["down_done"], 1)

            def chunk_done(c):
                pe.wait_ge(s["out_cm_ready"], c + 1)
                for r in range(MT // P):
                    last = nc.tensor.transpose(bank(7, P)[:, r * C:(r + 1) * C], out_cm[:, r * P:(r + 1) * P],
                                               ident[:])
                last.then_inc(s["out_ps"], 1)

            up(0, 0, None, 0, 0)
            up(0, 1, 0, 1, 1)
            for n in range(NSEQ):
                if n + 2 < NSEQ:
                    up(0, n + 2, n + 1, n % 2, n + 2)
                if n + 1 < NSEQ:
                    down(n, n % 2, n, start=(n == 0))
                for x in beside(B, "pe", pair=n):
                    step(*x)
            pe.wait_ge(s["post_free"], len(USE))
            with pe.Fori(1, NMC) as c:
                n0 = NSEQ * c
                pe.wait_ge(s["up_free"], n0 + 2)
                up(c, 0, None, 0, n0)
                down(PAIRS, 0, n0 - 1, stop=True)
                up(c, 1, 0, 1, n0 + 1)
                chunk_done(c - 1)
                up(c, 2, 1, 0, n0 + 2)
                down(0, 0, n0, start=True)
                with pe.Fori(0, PAIRS // 2 - 1) as i:
                    up(c, 2 * i + 3, 2 * i + 2, 1, n0 + 2 * i + 3)
                    down(2 * i + 1, 1, n0 + 2 * i + 1)
                    up(c, 2 * i + 4, 2 * i + 3, 0, n0 + 2 * i + 4)
                    down(2 * i + 2, 0, n0 + 2 * i + 2)
                down(PAIRS - 1, 1, n0 + PAIRS - 1)
            down(PAIRS, 0, NSEQ * NMC - 1, stop=True)
            chunk_done(NMC - 1)




def _pieces(w):
    w = w.reshape(MC, 128, C, TAPS).transpose(0, 2, 3, 1)
    out = np.zeros((2 * MC, C, WPIECE // 128, 128), w.dtype)
    for n in range(2 * MC):
        part = w[n // 2, :, 16 * (n % 2):16 * (n % 2) + 16]
        both = np.concatenate([part[:, 0::2], part[:, 1::2]], axis=1)
        out[n, :, :both.shape[1]] = both
    return out.reshape(2 * MC, C, WPIECE)


def _laid_out(i):
    f = lambda a: np.ascontiguousarray(np.asarray(a))
    x = f(i["x"])
    xp = np.zeros((B, TP + TAPS - 1, C), x.dtype)
    xp[:, LEFT:LEFT + T_IN] = x
    half = GW * WT
    d = {
        "xT": f([xp[b, LEFT:LEFT + TP].T for b in range(B)]),
        "xw": f([xp[b, WT * j:WT * j + WIN] for b in range(B) for j in range(NW)]),
        "WlT": f(np.asarray(i["L0_tok_Wl"]).T),
        "bl": f(i["L0_tok_bl"]).reshape(-1),
        "tok_bias": f(i["L0_tok_bias"]).reshape(-1, 1),
        "WcT": _pieces(np.asarray(i["L0_tok_Wc"])),
        "bc": f(np.asarray(i["L0_tok_bc"]).reshape(MC, 128).T),
        "W2T": f(np.asarray(i["L0_tok_W2"]).T.reshape(MC, 128, C).transpose(1, 0, 2)),
        "b2": f(i["L0_tok_b2"]),
        "bo": f(i["L0_attn_b_out"]),
        "Wo": f(i["L0_attn_W_out"]),
        "k": f(i["L1_attn_k"]).reshape(B, C, KEYS),
        "v": f(i["L1_attn_v"]).reshape(B, C, KEYS),
        "W1": f(i["L1_attn_w_qkvs"]),
        "fcT": f(np.asarray(i["L1_attn_fc_w"]).T),
        "fcb": f(i["L1_attn_fc_b"]),
        "gamma": f(i["L1_attn_gamma"]),
        "beta": f(i["L1_attn_beta"]),
        "rwT": f(np.asarray(i["L1_ffn_router_w"]).T),
        "rb": f(i["L1_ffn_bias"]).reshape(1, -1),
    }
    qkv = np.asarray(i["L0_attn_W_qkv"])
    for n, name in enumerate(("WqT", "WkT", "WvT")):
        d[name] = f(qkv[:, 64 * n:64 * (n + 1)].T)

    def pieces(w):
        return w.reshape(128, NWP, NSEQ * 128 // NWP).transpose(1, 0, 2)

    def projection(shared, experts):
        return pieces(np.concatenate([np.asarray(shared), np.asarray(experts)]).reshape(NSEQ * 128, C).T)

    down = np.concatenate([np.asarray(i["L1_ffn_shared_w_down"]), np.asarray(i["L1_ffn_w_down"])])
    d["experts"] = f(np.concatenate([
        projection(i["L1_ffn_shared_w_gate"], i["L1_ffn_w_gate"]),
        projection(i["L1_ffn_shared_w_up"], i["L1_ffn_w_up"]),
        pieces(down.reshape(NSEQ, 2, C, FF).transpose(1, 3, 0, 2).reshape(128, NSEQ * C))]))

    t = (half * np.arange(2)[None, :, None, None] + WT * np.arange(GW)[None, None, :, None]
         + np.arange(WT)[:, None, None, None])
    at = t + np.arange(TAPS) - LEFT
    m = np.where((at >= 0) & (at < T_IN), 0.0, -3e38).astype(np.float32)
    d["mask"] = f(np.stack([m[:, 0, 0], m[:, 1, GW - 1]], axis=1))
    d["ident"] = np.eye(128, dtype=np.float32)
    d["causal"] = np.triu(np.full((P, P), -1e30, np.float32), 1)
    d["before"] = np.triu(np.ones((P, P), np.float16), 1)
    r, c = np.arange(128)[:, None] % E, np.arange(PAIRS * 128)[None, :]
    d["sel"] = (r == 2 * (c // 128) + c % 128 // FF).astype(np.float16)
    return d


def kernel(**inputs):
    import concourse.bacc as bacc
    from concourse.bass_utils import run_bass_kernel_spmd

    arrays = _laid_out(inputs)
    nc = bacc.Bacc("TRN2", target_bir_lowering=False, num_devices=1)
    d = {n: nc.dram_tensor(f"in_{n}", a.shape, mybir.dt.from_np(a.dtype), kind="ExternalInput").ap()
         for n, a in arrays.items()}
    out = nc.dram_tensor("out", (B, T, C), F32, kind="ExternalOutput").ap()
    tower(nc, d, out)
    r = run_bass_kernel_spmd(nc, [{f"in_{n}": a for n, a in arrays.items()}], core_ids=[0])
    return r.results[0]["out"]
```
